# Optimizing a Trainium2 kernel written in Bass

```python
import numpy as np
import jax
import jax.numpy as jnp

def _softmax(x, axis=-1):
    return jax.nn.softmax(x, axis=axis)

def _gelu(x):
    return jax.nn.gelu(x, approximate=True)

def _silu(x):
    return jax.nn.silu(x)

def _sigmoid(x):
    return jax.nn.sigmoid(x)

def _layernorm(x, axis=-1, eps=1e-05):
    m = jnp.mean(x, axis=axis, keepdims=True)
    v = jnp.var(x, axis=axis, keepdims=True)
    return (x - m) / jnp.sqrt(v + eps)

def _scatter_add(tgt, idx, src, axis=0):
    return tgt.at[idx].add(src)

def _segment_sum(src, seg, n):
    return jax.ops.segment_sum(src, seg, n)
kernel_name = 'mk_xattn_ffn_d2_seqx_r4_890416'

def setup_inputs(seed: int=0):
    np.random.seed(seed)
    _w = jnp.asarray

    def _rec_inputs():
        import jax
        import jax.numpy as jnp
        _rk = jax.random.key(seed)
        x = -0.0005207 + 1.001 * jax.random.normal(jax.random.fold_in(_rk, 1), (8, 256, 512), jnp.float32)
        _lenS = 256 - jax.random.randint(jax.random.fold_in(_rk, 7), (8,), 0, max(1, 256 // 4) + 1, jnp.int32)
        _lenS2 = 256 - jax.random.randint(jax.random.fold_in(_rk, 8), (8,), 0, max(1, 256 // 4) + 1, jnp.int32)
        _ctx_2048P = jax.random.normal(jax.random.fold_in(_rk, 12), (8, 16, 512), jnp.float32)
        _ctx_2048c = jax.random.dirichlet(jax.random.fold_in(_rk, 512), 0.3 * jnp.ones((16,), jnp.float32), (8, 256))
        _ctx_2048t = jnp.einsum('bsk,bkd->bsd', _ctx_2048c, _ctx_2048P)
        _ctx_2048t = _ctx_2048t * jax.lax.rsqrt(jnp.mean(jnp.square(_ctx_2048t)) + 1e-12) * 0.953939
        ctx_2048 = -5.72187e-05 + 0.999849 * (_ctx_2048t + 0.3 * jax.random.normal(jax.random.fold_in(_rk, 612), (8, 256, 512), jnp.float32))
        _validS = jnp.arange(256)[None, :] < _lenS[:, None]
        _validS2 = jnp.arange(256)[None, :] < _lenS2[:, None]
        _causal = jnp.tril(jnp.ones((256, 256), dtype=bool))
        mask_BxSx4224_bf0 = jnp.logical_not(jnp.ones((8, 256, 1056), dtype=bool))
        mask_1xSxS2_ff0 = jnp.where(jnp.ones((1, 256, 256), dtype=bool), 0.0, -1000000000.0).astype(jnp.float32)
        return (x, ctx_2048, mask_BxSx4224_bf0, mask_1xSxS2_ff0)
    x, ctx_2048, mask_BxSx4224_bf0, mask_1xSxS2_ff0 = _rec_inputs()

    def _L0_xattn_setup():
        import jax, jax.numpy as jnp
        import numpy as np
        import math
        DIM = 512
        B, Q_LEN, KV_LEN = (8, 128, 1024)
        key = jax.random.key(seed)
        ks = jax.random.split(key, 8)
        x = jax.random.normal(ks[0], (B, Q_LEN, DIM), dtype=jnp.float32)
        mask = jnp.zeros((B, Q_LEN, KV_LEN + Q_LEN), dtype=bool)
        k_cache = jax.random.normal(ks[1], (B, KV_LEN, DIM), dtype=jnp.float32)
        v_cache = jax.random.normal(ks[2], (B, KV_LEN, DIM), dtype=jnp.float32)
        scale = 1.0 / math.sqrt(DIM)
        wq = jax.random.normal(ks[3], (DIM, DIM), dtype=jnp.float32) * scale
        wk = jax.random.normal(ks[4], (DIM, DIM), dtype=jnp.float32) * scale
        wv = jax.random.normal(ks[5], (DIM, DIM), dtype=jnp.float32) * scale
        wo = jax.random.normal(ks[6], (DIM, DIM), dtype=jnp.float32) * scale
        return {'x': x, 'mask': mask, 'k_cache': k_cache, 'v_cache': v_cache, 'wq': wq, 'wk': wk, 'wv': wv, 'wo': wo}
    _L0_xattn_all = _L0_xattn_setup()
    _L0_xattn_in = {k: v for k, v in _L0_xattn_all.items() if k in ('wq', 'wk', 'wv', 'wo')}
    del _L0_xattn_all

    def _L0_ffn_setup():
        import jax, jax.numpy as jnp
        import numpy as np
        D_MODEL = 512
        HIDDEN = 4 * D_MODEL
        B, S = (2, 1024)

        def bit_linear(x, w, b):
            gamma_x = jnp.clip(jnp.max(jnp.abs(x), axis=-1, keepdims=True), 1e-05, None)
            scale_x = 127.0 / gamma_x
            x_dq = jnp.clip(jnp.round(x * scale_x), -128.0, 127.0) / scale_x
            x_ste = x + jax.lax.stop_gradient(x_dq - x)
            gamma_w = jnp.clip(jnp.mean(jnp.abs(w)), 1e-05, None)
            w_dq = jnp.clip(jnp.round(w / gamma_w), -1.0, 1.0) * gamma_w
            w_ste = w + jax.lax.stop_gradient(w_dq - w)
            return jnp.einsum('bsd,hd->bsh', x_ste, w_ste) + b
        key = jax.random.key(seed)
        ks = jax.random.split(key, 7)
        std = 0.02
        return {'x': jax.random.normal(ks[0], (B, S, D_MODEL), dtype=jnp.float32), 'gate_w': jax.random.normal(ks[1], (HIDDEN, D_MODEL), dtype=jnp.float32) * std, 'gate_b': jnp.zeros((HIDDEN,), dtype=jnp.float32), 'val_w': jax.random.normal(ks[2], (HIDDEN, D_MODEL), dtype=jnp.float32) * std, 'val_b': jnp.zeros((HIDDEN,), dtype=jnp.float32), 'out_w': jax.random.normal(ks[3], (D_MODEL, HIDDEN), dtype=jnp.float32) * std, 'out_b': jnp.zeros((D_MODEL,), dtype=jnp.float32)}
    _L0_ffn_all = _L0_ffn_setup()
    _L0_ffn_in = {k: v for k, v in _L0_ffn_all.items() if k in ('gate_w', 'gate_b', 'val_w', 'val_b', 'out_w', 'out_b')}
    del _L0_ffn_all

    def _L1_xattn_setup():
        import jax, jax.numpy as jnp
        import numpy as np
        H = 512
        NH = 16
        NKV = 4
        HD = 128
        GROUPS = NH // NKV
        EPS = 1e-06
        B, S, SE = (1, 512, 1024)

        def _rmsnorm(x, w, eps=EPS):
            xf = x.astype(jnp.float32)
            var = jnp.mean(xf * xf, axis=-1, keepdims=True)
            return (xf * jax.lax.rsqrt(var + eps)).astype(x.dtype) * w
        key = jax.random.key(seed)
        ks = jax.random.split(key, 12)
        sc = 0.02
        return {'hidden_states': jax.random.normal(ks[0], (B, S, H), jnp.float32), 'encoder_hidden_states': jax.random.normal(ks[1], (B, SE, H), jnp.float32), 'attention_mask': jnp.zeros((B, S, SE), jnp.float32), 'Wq': jax.random.normal(ks[2], (H, NH * HD), jnp.float32) * sc, 'bq': jax.random.normal(ks[3], (NH * HD,), jnp.float32) * sc, 'Wk': jax.random.normal(ks[4], (H, NKV * HD), jnp.float32) * sc, 'bk': jax.random.normal(ks[5], (NKV * HD,), jnp.float32) * sc, 'Wv': jax.random.normal(ks[6], (H, NKV * HD), jnp.float32) * sc, 'bv': jax.random.normal(ks[7], (NKV * HD,), jnp.float32) * sc, 'Wo': jax.random.normal(ks[8], (NH * HD, H), jnp.float32) * sc, 'qn_w': jnp.ones((HD,), jnp.float32), 'kn_w': jnp.ones((HD,), jnp.float32)}
    _L1_xattn_all = _L1_xattn_setup()
    _L1_xattn_in = {k: v for k, v in _L1_xattn_all.items() if k in ('Wq', 'bq', 'Wk', 'bk', 'Wv', 'bv', 'Wo', 'qn_w', 'kn_w')}
    del _L1_xattn_all

    def _L1_ffn_setup():
        import jax, jax.numpy as jnp
        import numpy as np
        B, S, H, I, E, TOP_K, NS = (2, 512, 512, 352, 8, 2, 2)
        SI = I * NS
        INIT = 0.02
        key = jax.random.key(seed)
        ks = jax.random.split(key, 9)
        f32 = jnp.float32
        return {'hidden_states': jax.random.normal(ks[0], (B, S, H), f32), 'router_w': jax.random.normal(ks[1], (E, H), f32) * INIT, 'gate_w': jax.random.normal(ks[2], (E, H, I), f32) * INIT, 'up_w': jax.random.normal(ks[3], (E, H, I), f32) * INIT, 'down_w': jax.random.normal(ks[4], (E, I, H), f32) * INIT, 's_gate_w': jax.random.normal(ks[5], (H, SI), f32) * INIT, 's_gate_b': jnp.zeros((SI,), f32), 's_up_w': jax.random.normal(ks[6], (H, SI), f32) * INIT, 's_up_b': jnp.zeros((SI,), f32), 's_down_w': jax.random.normal(ks[7], (SI, H), f32) * INIT, 's_down_b': jnp.zeros((H,), f32)}
    _L1_ffn_all = _L1_ffn_setup()
    _L1_ffn_in = {k: v for k, v in _L1_ffn_all.items() if k in ('router_w', 'gate_w', 'up_w', 'down_w', 's_gate_w', 's_gate_b', 's_up_w', 's_up_b', 's_down_w', 's_down_b')}
    del _L1_ffn_all
    return {'x': x, 'ctx_2048': ctx_2048, 'mask_BxSx4224_bf0': mask_BxSx4224_bf0, 'mask_1xSxS2_ff0': mask_1xSxS2_ff0, 'L0_xattn_wq': _L0_xattn_in['wq'], 'L0_xattn_wk': _L0_xattn_in['wk'], 'L0_xattn_wv': _L0_xattn_in['wv'], 'L0_xattn_wo': _L0_xattn_in['wo'], 'L0_ffn_gate_w': _L0_ffn_in['gate_w'], 'L0_ffn_gate_b': _L0_ffn_in['gate_b'], 'L0_ffn_val_w': _L0_ffn_in['val_w'], 'L0_ffn_val_b': _L0_ffn_in['val_b'], 'L0_ffn_out_w': _L0_ffn_in['out_w'], 'L0_ffn_out_b': _L0_ffn_in['out_b'], 'L1_xattn_Wq': _L1_xattn_in['Wq'], 'L1_xattn_bq': _L1_xattn_in['bq'], 'L1_xattn_Wk': _L1_xattn_in['Wk'], 'L1_xattn_bk': _L1_xattn_in['bk'], 'L1_xattn_Wv': _L1_xattn_in['Wv'], 'L1_xattn_bv': _L1_xattn_in['bv'], 'L1_xattn_Wo': _L1_xattn_in['Wo'], 'L1_xattn_qn_w': _L1_xattn_in['qn_w'], 'L1_xattn_kn_w': _L1_xattn_in['kn_w'], 'L1_ffn_router_w': _L1_ffn_in['router_w'], 'L1_ffn_gate_w': _L1_ffn_in['gate_w'], 'L1_ffn_up_w': _L1_ffn_in['up_w'], 'L1_ffn_down_w': _L1_ffn_in['down_w'], 'L1_ffn_s_gate_w': _L1_ffn_in['s_gate_w'], 'L1_ffn_s_gate_b': _L1_ffn_in['s_gate_b'], 'L1_ffn_s_up_w': _L1_ffn_in['s_up_w'], 'L1_ffn_s_up_b': _L1_ffn_in['s_up_b'], 'L1_ffn_s_down_w': _L1_ffn_in['s_down_w'], 'L1_ffn_s_down_b': _L1_ffn_in['s_down_b']}

def reference(x, ctx_2048, mask_BxSx4224_bf0, mask_1xSxS2_ff0, L0_xattn_wq, L0_xattn_wk, L0_xattn_wv, L0_xattn_wo, L0_ffn_gate_w, L0_ffn_gate_b, L0_ffn_val_w, L0_ffn_val_b, L0_ffn_out_w, L0_ffn_out_b, L1_xattn_Wq, L1_xattn_bq, L1_xattn_Wk, L1_xattn_bk, L1_xattn_Wv, L1_xattn_bv, L1_xattn_Wo, L1_xattn_qn_w, L1_xattn_kn_w, L1_ffn_router_w, L1_ffn_gate_w, L1_ffn_up_w, L1_ffn_down_w, L1_ffn_s_gate_w, L1_ffn_s_gate_b, L1_ffn_s_up_w, L1_ffn_s_up_b, L1_ffn_s_down_w, L1_ffn_s_down_b):
    import jax
    import jax.numpy as jnp

    def _L0_xattn_ref(x, mask, k_cache, v_cache, wq, wk, wv, wo):
        import jax, jax.numpy as jnp
        import numpy as np
        import math
        DIM = 512
        B, Q_LEN, KV_LEN = (8, 128, 1024)
        q = jnp.einsum('bsd,ed->bse', x, wq)
        k_new = jnp.einsum('bsd,ed->bse', x, wk)
        v_new = jnp.einsum('bsd,ed->bse', x, wv)
        k = jnp.concatenate([k_cache, k_new], axis=1)
        v = jnp.concatenate([v_cache, v_new], axis=1)
        scale = 1.0 / math.sqrt(q.shape[-1])
        scores = jnp.einsum('bqd,bkd->bqk', q, k) * scale
        attn = jax.nn.softmax(scores, axis=-1)
        out = jnp.einsum('bqk,bkd->bqd', attn, v)
        return jnp.einsum('bqd,ed->bqe', out, wo)

    def _L0_ffn_ref(x, gate_w, gate_b, val_w, val_b, out_w, out_b):
        import jax, jax.numpy as jnp
        import numpy as np
        D_MODEL = 512
        HIDDEN = 4 * D_MODEL
        B, S = (2, 1024)

        def bit_linear(x, w, b):
            gamma_x = jnp.clip(jnp.max(jnp.abs(x), axis=-1, keepdims=True), 1e-05, None)
            scale_x = 127.0 / gamma_x
            x_dq = jnp.clip(jnp.round(x * scale_x), -128.0, 127.0) / scale_x
            x_ste = x + jax.lax.stop_gradient(x_dq - x)
            gamma_w = jnp.clip(jnp.mean(jnp.abs(w)), 1e-05, None)
            w_dq = jnp.clip(jnp.round(w / gamma_w), -1.0, 1.0) * gamma_w
            w_ste = w + jax.lax.stop_gradient(w_dq - w)
            return jnp.einsum('bsd,hd->bsh', x_ste, w_ste) + b
        gate = jax.nn.silu(bit_linear(x, gate_w, gate_b))
        val = bit_linear(x, val_w, val_b)
        return bit_linear(gate * val, out_w, out_b)

    def _L1_xattn_ref(hidden_states, encoder_hidden_states, attention_mask, Wq, bq, Wk, bk, Wv, bv, Wo, qn_w, kn_w):
        import jax, jax.numpy as jnp
        import numpy as np
        H = 512
        NH = 16
        NKV = 4
        HD = 128
        GROUPS = NH // NKV
        EPS = 1e-06
        B, S, SE = (1, 512, 1024)

        def _rmsnorm(x, w, eps=EPS):
            xf = x.astype(jnp.float32)
            var = jnp.mean(xf * xf, axis=-1, keepdims=True)
            return (xf * jax.lax.rsqrt(var + eps)).astype(x.dtype) * w
        b, s, _ = hidden_states.shape
        se = encoder_hidden_states.shape[1]
        q = (hidden_states @ Wq + bq).reshape(b, s, NH, HD).transpose(0, 2, 1, 3)
        k = (encoder_hidden_states @ Wk + bk).reshape(b, se, NKV, HD).transpose(0, 2, 1, 3)
        v = (encoder_hidden_states @ Wv + bv).reshape(b, se, NKV, HD).transpose(0, 2, 1, 3)
        k = jnp.repeat(k, GROUPS, axis=1)
        v = jnp.repeat(v, GROUPS, axis=1)
        q = _rmsnorm(q, qn_w)
        k = _rmsnorm(k, kn_w)
        scale = 1.0 / np.sqrt(HD).astype(np.float32)
        scores = jnp.einsum('bhsd,bhed->bhse', q, k) * scale
        scores = scores + attention_mask[:, None, :, :]
        probs = jax.nn.softmax(scores.astype(jnp.float32), axis=-1).astype(q.dtype)
        out = jnp.einsum('bhse,bhed->bhsd', probs, v)
        out = out.transpose(0, 2, 1, 3).reshape(b, s, NH * HD)
        return out @ Wo

    def _L1_ffn_ref(hidden_states, router_w, gate_w, up_w, down_w, s_gate_w, s_gate_b, s_up_w, s_up_b, s_down_w, s_down_b):
        import jax, jax.numpy as jnp
        import numpy as np
        B, S, H, I, E, TOP_K, NS = (2, 512, 512, 352, 8, 2, 2)
        SI = I * NS
        INIT = 0.02
        b, s, h = hidden_states.shape
        x = hidden_states.reshape(-1, h)
        T = x.shape[0]
        num_experts = router_w.shape[0]
        logits = x @ router_w.T
        probs = jax.nn.softmax(logits.astype(jnp.float32), axis=-1)
        topk_w, topk_idx = jax.lax.top_k(probs, TOP_K)
        topk_w = topk_w / jnp.sum(topk_w, axis=-1, keepdims=True)
        combine = jnp.zeros((T, num_experts), probs.dtype)
        combine = combine.at[jnp.arange(T)[:, None], topk_idx].add(topk_w)

        def expert_step(acc, ws):
            gw, uw, dw, ce = ws
            out = jax.nn.silu(x @ gw) * (x @ uw) @ dw
            return (acc + ce[:, None].astype(out.dtype) * out, None)
        moe_out, _ = jax.lax.scan(expert_step, jnp.zeros_like(x), (gate_w, up_w, down_w, combine.T))
        shared = jax.nn.silu(x @ s_gate_w + s_gate_b) * (x @ s_up_w + s_up_b) @ s_down_w + s_down_b
        return (moe_out + shared).reshape(b, s, h)
    x = x + _L0_xattn_ref(_layernorm(x, axis=-1), mask_BxSx4224_bf0, ctx_2048, ctx_2048, L0_xattn_wq, L0_xattn_wk, L0_xattn_wv, L0_xattn_wo)
    x = x + _L0_ffn_ref(_layernorm(x, axis=-1), L0_ffn_gate_w, L0_ffn_gate_b, L0_ffn_val_w, L0_ffn_val_b, L0_ffn_out_w, L0_ffn_out_b)
    x = x + _L1_xattn_ref(_layernorm(x, axis=-1), ctx_2048, mask_1xSxS2_ff0, L1_xattn_Wq, L1_xattn_bq, L1_xattn_Wk, L1_xattn_bk, L1_xattn_Wv, L1_xattn_bv, L1_xattn_Wo, L1_xattn_qn_w, L1_xattn_kn_w)
    x = x + _L1_ffn_ref(_layernorm(x, axis=-1), L1_ffn_router_w, L1_ffn_gate_w, L1_ffn_up_w, L1_ffn_down_w, L1_ffn_s_gate_w, L1_ffn_s_gate_b, L1_ffn_s_up_w, L1_ffn_s_up_b, L1_ffn_s_down_w, L1_ffn_s_down_b)
    return x

_drawn_inputs = setup_inputs


def setup_inputs(seed=0):
    import zlib

    import numpy as np

    out = dict(_drawn_inputs(seed))
    spreads = {'L0_ffn_gate_b': (0.0, 0.8),
     'L0_ffn_val_b': (0.0, 0.659),
     'L0_ffn_out_b': (0.0, 0.1),
     'L1_xattn_qn_w': (1.0, 0.6),
     'L1_xattn_kn_w': (1.0, 0.6),
     'L1_ffn_s_gate_b': (0.0, 0.651),
     'L1_ffn_s_up_b': (0.0, 0.677),
     'L1_ffn_s_down_b': (0.0, 0.1)}
    factors = {'L1_xattn_bq': 8.0, 'L1_xattn_bk': 8.0, 'L1_xattn_bv': 3.264}
    for name, (base, spread) in spreads.items():
        noise = np.random.default_rng([zlib.crc32(name.encode()), seed]).standard_normal(out[name].shape)
        drawn = base * np.exp(spread * noise) if base else spread * noise
        out[name] = jnp.asarray(drawn.astype(out[name].dtype))
    for name, factor in factors.items():
        out[name] = (out[name] * factor).astype(out[name].dtype)
    return out
```

```python
from contextlib import ExitStack

import concourse.bass as bass
from concourse import mybir

ALU = mybir.AluOpType
ACT = mybir.ActivationFunctionType
AX = mybir.AxisListType
F32 = mybir.dt.float32
F32R = mybir.dt.float32r
BF16 = mybir.dt.bfloat16
U32 = mybir.dt.uint32

P = 128
D = 512
KD = D // P
ROUND = 12582912.0
LN_EPS = 1e-5


def at(count):
    return count + 1


class Phase(ExitStack):

    def __init__(self, nc):
        super().__init__()
        self.nc, self.semaphores, self.from_zero = nc, [], []

    def semaphore(self, name):
        self.semaphores.append(self.nc.alloc_semaphore(name=name))
        return self.semaphores[-1]

    def queue_semaphore(self, name):
        self.from_zero.append(self.nc.alloc_semaphore(name=name))
        return self.from_zero[-1]

    def start(self):
        for s in self.semaphores:
            self.nc.gpsimd.sem_inc(s, 1)
        self.nc.all_engine_barrier()

    def __exit__(self, *exc):
        super().__exit__(*exc)
        self.nc.clear_and_free_semaphores(self.semaphores + self.from_zero)


class Pair:

    def __init__(self, ctx, nc, name, shape):
        self.hi = ctx.enter_context(nc.sbuf_tensor(name + "_hi", shape, F32R))
        self.lo = ctx.enter_context(nc.sbuf_tensor(name + "_lo", shape, F32R))


def f32(ap):
    return ap.bitcast(F32)


def matmul3(pe, out, w, x, first, last):
    pe.matmul(out, w[1], x[0], start=first, stop=False)
    pe.matmul(out, w[0], x[1], start=False, stop=False)
    return pe.matmul(out, w[0], x[0], start=False, stop=last)


def part(pair, *index):
    return pair.hi[index], pair.lo[index]


class Flow:

    def __init__(self, ctx, nc, name):
        self.mm = ctx.semaphore(name + "_product")
        self.hi = ctx.semaphore(name + "_hi_written")
        self.lo = ctx.semaphore(name + "_lo_written")


def layernorm_stats(dve, ctx_sems, X, stats, mv, tiles):
    s_stats, s_mv = ctx_sems
    for t in range(tiles):
        dve.bn_stats(stats[:, t, :], X[:, t, :]).then_inc(s_stats, 1)
    for t in range(tiles):
        dve.wait_ge(s_stats, at(t + 1))
        dve.bn_aggr(mv[:, t, :], stats[:, t, :]).then_inc(s_mv, 1)


def attention0(nc, banks, X, eps, ident, x_dram, ctx_dram, ctxT_dram, w_dram, B, S):
    T = B * S // P
    QT = S // P
    KT = 2 * QT
    SCALE = float(D) ** -0.5
    with Phase(nc) as ctx:
        def sb(name, shape, dt=F32):
            return ctx.enter_context(nc.sbuf_tensor("a0_" + name, shape, dt))

        def sem(name):
            return ctx.semaphore("a0_" + name)

        def pair(name, shape):
            return Pair(ctx, nc, "a0_" + name, shape)

        def flow(name):
            return Flow(ctx, nc, "a0_" + name)

        W = [pair(n, [P, KD, D]) for n in ("wq", "wk", "wv", "wo")]
        wq, wk, wv, wo = W
        wraw = [sb(f"wraw{j}", [P, KD, D]) for j in range(2)]
        stats = sb("stats", [P, T, 6])
        mv = sb("mv", [P, T, 2])
        std = sb("std", [P, T])
        rstd = sb("rstd", [P, T])
        xn = sb("xn", [P, QT, D])
        xT = pair("xT", [P, KD, S])
        qT = pair("qT", [P, KD, S])
        kT = pair("kT", [P, KD, 2 * S])
        V = pair("V", [P, KT, D])
        cTraw = sb("cTraw", [P, KD, S])
        craw = sb("craw", [P, QT, D])
        probs = sb("probs", [P, QT, 2 * S])
        pT = pair("pT", [P, KT, S])
        oT = pair("oT", [P, KD, S])
        nmax = sb("nmax", [P, QT])
        den = sb("den", [P, QT])
        rden = sb("rden", [P, QT])
        bank = banks

        s_x = sem("x_loaded")
        s_w = [sem(f"w{j}_loaded") for j in range(4)]
        s_whi = sem("w_hi_written")
        s_wlo = sem("w_lo_written")
        s_stats, s_mv, s_std, s_rstd = sem("stats"), sem("mean_var"), sem("std"), sem("rstd")
        s_cT, s_c = sem("ctxT_loaded"), sem("ctx_loaded")
        s_cThi, s_cTlo = sem("ctxT_hi"), sem("ctxT_lo")
        s_chi, s_clo = sem("ctx_hi"), sem("ctx_lo")
        s_xn = sem("xn")
        tr, q, k, v, o, pt = (flow(n) for n in ("xT", "q", "k", "v", "o", "pT"))
        s_scores, s_nmax, s_exp, s_rden = sem("scores"), sem("nmax"), sem("exp"), sem("rden")
        s_proj, s_added = sem("projected"), sem("added")

        ctx.start()
        block = ctx.enter_context(nc.Block())

        @block.sync
        def _(sp):
            for j in (0, 1):
                sp.dma_start(wraw[j][:], w_dram[j]).then_inc(s_w[j], 16)
            sp.dma_start(X[:], x_dram).then_inc(s_x, 16)
            for j in (2, 3):
                sp.wait_ge(s_wlo, at(j - 1))
                sp.dma_start(wraw[j - 2][:], w_dram[j]).then_inc(s_w[j], 16)
            with sp.Fori(0, B) as i:
                sp.wait_ge(s_cTlo, at(i))
                sp.dma_start(cTraw[:], ctxT_dram[:, :, bass.ds(i * S, S)]).then_inc(s_cT, 16)
                sp.wait_ge(s_clo, at(i))
                sp.dma_start(craw[:], ctx_dram[:, bass.ds(i * QT, QT), :]).then_inc(s_c, 16)

        @block.gpsimd
        def _(pool):
            with pool.Fori(0, B) as i:
                pool.wait_ge(s_cThi, at(i + 1))
                pool.tensor_tensor(kT.lo[:, :, 0:S], cTraw[:], f32(kT.hi[:, :, 0:S]), ALU.subtract).then_inc(s_cTlo, 1)
                pool.wait_ge(s_chi, at(i + 1))
                pool.tensor_tensor(V.lo[:, 0:QT, :], craw[:], f32(V.hi[:, 0:QT, :]), ALU.subtract).then_inc(s_clo, 1)

        @block.scalar
        def _(act):
            for j in range(4):
                act.wait_ge(s_w[j], at(16))
                act.activation(W[j].hi[:], wraw[j % 2][:], ACT.Copy).then_inc(s_whi, 1)
                if j == 0:
                    act.wait_ge(s_mv, at(T))
                    act.activation(std[:], mv[:, :, 1], ACT.Sqrt, bias=eps[:]).then_inc(s_std, 1)
            with act.Fori(0, B) as i:
                act.wait_ge(s_cT, at(i * 16 + 16))
                act.activation(kT.hi[:, :, 0:S], cTraw[:], ACT.Copy).then_inc(s_cThi, 1)
                act.wait_ge(s_c, at(i * 16 + 16))
                act.activation(V.hi[:, 0:QT, :], craw[:], ACT.Copy).then_inc(s_chi, 1)
                for t in range(QT):
                    act.wait_ge(tr.mm, at(i * QT + t + 1))
                    act.activation(xT.hi[:, :, t * P:(t + 1) * P],
                                   bank[t][:].rearrange("p (k s) -> p k s", k=KD), ACT.Copy).then_inc(tr.hi, 1)
                for n, (f, dst, b0, scale) in enumerate(((q, qT.hi, 2, SCALE), (k, kT.hi, 4, 1.0))):
                    for m in range(2):
                        act.wait_ge(f.mm, at(i * 2 + m + 1))
                        dd = dst[:, 2 * m:2 * m + 2, 0:S] if n == 0 else dst[:, 2 * m:2 * m + 2, S:2 * S]
                        act.activation(dd, bank[b0 + m][:].rearrange("p (k s) -> p k s", k=2), ACT.Copy,
                                       scale=scale).then_inc(f.hi, 1)
                for t in range(QT):
                    act.wait_ge(v.mm, at(i * QT + t + 1))
                    act.activation(V.hi[:, QT + t, :], bank[6 + t][:], ACT.Copy).then_inc(v.hi, 1)
                for t in range(QT):
                    act.wait_ge(s_nmax, at(i * QT + t + 1))
                    act.activation(probs[:, t, :], bank[t][:], ACT.Exp, bias=nmax[:, t:t + 1],
                                   accum_out=den[:, t:t + 1]).then_inc(s_exp, 1)
                for t in range(QT):
                    act.wait_ge(pt.mm, at(i * QT + t + 1))
                    act.activation(pT.hi[:, :, t * P:(t + 1) * P],
                                   bank[2 + t][:].rearrange("p (k s) -> p k s", k=KT), ACT.Copy).then_inc(pt.hi, 1)
                for m in range(2):
                    act.wait_ge(o.mm, at(i * 2 + m + 1))
                    if m == 0:
                        act.wait_ge(s_proj, at(i * QT))
                    act.activation(oT.hi[:, 2 * m:2 * m + 2, :],
                                   bank[4 + m][:].rearrange("p (k s) -> p k s", k=2), ACT.Copy).then_inc(o.hi, 1)

        @block.vector
        def _(dve):
            dve.wait_ge(s_x, at(16))
            layernorm_stats(dve, (s_stats, s_mv), X, stats, mv, T)
            dve.wait_ge(s_std, at(1))
            dve.reciprocal(rstd[:], std[:]).then_inc(s_rstd, 1)
            for j in range(4):
                dve.wait_ge(s_whi, at(j + 1))
                dve.tensor_tensor(W[j].lo[:], wraw[j % 2][:], f32(W[j].hi[:]), ALU.subtract).then_inc(s_wlo, 1)
            dve.wait_ge(s_rstd, at(1))
            with dve.Fori(0, B) as i:
                for t in range(QT):
                    dve.tensor_scalar(xn[:, t, :], X[:, bass.ds(i * QT + t, 1), :], mv[:, bass.ds(i * QT + t, 1), 0],
                                      rstd[:, bass.ds(i * QT + t, 1)], ALU.subtract, ALU.mult).then_inc(s_xn, 1)
                for t in range(QT):
                    dve.wait_ge(tr.hi, at(i * QT + t + 1))
                    dst = slice(t * P, (t + 1) * P)
                    dve.tensor_tensor(xT.lo[:, :, dst], bank[t][:].rearrange("p (k s) -> p k s", k=KD),
                                      f32(xT.hi[:, :, dst]), ALU.subtract).then_inc(tr.lo, 1)
                for n, (f, dst, b0, scale) in enumerate(((q, qT, 2, SCALE), (k, kT, 4, 1.0))):
                    for m in range(2):
                        dve.wait_ge(f.hi, at(i * 2 + m + 1))
                        cols = slice(0, S) if n == 0 else slice(S, 2 * S)
                        dve.scalar_tensor_tensor(dst.lo[:, 2 * m:2 * m + 2, cols],
                                                 bank[b0 + m][:].rearrange("p (k s) -> p k s", k=2), scale,
                                                 f32(dst.hi[:, 2 * m:2 * m + 2, cols]), ALU.mult,
                                                 ALU.subtract).then_inc(f.lo, 1)
                for t in range(QT):
                    dve.wait_ge(v.hi, at(i * QT + t + 1))
                    dve.tensor_tensor(V.lo[:, QT + t, :], bank[6 + t][:], f32(V.hi[:, QT + t, :]),
                                      ALU.subtract).then_inc(v.lo, 1)
                for t in range(QT):
                    dve.wait_ge(s_scores, at(i * QT + t + 1))
                    dve.tensor_reduce(nmax[:, t:t + 1], bank[t][:], AX.X, ALU.max, negate=True).then_inc(s_nmax, 1)
                for t in range(QT):
                    dve.wait_ge(s_exp, at(i * QT + t + 1))
                    dve.reciprocal(rden[:, t:t + 1], den[:, t:t + 1]).then_inc(s_rden, 1)
                for t in range(QT):
                    dve.wait_ge(pt.hi, at(i * QT + t + 1))
                    dst = slice(t * P, (t + 1) * P)
                    dve.tensor_tensor(pT.lo[:, :, dst], bank[2 + t][:].rearrange("p (k s) -> p k s", k=KT),
                                      f32(pT.hi[:, :, dst]), ALU.subtract).then_inc(pt.lo, 1)
                for m in range(2):
                    dve.wait_ge(o.hi, at(i * 2 + m + 1))
                    dve.tensor_tensor(oT.lo[:, 2 * m:2 * m + 2, :],
                                      bank[4 + m][:].rearrange("p (k s) -> p k s", k=2),
                                      f32(oT.hi[:, 2 * m:2 * m + 2, :]), ALU.subtract).then_inc(o.lo, 1)
                for t in range(QT):
                    dve.wait_ge(s_proj, at(i * QT + t + 1))
                    dve.wait_ge(s_rden, at(i * QT + t + 1))
                    row = X[:, bass.ds(i * QT + t, 1), :]
                    dve.scalar_tensor_tensor(row, bank[6 + t][:].rearrange("p (a n) -> p a n", a=1),
                                             rden[:, t:t + 1], row, ALU.mult, ALU.add).then_inc(s_added, 1)

        @block.tensor
        def _(pe):
            with pe.Fori(0, B) as i:
                for t in range(QT):
                    pe.wait_ge(s_xn, at(i * QT + t + 1))
                    for c in range(KD):
                        last = pe.transpose(bank[t][:, c * P:(c + 1) * P], xn[:, t, c * P:(c + 1) * P], ident[:])
                    last.then_inc(tr.mm, 1)
                pe.wait_ge(tr.lo, at(i * QT + QT))
                for n, (f, w, b0) in enumerate(((q, wq, 2), (k, wk, 4))):
                    pe.wait_ge(s_wlo, at(n + 1))
                    for m in range(2):
                        for h in range(2):
                            e = 2 * m + h
                            for c in range(KD):
                                last = matmul3(pe, bank[b0 + m][:, h * S:(h + 1) * S],
                                               part(w, slice(None), c, slice(e * P, (e + 1) * P)),
                                               part(xT, slice(None), c), c == 0, c == KD - 1)
                        last.then_inc(f.mm, 1)
                pe.wait_ge(s_wlo, at(3))
                pe.wait_ge(s_added, at(i * QT))
                for t in range(QT):
                    for c in range(KD):
                        last = matmul3(pe, bank[6 + t][:], part(xT, slice(None), c, slice(t * P, (t + 1) * P)),
                                       part(wv, slice(None), c), c == 0, c == KD - 1)
                    last.then_inc(v.mm, 1)
                pe.wait_ge(q.lo, at(i * 2 + 2))
                pe.wait_ge(k.lo, at(i * 2 + 2))
                pe.wait_ge(s_cTlo, at(i + 1))
                for t in range(QT):
                    for c in range(KD):
                        last = matmul3(pe, bank[t][:], part(qT, slice(None), c, slice(t * P, (t + 1) * P)),
                                       part(kT, slice(None), c), c == 0, c == KD - 1)
                    last.then_inc(s_scores, 1)
                for t in range(QT):
                    pe.wait_ge(s_exp, at(i * QT + t + 1))
                    for c in range(KT):
                        last = pe.transpose(bank[2 + t][:, c * P:(c + 1) * P], probs[:, t, c * P:(c + 1) * P],
                                            ident[:])
                    last.then_inc(pt.mm, 1)
                pe.wait_ge(pt.lo, at(i * QT + QT))
                pe.wait_ge(v.lo, at(i * QT + QT))
                pe.wait_ge(s_clo, at(i + 1))
                for m in range(2):
                    for h in range(2):
                        e = 2 * m + h
                        for c in range(KT):
                            last = matmul3(pe, bank[4 + m][:, h * S:(h + 1) * S],
                                           part(V, slice(None), c, slice(e * P, (e + 1) * P)),
                                           part(pT, slice(None), c), c == 0, c == KT - 1)
                    last.then_inc(o.mm, 1)
                pe.wait_ge(o.lo, at(i * 2 + 2))
                pe.wait_ge(s_wlo, at(4))
                for t in range(QT):
                    for c in range(KD):
                        last = matmul3(pe, bank[6 + t][:], part(oT, slice(None), c, slice(t * P, (t + 1) * P)),
                                       part(wo, slice(None), c), c == 0, c == KD - 1)
                    last.then_inc(s_proj, 1)


def bitlinear_weights(nc, banks, eps, ones, w_dram, wq, gamma):
    N = 3
    FR = w_dram[0].shape[1] * w_dram[0].shape[2]
    CH = 4
    C = FR // CH
    with Phase(nc) as ctx:
        def sb(name, shape, dt=F32):
            return ctx.enter_context(nc.sbuf_tensor("bw_" + name, shape, dt))

        def sem(name):
            return ctx.semaphore("bw_" + name)

        raw = [sb(f"raw{j}", [P, FR]) for j in range(N)]
        junk = sb("junk", [P, FR], BF16)
        magic = sb("magic", [P, 1])
        asum = sb("asum", [P, N])
        rgamma = sb("rgamma", [P, N])
        tot = banks[0]
        s_raw = [sem(f"raw{j}_loaded") for j in range(N)]
        s_magic, s_asum, s_tot, s_g, s_rg = (sem(n) for n in ("magic", "abs_sum", "total", "gamma", "rgamma"))
        s_sc, s_min, s_done = sem("scaled"), sem("min"), sem("ternary")
        ctx.start()
        block = ctx.enter_context(nc.Block())

        @block.sync
        def _(sp):
            for j in range(N):
                sp.dma_start(raw[j][:].rearrange("p (k n) -> p k n", k=w_dram[j].shape[1]),
                             w_dram[j]).then_inc(s_raw[j], 16)

        @block.scalar
        def _(act):
            for j in range(N):
                act.wait_ge(s_raw[j], at(16))
                if j:
                    act.wait_ge(s_asum, at(j))
                act.activation(junk[:], raw[j][:], ACT.Abs, accum_out=asum[:, j:j + 1]).then_inc(s_asum, 1)

        @block.tensor
        def _(pe):
            for j in range(N):
                pe.wait_ge(s_asum, at(j + 1))
                pe.wait_ge(s_g, at(j))
                pe.matmul(tot[:, j:j + 1], ones[:], asum[:, j:j + 1], start=True, stop=True).then_inc(s_tot, 1)

        @block.gpsimd
        def _(pool):
            pass

        @block.vector
        def _(dve):
            n = 0
            for j in range(N):
                dve.wait_ge(s_tot, at(j + 1))
                dve.tensor_scalar(gamma[:, j:j + 1], tot[:, j:j + 1], 1.0 / (P * FR), 1e-5, ALU.mult,
                                  ALU.max).then_inc(s_g, 1)
                dve.wait_ge(s_g, at(j + 1))
                dve.reciprocal(rgamma[:, j:j + 1], gamma[:, j:j + 1]).then_inc(s_rg, 1)
                dve.wait_ge(s_rg, at(j + 1))
                w = wq[j][:].rearrange("p k n -> p (k n)")
                dve.tensor_scalar(raw[j][:], raw[j][:], rgamma[:, j:j + 1], ROUND, ALU.mult, ALU.add).then_inc(s_sc, 1)
                dve.wait_ge(s_sc, at(j + 1))
                dve.tensor_scalar(w, raw[j][:], ROUND, 1.0, ALU.subtract, ALU.min).then_inc(s_min, 1)
                dve.wait_ge(s_min, at(j + 1))
                dve.tensor_scalar(w, w, -1.0, None, ALU.max).then_inc(s_done, 1)


def ffn0(nc, banks, X, eps, ident, ones, w_dram, b_dram, T):
    H = w_dram[0].shape[2]
    NH = H // 512
    KH = H // P
    with Phase(nc) as ctx:
        def sb(name, shape, dt=F32):
            return ctx.enter_context(nc.sbuf_tensor("f0_" + name, shape, dt))

        def sem(name):
            return ctx.semaphore("f0_" + name)

        wg, wv = (sb(n, [P, KD, H], BF16) for n in ("wg", "wv"))
        wo = sb("wo", [P, KH, D], BF16)
        gamma = sb("gamma", [P, 3])
        bitlinear_weights(nc, banks, eps, ones, w_dram, (wg, wv, wo), gamma)

        bg, bv = (sb(n, [P, H]) for n in ("bg", "bv"))
        bo = sb("bo", [P, D])
        identb = sb("identb", [P, P], BF16)
        stats = sb("stats", [P, T, 6])
        mv = sb("mv", [P, T, 2])
        std = sb("std", [P, T])
        rstd = sb("rstd", [P, T])
        xn = sb("xn", [P, D])
        xr = sb("xr", [P, D])
        xq = sb("xq", [P, D], BF16)
        xqT = sb("xqT", [P, KD, P], BF16)
        ax = sb("ax", [P, T])
        rx = sb("rx", [P, T])
        sx = sb("sx", [P, T])
        sg = sb("sg", [P, 2, T])
        g = sb("g", [P, 2, 512])
        gs = sb("gs", [P, 2, 512])
        vv = sb("vv", [P, 2, 512])
        h = sb("h", [P, H])
        hr = sb("hr", [P, H])
        hq = sb("hq", [P, H], BF16)
        hqT = sb("hqT", [P, KH, P], BF16)
        ah, rh, sh, so = (sb(n, [P, 1]) for n in ("ah", "rh", "sh", "so"))
        magic = sb("magic", [P, 1])
        gb, vb = banks[0:2], banks[2:4]
        hb = [b[:].bitcast(BF16) for b in banks[4:6]]
        xb, ob = banks[6][:].bitcast(BF16), banks[7]

        s_b = sem("biases_loaded")
        s_id = sem("constants")
        s_stats, s_mv, s_std, s_rstd = sem("stats"), sem("mean_var"), sem("std"), sem("rstd")
        s_xn, s_ax, s_axc, s_rx, s_sx, s_sgv, s_xr, s_xq = (sem(n) for n in (
            "xn", "absmax_x", "absmax_x_clipped", "rx", "sx", "sg", "x_rounded", "xq"))
        s_bo = sem("out_bias_added")
        s_xT, s_xTc = sem("xqT_product"), sem("xqT_copied")
        s_g, s_gb, s_gs, s_v, s_vb, s_h = (sem(n) for n in ("gate", "gate_biased", "silu", "val", "val_biased", "h"))
        s_ah, s_ahc, s_rh, s_sh, s_so, s_hr, s_hq = (sem(n) for n in (
            "absmax_h", "absmax_h_clipped", "rh", "sh", "so", "h_rounded", "hq"))
        s_hT, s_hTc, s_out, s_added = sem("hqT_product"), sem("hqT_copied"), sem("out"), sem("added")

        ctx.start()
        block = ctx.enter_context(nc.Block())

        @block.sync
        def _(sp):
            sp.dma_start(bg[:], b_dram[0].partition_broadcast(P)).then_inc(s_b, 16)
            sp.dma_start(bv[:], b_dram[1].partition_broadcast(P)).then_inc(s_b, 16)
            sp.dma_start(bo[:], b_dram[2].partition_broadcast(P)).then_inc(s_b, 16)

        @block.gpsimd
        def _(pool):
            pool.memset(magic[:], ROUND).then_inc(s_id, 1)
            pool.tensor_copy(identb[:], ident[:]).then_inc(s_id, 1)
            pool.wait_ge(s_b, at(48))

            def out_bias(t):
                pool.wait_ge(s_xn, at(t + 1))
                row = X[:, bass.ds(t, 1), :]
                pool.tensor_tensor(row, row, bo[:].rearrange("p (a n) -> p a n", a=1), ALU.add).then_inc(s_bo, 1)

            def hidden(t):
                for j in range(NH):
                    pool.wait_ge(s_vb, at(t * NH + j + 1))
                    pool.wait_ge(s_gs, at(t * NH + j + 1))
                    if j == 0:
                        pool.wait_ge(s_hr, at(t))
                    pool.tensor_tensor(h[:, j * 512:(j + 1) * 512], vv[:, j % 2, :], gs[:, j % 2, :],
                                       ALU.mult).then_inc(s_h, 1)

            out_bias(0)
            out_bias(1)
            hidden(0)
            with pool.Fori(0, T - 2) as t:
                out_bias(t + 2)
                hidden(t + 1)
            hidden(T - 1)

        @block.scalar
        def _(act):
            act.wait_ge(s_mv, at(T))
            act.activation(std[:], mv[:, :, 1], ACT.Sqrt, bias=eps[:]).then_inc(s_std, 1)
            act.wait_ge(s_id, at(2))

            def xT_copy(t):
                act.wait_ge(s_xT, at(t + 1))
                act.wait_ge(s_v, at(t * NH))
                act.activation(xqT[:], xb[:, 0:D].rearrange("p (k s) -> p k s", k=KD), ACT.Copy).then_inc(s_xTc, 1)

            def silu(t):
                for j in range(NH):
                    act.wait_ge(s_gb, at(t * NH + j + 1))
                    act.wait_ge(s_h, at(t * NH + max(j - 1, 0)))
                    act.activation(gs[:, j % 2, :], g[:, j % 2, :], ACT.Silu).then_inc(s_gs, 1)

            def h_round(t):
                act.wait_ge(s_sh, at(t + 1))
                act.wait_ge(s_hq, at(t))
                act.activation(hr[:], h[:], ACT.Identity, bias=magic[:], scale=sh[:]).then_inc(s_hr, 1)

            def hT_copy(t):
                for j in range(2):
                    act.wait_ge(s_hT, at(t * 2 + j + 1))
                    if j == 0:
                        act.wait_ge(s_out, at(t))
                    act.activation(hqT[:, 8 * j:8 * j + 8, :], hb[j][:].rearrange("p (k s) -> p k s", k=8),
                                   ACT.Copy).then_inc(s_hTc, 1)

            xT_copy(0)
            silu(0)
            xT_copy(1)
            h_round(0)
            with act.Fori(0, T - 2) as t:
                silu(t + 1)
                hT_copy(t)
                xT_copy(t + 2)
                h_round(t + 1)
            silu(T - 1)
            hT_copy(T - 2)
            h_round(T - 1)
            hT_copy(T - 1)

        @block.vector
        def _(dve):
            layernorm_stats(dve, (s_stats, s_mv), X, stats, mv, T)
            dve.wait_ge(s_std, at(1))
            dve.reciprocal(rstd[:], std[:]).then_inc(s_rstd, 1)
            dve.wait_ge(s_rstd, at(1))
            dve.wait_ge(s_b, at(48))

            def quantise_x(t):
                col = bass.ds(t, 1)
                dve.tensor_scalar(xn[:].rearrange("p (a n) -> p a n", a=1), X[:, col, :], mv[:, col, 0], rstd[:, col],
                                  ALU.subtract, ALU.mult).then_inc(s_xn, 1)
                dve.wait_ge(s_xn, at(t + 1))
                dve.tensor_reduce(ax[:, col], xn[:], AX.X, ALU.max, apply_absolute_value=True).then_inc(s_ax, 1)
                dve.wait_ge(s_ax, at(t + 1))
                dve.tensor_scalar(ax[:, col], ax[:, col], 1e-5, None, ALU.max).then_inc(s_axc, 1)
                dve.wait_ge(s_axc, at(t + 1))
                dve.reciprocal(rx[:, col], ax[:, col]).then_inc(s_rx, 1)
                for n in range(2):
                    dve.tensor_scalar(sg[:, n, col], ax[:, col], gamma[:, n:n + 1], 1.0 / 127, ALU.mult,
                                      ALU.mult).then_inc(s_sgv, 1)
                dve.wait_ge(s_rx, at(t + 1))
                dve.tensor_scalar(sx[:, col], rx[:, col], 127.0, None, ALU.mult).then_inc(s_sx, 1)
                dve.wait_ge(s_sx, at(t + 1))
                dve.tensor_scalar(xr[:], xn[:], sx[:, col], ROUND, ALU.mult, ALU.add).then_inc(s_xr, 1)
                dve.wait_ge(s_xr, at(t + 1))
                dve.wait_ge(s_xT, at(t))
                dve.tensor_scalar(xq[:], xr[:], ROUND, 127.0, ALU.subtract, ALU.min).then_inc(s_xq, 1)

            def hidden(t):
                dve.wait_ge(s_sgv, at(2 * t + 2))
                for j in range(NH):
                    cols = slice(j * 512, (j + 1) * 512)
                    for n, (s_in, src, dst, b, s_free, s_done) in enumerate(((s_g, gb, g, bg, s_gs, s_gb),
                                                                             (s_v, vb, vv, bv, s_h, s_vb))):
                        dve.wait_ge(s_in, at(t * NH + j + 1))
                        dve.wait_ge(s_free, at(t * NH + max(j - 1, 0)))
                        dve.scalar_tensor_tensor(dst[:, j % 2, :], src[j % 2][:], sg[:, n, bass.ds(t, 1)], b[:, cols],
                                                 ALU.mult, ALU.add).then_inc(s_done, 1)

            def quantise_h(t):
                dve.wait_ge(s_h, at(t * NH + NH))
                dve.tensor_reduce(ah[:], h[:], AX.X, ALU.max, apply_absolute_value=True).then_inc(s_ah, 1)
                dve.wait_ge(s_ah, at(t + 1))
                dve.tensor_scalar(ah[:], ah[:], 1e-5, None, ALU.max).then_inc(s_ahc, 1)
                dve.wait_ge(s_ahc, at(t + 1))
                dve.reciprocal(rh[:], ah[:]).then_inc(s_rh, 1)
                dve.wait_ge(s_rh, at(t + 1))
                dve.tensor_scalar(sh[:], rh[:], 127.0, None, ALU.mult).then_inc(s_sh, 1)

            def quantised_h(t):
                dve.wait_ge(s_hr, at(t + 1))
                dve.wait_ge(s_hT, at(2 * t))
                dve.tensor_scalar(hq[:], hr[:], ROUND, 127.0, ALU.subtract, ALU.min).then_inc(s_hq, 1)
                dve.wait_ge(s_added, at(t))
                dve.tensor_scalar(so[:], ah[:], gamma[:, 2:3], 1.0 / 127, ALU.mult, ALU.mult).then_inc(s_so, 1)

            def add(t):
                dve.wait_ge(s_out, at(t + 1))
                dve.wait_ge(s_bo, at(t + 1))
                dve.wait_ge(s_so, at(t + 1))
                row = X[:, bass.ds(t, 1), :]
                dve.scalar_tensor_tensor(row, ob[:].rearrange("p (a n) -> p a n", a=1), so[:], row, ALU.mult,
                                         ALU.add).then_inc(s_added, 1)

            quantise_x(0)
            quantise_x(1)
            hidden(0)
            quantise_h(0)
            quantised_h(0)
            with dve.Fori(0, T - 2) as t:
                quantise_x(t + 2)
                hidden(t + 1)
                quantise_h(t + 1)
                add(t)
                quantised_h(t + 1)
            hidden(T - 1)
            quantise_h(T - 1)
            add(T - 2)
            quantised_h(T - 1)
            add(T - 1)

        @block.tensor
        def _(pe):
            pe.wait_ge(s_id, at(2))

            def xT(t):
                pe.wait_ge(s_xq, at(t + 1))
                pe.wait_ge(s_xTc, at(t))
                for c in range(KD):
                    last = pe.transpose(xb[:, c * P:(c + 1) * P], xq[:, c * P:(c + 1) * P], identb[:])
                last.then_inc(s_xT, 1)

            def up(t):
                pe.wait_ge(s_xTc, at(t + 1))
                for j in range(NH):
                    for w, dst, s_free, s_done in ((wg, gb, s_gb, s_g), (wv, vb, s_vb, s_v)):
                        pe.wait_ge(s_free, at(t * NH + max(j - 1, 0)))
                        for c in range(KD):
                            last = pe.matmul(dst[j % 2][:], xqT[:, c, :], w[:, c, j * 512:(j + 1) * 512],
                                             start=c == 0, stop=c == KD - 1)
                        last.then_inc(s_done, 1)

            def hT(t):
                pe.wait_ge(s_hq, at(t + 1))
                for j in range(2):
                    pe.wait_ge(s_hTc, at(t * 2))
                    for c in range(8):
                        last = pe.transpose(hb[j][:, c * P:(c + 1) * P], hq[:, (8 * j + c) * P:(8 * j + c + 1) * P],
                                            identb[:])
                    last.then_inc(s_hT, 1)

            def down(t):
                pe.wait_ge(s_hTc, at(t * 2 + 2))
                pe.wait_ge(s_added, at(t))
                for c in range(KH):
                    last = pe.matmul(ob[:], hqT[:, c, :], wo[:, c, :], start=c == 0, stop=c == KH - 1)
                last.then_inc(s_out, 1)

            xT(0)
            up(0)
            xT(1)
            with pe.Fori(0, T - 2) as t:
                up(t + 1)
                hT(t)
                xT(t + 2)
                down(t)
            up(T - 1)
            hT(T - 2)
            down(T - 2)
            hT(T - 1)
            down(T - 1)


def keys_values1(nc, banks, X, eps, eps_rms, ident, ones, xT, ctxT_dram, wk_dram, wv_dram, bk_dram, bv_dram, qn_dram, kn_dram,
                 k_dram, v_dram, B, S, G):
    T = B * S // P
    QT = S // P
    HD = P
    with Phase(nc) as ctx:
        def sb(name, shape, dt=F32):
            return ctx.enter_context(nc.sbuf_tensor("kv_" + name, shape, dt))

        def sem(name):
            return ctx.semaphore("kv_" + name)

        wk, wv = (Pair(ctx, nc, "kv_" + n, [P, KD, D]) for n in ("wk", "wv"))
        wraw = sb("wraw", [P, KD, D])
        bk = sb("bk", [P, G])
        qn, kn, wn = (sb(n, [P, 1]) for n in ("qn", "kn", "wn"))
        bv = sb("bv", [P, D])
        stats = sb("stats", [P, T, 6])
        mv = sb("mv", [P, T, 2])
        std, rstd = sb("std", [P, T]), sb("rstd", [P, T])
        xn = sb("xn", [P, QT, D])
        cTraw = sb("cTraw", [P, KD, S])
        cT = Pair(ctx, nc, "kv_cT", [P, KD, S])
        kf, ksq, kstd, rk, kw = (sb(n, [P, G, S]) for n in ("kf", "ksq", "kstd", "rk", "kw"))
        vf = sb("vf", [P, QT, D])
        K = Pair(ctx, nc, "kv_K", [P, G, S])
        V = Pair(ctx, nc, "kv_V", [P, QT, D])
        tb, kb, sb2, vb = banks[0:2], banks[2:4], banks[4:6], banks[6:8]

        s_small, s_w, s_whi, s_wlo, s_wn = (sem(n) for n in ("small_loaded", "w_loaded", "w_hi", "w_lo", "norm_weight"))
        s_stats, s_mv, s_std, s_rstd = sem("stats"), sem("mean_var"), sem("std"), sem("rstd")
        s_c, s_chi, s_clo = sem("ctxT_loaded"), sem("ctxT_hi"), sem("ctxT_lo")
        s_xn = sem("xn")
        tr = Flow(ctx, nc, "kv_xT")
        s_k, s_kf, s_ksq, s_sum, s_kstd, s_rk, s_kw = (sem(n) for n in (
            "k_product", "k_biased", "k_squared", "k_sum", "k_std", "k_rstd", "k_normed"))
        s_khi, s_klo, s_v, s_vf, s_vhi, s_vlo = (sem(n) for n in ("k_hi", "k_lo", "v_product", "v_biased", "v_hi", "v_lo"))
        s_kst, s_vst = (ctx.queue_semaphore("kv_" + n) for n in ("k_stored", "v_stored"))
        s_stored = sem("stored")
        ctx.start()
        block = ctx.enter_context(nc.Block())

        @block.sync
        def _(sp):
            sp.dma_start(wraw[:], wk_dram).then_inc(s_w, 16)
            sp.dma_start(bk[:], bk_dram).then_inc(s_small, 16)
            sp.dma_start(qn[:], qn_dram).then_inc(s_small, 16)
            sp.dma_start(kn[:], kn_dram).then_inc(s_small, 16)
            sp.dma_start(bv[:], bv_dram.partition_broadcast(P)).then_inc(s_small, 16)
            sp.dma_start(cTraw[:], ctxT_dram[:, :, 0:S]).then_inc(s_c, 16)
            sp.wait_ge(s_wlo, at(1))
            sp.dma_start(wraw[:], wv_dram).then_inc(s_w, 16)

            with sp.Fori(0, B - 1) as i:
                sp.wait_ge(s_clo, at(i + 1))
                sp.dma_start(cTraw[:], ctxT_dram[:, :, bass.ds(i * S + S, S)]).then_inc(s_c, 16)

        @block.gpsimd
        def _(pool):
            with pool.Fori(0, B) as i:
                pool.wait_ge(s_klo, at(i + 1))
                for n, t in enumerate((K.hi, K.lo)):
                    pool.dma_start(k_dram[n][:, :, bass.ds(i * S, S)], f32(t[:])).then_inc(s_kst, 16)
                pool.wait_ge(s_vlo, at(i + 1))
                for n, t in enumerate((V.hi, V.lo)):
                    pool.dma_start(v_dram[n][:, bass.ds(i * QT, QT), :], f32(t[:])).then_inc(s_vst, 16)
                pool.wait_ge(s_kst, i * 32 + 32)
                pool.wait_ge(s_vst, i * 32 + 32)
                pool.sem_inc(s_stored, 1)

        @block.scalar
        def _(act):
            for j, w in enumerate((wk, wv)):
                act.wait_ge(s_w, at(16 * (j + 1)))
                act.activation(w.hi[:], wraw[:], ACT.Copy).then_inc(s_whi, 1)
                if j == 0:
                    act.wait_ge(s_mv, at(T))
                    act.activation(std[:], mv[:, :, 1], ACT.Sqrt, bias=eps[:]).then_inc(s_std, 1)
            act.wait_ge(s_small, at(64))
            with act.Fori(0, B) as i:
                act.wait_ge(s_c, at(i * 16 + 16))
                act.wait_ge(s_v, at(i * QT))
                act.activation(cT.hi[:], cTraw[:], ACT.Copy).then_inc(s_chi, 1)
                for g in range(G):
                    act.wait_ge(s_kf, at(i * G + g + 1))
                    act.activation(ksq[:, g, :], kf[:, g, :], ACT.Square).then_inc(s_ksq, 1)
                for t in range(QT):
                    act.wait_ge(tr.mm, at(i * QT + t + 1))
                    act.wait_ge(s_small, at(64))
                    act.activation(xT.hi[:, :, bass.ds(i * S + t * P, P)], tb[t][:].rearrange("p (k s) -> p k s", k=KD),
                                   ACT.Copy).then_inc(tr.hi, 1)
                for m in range(2):
                    act.wait_ge(s_sum, at(i * 2 + m + 1))
                    act.activation(kstd[:, 2 * m:2 * m + 2, :], sb2[m][:].rearrange("p (k s) -> p k s", k=2),
                                   ACT.Sqrt, bias=eps_rms[:], scale=1.0 / HD).then_inc(s_kstd, 1)
                act.wait_ge(s_vf, at(i * QT + QT))
                act.wait_ge(s_stored, at(i))
                act.activation(V.hi[:], vf[:], ACT.Copy).then_inc(s_vhi, 1)
                act.wait_ge(s_kw, at(i + 1))
                act.activation(K.hi[:], kw[:], ACT.Copy).then_inc(s_khi, 1)

        @block.vector
        def _(dve):
            layernorm_stats(dve, (s_stats, s_mv), X, stats, mv, T)
            dve.wait_ge(s_std, at(1))
            dve.reciprocal(rstd[:], std[:]).then_inc(s_rstd, 1)
            for j, w in enumerate((wk, wv)):
                dve.wait_ge(s_whi, at(j + 1))
                dve.tensor_tensor(w.lo[:], wraw[:], f32(w.hi[:]), ALU.subtract).then_inc(s_wlo, 1)
            dve.wait_ge(s_rstd, at(1))
            dve.wait_ge(s_small, at(64))
            dve.tensor_tensor(wn[:], qn[:], kn[:], ALU.mult).then_inc(s_wn, 1)
            dve.wait_ge(s_wn, at(1))
            with dve.Fori(0, B) as i:
                dve.wait_ge(s_chi, at(i + 1))
                dve.tensor_tensor(cT.lo[:], cTraw[:], f32(cT.hi[:]), ALU.subtract).then_inc(s_clo, 1)
                for t in range(QT):
                    col = bass.ds(i * QT + t, 1)
                    dve.tensor_scalar(xn[:, t:t + 1, :], X[:, col, :], mv[:, col, 0], rstd[:, col],
                                      ALU.subtract, ALU.mult).then_inc(s_xn, 1)
                for g in range(G):
                    dve.wait_ge(s_k, at(i * 2 + g // 2 + 1))
                    dve.wait_ge(s_kw, at(i))
                    dve.tensor_scalar(kf[:, g, :], kb[g // 2][:, (g % 2) * S:(g % 2 + 1) * S], bk[:, g:g + 1], None,
                                      ALU.add).then_inc(s_kf, 1)
                for t in range(QT):
                    dve.wait_ge(tr.hi, at(i * QT + t + 1))
                    cols = bass.ds(i * S + t * P, P)
                    dve.tensor_tensor(xT.lo[:, :, cols], tb[t][:].rearrange("p (k s) -> p k s", k=KD),
                                      f32(xT.hi[:, :, cols]), ALU.subtract).then_inc(tr.lo, 1)
                for t in range(QT):
                    dve.wait_ge(s_v, at(i * QT + t + 1))
                    dve.wait_ge(s_vlo, at(i))
                    dve.tensor_tensor(vf[:, t, :], vb[t][:], bv[:], ALU.add).then_inc(s_vf, 1)
                dve.wait_ge(s_kstd, at(i * 2 + 2))
                dve.reciprocal(rk[:], kstd[:]).then_inc(s_rk, 1)
                dve.wait_ge(s_rk, at(i + 1))
                dve.wait_ge(s_kf, at(i * G + G))
                dve.wait_ge(s_klo, at(i))
                dve.scalar_tensor_tensor(kw[:], kf[:], wn[:], rk[:], ALU.mult, ALU.mult).then_inc(s_kw, 1)
                dve.wait_ge(s_vhi, at(i + 1))
                dve.wait_ge(s_stored, at(i))
                dve.tensor_tensor(V.lo[:], vf[:], f32(V.hi[:]), ALU.subtract).then_inc(s_vlo, 1)
                dve.wait_ge(s_khi, at(i + 1))
                dve.tensor_tensor(K.lo[:], kw[:], f32(K.hi[:]), ALU.subtract).then_inc(s_klo, 1)

        @block.tensor
        def _(pe):
            with pe.Fori(0, B) as i:
                pe.wait_ge(s_wlo, at(1))
                pe.wait_ge(s_clo, at(i + 1))
                pe.wait_ge(s_kf, at(i * G))
                for g in range(G):
                    for c in range(KD):
                        last = matmul3(pe, kb[g // 2][:, (g % 2) * S:(g % 2 + 1) * S],
                                       part(wk, slice(None), c, slice(g * P, (g + 1) * P)),
                                       part(cT, slice(None), c), c == 0, c == KD - 1)
                    if g % 2:
                        last.then_inc(s_k, 1)
                for t in range(QT):
                    pe.wait_ge(s_xn, at(i * QT + t + 1))
                    for c in range(KD):
                        last = pe.transpose(tb[t][:, c * P:(c + 1) * P], xn[:, t, c * P:(c + 1) * P], ident[:])
                    last.then_inc(tr.mm, 1)
                pe.wait_ge(s_wlo, at(2))
                for t in range(QT):
                    pe.wait_ge(s_vf, at(i * QT + t))
                    for c in range(KD):
                        last = matmul3(pe, vb[t][:], part(cT, slice(None), c, slice(t * P, (t + 1) * P)),
                                       part(wv, slice(None), c), c == 0, c == KD - 1)
                    last.then_inc(s_v, 1)
                for m in range(2):
                    pe.wait_ge(s_ksq, at(i * G + 2 * m + 2))
                    pe.matmul(sb2[m][:], ones[:], ksq[:, 2 * m:2 * m + 2, :].rearrange("p k s -> p (k s)"),
                              start=True, stop=True).then_inc(s_sum, 1)


def attention1(nc, banks, X, ident, ones, xT, mask_dram, wq_dram, wo_dram, bq_dram, k_dram, v_dram, B, S, G):
    QT = S // P
    NB = 2
    C = NB * S
    NC = B // NB
    HG = 4
    CT = C // P
    U = NC * HG
    HD = P
    RMS_EPS = 1e-6
    with Phase(nc) as ctx:
        def sb(name, shape, dt=F32):
            return ctx.enter_context(nc.sbuf_tensor("a1_" + name, shape, dt))

        def sem(name):
            return ctx.semaphore("a1_" + name)

        def pair(name, shape):
            return Pair(ctx, nc, "a1_" + name, shape)

        wq, wo = pair("wq", [P, KD, HG * HD]), pair("wo", [P, HG, D])
        wraw = sb("wraw", [P, KD, D])
        bq = sb("bq", [P, G * HG])
        bqg = sb("bqg", [P, HG])
        mask = sb("mask", [P, QT, S])
        q = [pair(f"q{j}", [P, C]) for j in range(2)]
        sq = [sb(f"sq{j}", [P, C]) for j in range(2)]
        K = pair("K", [P, C])
        V = pair("V", [P, CT, HD])
        sc = [sb(f"scores{j}", [P, CT, S]) for j in range(2)]
        pT = [pair(f"pT{b}", [P, QT, S]) for b in range(NB)]
        oT = pair("oT", [P, HG, C])
        ssq = sb("ssq", [P, HG, CT])
        mhalf = sb("mhalf", [P, CT])
        rq = sb("rq", [P, HG, CT])
        nmax, den, rden = (sb(n, [P, 2, CT]) for n in ("nmax", "den", "rden"))
        qb, scb, ptb, ob, ssb = banks[0:2], banks[2:4], banks[4:6], banks[6], banks[7]

        s_small, s_const, s_bqg = sem("small_loaded"), sem("constants"), sem("group_bias")
        s_wload = ctx.queue_semaphore("a1_w_loaded")
        s_wqhi, s_wqlo, s_wohi, s_wolo = sem("wq_hi"), sem("wq_lo"), sem("wo_hi"), sem("wo_lo")
        s_k, s_v = sem("K_loaded"), sem("V_loaded")
        fq, ft, fo = (Flow(ctx, nc, "a1_" + n) for n in ("q", "pT", "oT"))
        s_sq, s_ssq, s_ssqc, s_rq = sem("q_squared"), sem("q_sum"), sem("q_sum_copied"), sem("q_rstd")
        s_sc, s_masked, s_nmax, s_exp, s_rden, s_p = (sem(n) for n in (
            "scores", "masked", "nmax", "exp", "rden", "probs"))
        s_out, s_added = sem("out"), sem("added")
        ctx.start()
        block = ctx.enter_context(nc.Block())


        @block.sync
        def _(sp):
            sp.dma_start(bq[:], bq_dram).then_inc(s_small, 16)
            sp.dma_start(mask[:], mask_dram).then_inc(s_small, 16)

            def load(g, c):
                n = g * NC + c
                cols = slice(c * C, (c + 1) * C)
                sp.wait_ge(s_sc, at(n * HG))
                sp.wait_ge(s_small, at(32))
                for m, t in enumerate((K.hi, K.lo)):
                    sp.dma_start(f32(t[:]).rearrange("p (a n) -> p a n", a=1), k_dram[m][:, bass.ds(g, 1), cols]).then_inc(s_k, 16)
                sp.wait_ge(fo.mm, at(n * HG))
                sp.wait_ge(s_small, at(32))
                for m, t in enumerate((V.hi, V.lo)):
                    sp.dma_start(f32(t[:]), v_dram[m][:, c * CT:(c + 1) * CT, bass.ds(g * HD, HD)]).then_inc(s_v, 16)

            with sp.Fori(0, G) as g:
                for c in range(NC):
                    load(g, c)

        @block.gpsimd
        def _(pool):
            def load(w, s_free, n):
                pool.dma_start(wraw[:], w).then_inc(s_wload, 16)

            pool.dma_start(wraw[:], wq_dram[:, :, 0:HG * HD]).then_inc(s_wload, 16)
            pool.memset(mhalf[:], -0.5).then_inc(s_const, 1)
            pool.wait_ge(s_const, at(1))

            def rstd(u, h):
                pool.wait_ge(s_ssqc, at(u + 1))
                pool.tensor_tensor(rq[:, h, :], ssq[:, h, :], mhalf[:], ALU.pow).then_inc(s_rq, 1)

            def wq_lo(g):
                pool.wait_ge(s_wqhi, at(g + 1))
                pool.tensor_tensor(wq.lo[:], wraw[:], f32(wq.hi[:]), ALU.subtract).then_inc(s_wqlo, 1)
                pool.wait_ge(s_wqlo, at(g + 1))
                pool.dma_start(wraw[:], wo_dram[:, bass.ds(g * HG, HG), :]).then_inc(s_wload, 16)

            def wo_lo(g, more):
                pool.wait_ge(s_wohi, at(g + 1))
                pool.tensor_tensor(wo.lo[:], wraw[:], f32(wo.hi[:]), ALU.subtract).then_inc(s_wolo, 1)
                if more:
                    pool.wait_ge(s_wolo, at(g + 1))
                    pool.dma_start(wraw[:], wq_dram[:, :, bass.ds((g + 1) * HG * HD, HG * HD)]).then_inc(s_wload, 16)

            def group(g, more):
                for c in range(NC):
                    u = g * U + c * HG
                    rstd(u + 1, 1)
                    if c == 0:
                        wo_lo(g, more)
                    rstd(u + 2, 2)
                    rstd(u + 3, 3)
                    if c == NC - 1 and more:
                        wq_lo(g + 1)
                    if c < NC - 1 or more:
                        rstd(u + 4, 0)

            wq_lo(0)
            rstd(0, 0)
            with pool.Fori(0, G - 1) as g:
                group(g, True)
            group(G - 1, False)

        @block.scalar
        def _(act):
            def wq_hi(g):
                act.wait_ge(s_wload, g * 32 + 16)
                act.wait_ge(fq.mm, at(g * U))
                act.wait_ge(fq.lo, at(g * U))
                act.activation(wq.hi[:], wraw[:], ACT.Copy).then_inc(s_wqhi, 1)
                act.activation(bqg[:], bq[:, bass.ds(g * HG, HG)], ACT.Copy).then_inc(s_bqg, 1)

            def wo_hi(g):
                act.wait_ge(s_wload, g * 32 + 32)
                act.wait_ge(s_out, at(g * NC * CT))
                act.activation(wo.hi[:], wraw[:], ACT.Copy).then_inc(s_wohi, 1)

            def queries(u, g, h, first=False):
                act.wait_ge(fq.mm, at(u + 1))
                if not first:
                    act.wait_ge(s_ssq, at(u - 1))
                act.wait_ge(s_bqg, at(g + 1))
                b = bqg[:, h:h + 1]
                act.activation(sq[h % 2][:], qb[h % 2][:], ACT.Square, bias=b).then_inc(s_sq, 1)
                act.activation(q[h % 2].hi[:], qb[h % 2][:], ACT.Identity, bias=b).then_inc(fq.hi, 1)

            def exp(u, h):
                for t in range(CT):
                    act.wait_ge(s_nmax, at(u * NB + t // QT + 1))
                    if t == 0:
                        act.wait_ge(s_rden, at(u * 1))
                    row = sc[h % 2][:, t, :]
                    act.activation(row, row, ACT.Exp, bias=nmax[:, h % 2, t:t + 1],
                                   accum_out=den[:, h % 2, t:t + 1]).then_inc(s_exp, 1)

            def transposed(u):
                for b in range(NB):
                    act.wait_ge(ft.mm, at(u * NB + b + 1))
                    act.activation(pT[b].hi[:], ptb[b][:].rearrange("p (k s) -> p k s", k=QT), ACT.Copy).then_inc(ft.hi, 1)

            def output(u, n, h):
                act.wait_ge(fo.mm, at(u + 1))
                if h == 0:
                    act.wait_ge(s_out, at(n * CT))
                act.activation(oT.hi[:, h, :], ob[:], ACT.Copy).then_inc(fo.hi, 1)

            def group(g, more):
                for c in range(NC):
                    u, n = g * U + c * HG, g * NC + c
                    exp(u, 0)
                    if c == 0:
                        wo_hi(g)
                    queries(u + 2, g, 2)
                    exp(u + 1, 1)
                    transposed(u)
                    output(u, n, 0)
                    queries(u + 3, g, 3)
                    if c == NC - 1 and more:
                        wq_hi(g + 1)
                    exp(u + 2, 2)
                    transposed(u + 1)
                    output(u + 1, n, 1)
                    exp(u + 3, 3)
                    transposed(u + 2)
                    output(u + 2, n, 2)
                    last = c == NC - 1
                    if not last or more:
                        queries(u + 4, g + 1 if last else g, 0)
                    transposed(u + 3)
                    output(u + 3, n, 3)
                    if not last or more:
                        queries(u + 5, g + 1 if last else g, 1)

            act.wait_ge(s_small, at(32))
            wq_hi(0)
            queries(0, 0, 0, True)
            queries(1, 0, 1, True)
            with act.Fori(0, G - 1) as g:
                group(g, True)
            group(G - 1, False)

        @block.vector
        def _(dve):
            def queries(u, g, h):
                dve.wait_ge(fq.hi, at(u + 1))
                dve.scalar_tensor_tensor(q[h % 2].lo[:], qb[h % 2][:], bqg[:, h:h + 1],
                                         f32(q[h % 2].hi[:]), ALU.add, ALU.subtract).then_inc(fq.lo, 1)

            def square_sums(u, h):
                dve.wait_ge(s_ssq, at(u + 1))
                dve.tensor_scalar(ssq[:, h, :], ssb[:, 0:CT], HD * RMS_EPS, None, ALU.add).then_inc(s_ssqc, 1)

            def scores(u, h):
                dve.wait_ge(s_rq, at(u + 1))
                for b in range(NB):
                    dve.wait_ge(s_sc, at(u * 1 + 1))
                    for t in range(QT):
                        i = b * QT + t
                        dve.scalar_tensor_tensor(sc[h % 2][:, i, :], scb[b][:, t * S:(t + 1) * S], rq[:, h, i:i + 1],
                                                 mask[:, t, :], ALU.mult, ALU.add).then_inc(s_masked, 1)
                for b in range(NB):
                    dve.wait_ge(s_masked, at(u * CT + QT * (b + 1)))
                    dve.tensor_reduce(nmax[:, h % 2, b * QT:(b + 1) * QT], sc[h % 2][:, b * QT:(b + 1) * QT, :], AX.X,
                                      ALU.max, negate=True).then_inc(s_nmax, 1)

            def normalise(u, h):
                dve.wait_ge(s_exp, at(u * CT + CT))
                dve.reciprocal(rden[:, h % 2, :], den[:, h % 2, :]).then_inc(s_rden, 1)
                dve.wait_ge(s_rden, at(u + 1))
                for t in range(CT):
                    row = sc[h % 2][:, t, :]
                    dve.tensor_scalar(row, row, rden[:, h % 2, t:t + 1], None, ALU.mult).then_inc(s_p, 1)

            def transposed(u):
                for b in range(NB):
                    dve.wait_ge(ft.hi, at(u * NB + b + 1))
                    dve.tensor_tensor(pT[b].lo[:], ptb[b][:].rearrange("p (k s) -> p k s", k=QT), f32(pT[b].hi[:]),
                                      ALU.subtract).then_inc(ft.lo, 1)

            def output(u, h):
                dve.wait_ge(fo.hi, at(u + 1))
                dve.tensor_tensor(oT.lo[:, h, :], ob[:], f32(oT.hi[:, h, :]), ALU.subtract).then_inc(fo.lo, 1)

            def add(n, c):
                for t in range(CT):
                    dve.wait_ge(s_out, at(n * CT + t + 1))
                    row = X[:, c * CT + t, :]
                    dve.tensor_tensor(row, row, scb[t % 2][:], ALU.add).then_inc(s_added, 1)

            def group(g, more):
                for c in range(NC):
                    u, n = g * U + c * HG, g * NC + c
                    last = c == NC - 1
                    square_sums(u + 1, 1)
                    scores(u, 0)
                    queries(u + 2, g, 2)
                    normalise(u, 0)
                    scores(u + 1, 1)
                    transposed(u)
                    output(u, 0)
                    normalise(u + 1, 1)
                    square_sums(u + 2, 2)
                    queries(u + 3, g, 3)
                    scores(u + 2, 2)
                    transposed(u + 1)
                    output(u + 1, 1)
                    normalise(u + 2, 2)
                    square_sums(u + 3, 3)
                    scores(u + 3, 3)
                    transposed(u + 2)
                    output(u + 2, 2)
                    normalise(u + 3, 3)
                    if not last or more:
                        queries(u + 4, g + 1 if last else g, 0)
                    transposed(u + 3)
                    output(u + 3, 3)
                    if not last or more:
                        square_sums(u + 4, 0)
                        queries(u + 5, g + 1 if last else g, 1)
                    add(n, c)

            dve.wait_ge(s_small, at(32))
            queries(0, 0, 0)
            square_sums(0, 0)
            queries(1, 0, 1)
            with dve.Fori(0, G - 1) as g:
                group(g, True)
            group(G - 1, False)

        @block.tensor
        def _(pe):
            def queries(u, g, c, h, first=False):
                if c == 0 and h == 0:
                    pe.wait_ge(s_wqlo, at(g + 1))
                if not first:
                    pe.wait_ge(fq.lo, at(u - 1))
                for k in range(KD):
                    last = matmul3(pe, qb[h % 2][:], part(wq, slice(None), k, slice(h * HD, (h + 1) * HD)),
                                   part(xT, slice(None), k, slice(c * C, (c + 1) * C)), k == 0, k == KD - 1)
                last.then_inc(fq.mm, 1)

            def square_sums(u, h):
                pe.wait_ge(s_sq, at(u + 1))
                pe.wait_ge(s_ssqc, at(u))
                for t in range(CT):
                    last = pe.matmul(ssb[:, t:t + 1], sq[h % 2][:, t * P:(t + 1) * P], ones[:, 0:1], start=True,
                                     stop=True)
                last.then_inc(s_ssq, 1)

            def scores(u, n, h):
                pe.wait_ge(fq.lo, at(u + 1))
                pe.wait_ge(s_masked, at(u * CT))
                if h == 0:
                    pe.wait_ge(s_added, at(n * CT))
                    pe.wait_ge(s_k, at(n * 32 + 32))
                for b in range(NB):
                    for t in range(QT):
                        i = b * QT + t
                        last = matmul3(pe, scb[b][:, t * S:(t + 1) * S],
                                       part(q[h % 2], slice(None), slice(i * P, (i + 1) * P)),
                                       part(K, slice(None), slice(b * S, (b + 1) * S)), True, True)
                last.then_inc(s_sc, 1)

            def transposed(u, h):
                for b in range(NB):
                    for t in range(QT):
                        i = b * QT + t
                        pe.wait_ge(s_p, at(u * CT + i + 1))
                        for k in range(QT):
                            last = pe.transpose(ptb[b][:, k * S + t * P:k * S + (t + 1) * P],
                                                sc[h % 2][:, i, k * P:(k + 1) * P], ident[:])
                    last.then_inc(ft.mm, 1)

            def output(u, n, h):
                if h == 0:
                    pe.wait_ge(s_v, at(n * 32 + 32))
                pe.wait_ge(fo.lo, at(u))
                for b in range(NB):
                    pe.wait_ge(ft.lo, at(u * NB + b + 1))
                    for k in range(QT):
                        last = matmul3(pe, ob[:, b * S:(b + 1) * S], part(V, slice(None), b * QT + k),
                                       part(pT[b], slice(None), k), k == 0, k == QT - 1)
                last.then_inc(fo.mm, 1)

            def project(u, n):
                pe.wait_ge(fo.lo, at(u + 4))
                pe.wait_ge(s_masked, at(u * CT + 4 * CT))
                for t in range(CT):
                    pe.wait_ge(s_added, at(n * CT + max(t - 1, 0)))
                    for k in range(HG):
                        last = matmul3(pe, scb[t % 2][:], part(oT, slice(None), k, slice(t * P, (t + 1) * P)),
                                       part(wo, slice(None), k), k == 0, k == HG - 1)
                    last.then_inc(s_out, 1)

            def group(g, more):
                for c in range(NC):
                    u, n = g * U + c * HG, g * NC + c
                    last = c == NC - 1
                    g2, c2 = (g + 1, 0) if last else (g, c + 1)
                    square_sums(u + 1, 1)
                    scores(u, n, 0)
                    queries(u + 2, g, c, 2)
                    scores(u + 1, n, 1)
                    transposed(u, 0)
                    output(u, n, 0)
                    square_sums(u + 2, 2)
                    queries(u + 3, g, c, 3)
                    scores(u + 2, n, 2)
                    transposed(u + 1, 1)
                    output(u + 1, n, 1)
                    square_sums(u + 3, 3)
                    scores(u + 3, n, 3)
                    transposed(u + 2, 2)
                    output(u + 2, n, 2)
                    if not last or more:
                        queries(u + 4, g2, c2, 0)
                    transposed(u + 3, 3)
                    output(u + 3, n, 3)
                    if not last or more:
                        square_sums(u + 4, 0)
                        queries(u + 5, g2, c2, 1)
                    if c == 0:
                        pe.wait_ge(s_wolo, at(g + 1))
                    project(u, n)

            queries(0, 0, 0, 0, True)
            queries(1, 0, 0, 1, True)
            square_sums(0, 0)
            with pe.Fori(0, G - 1) as g:
                group(g, True)
            group(G - 1, False)


def router(nc, banks, X, eps, ident, xT, combine, rw_dram, sdb_dram, T, E):
    TOP = 2
    with Phase(nc) as ctx:
        def sb(name, shape, dt=F32):
            return ctx.enter_context(nc.sbuf_tensor("r_" + name, shape, dt))

        def sem(name):
            return ctx.semaphore("r_" + name)

        rw = sb("rw", [P, KD, E])
        sdb = sb("sdb", [P, D])
        stats = sb("stats", [P, T, 6])
        mv = sb("mv", [P, T, 2])
        std, rstd = sb("std", [P, T]), sb("rstd", [P, T])
        xn = [sb(f"xn{j}", [P, D]) for j in range(2)]
        xt = [sb(f"xt{j}", [P, KD, P]) for j in range(2)]
        logits = sb("logits", [P, T, E])
        nmax = sb("nmax", [P, T])
        ex = sb("ex", [P, T, E])
        top = sb("top", [P, T, 8])
        topi = sb("topi", [P, T, 8], U32)
        atf = sb("atf", [P, T, 8])
        expert = sb("expert", [P, E])
        hot = sb("hot", [P, T, TOP, E])
        tsum, rsum = sb("tsum", [P, T]), sb("rsum", [P, T])
        tb, lb = banks[0:2], banks[2:4]
        s_ld, s_const = sem("loaded"), sem("constants")
        s_stats, s_mv, s_std, s_rstd = sem("stats"), sem("mean_var"), sem("std"), sem("rstd")
        s_xn, s_bias, s_tr, s_xt, s_hi, s_lo = (sem(n) for n in ("xn", "bias_added", "transposed", "xt", "xT_hi", "xT_lo"))
        s_log, s_logc, s_nmax, s_sub, s_exp, s_top, s_at = (sem(n) for n in (
            "logits", "logits_copied", "nmax", "sub", "exp", "top", "at"))
        s_atf, s_sum, s_rsum, s_hot, s_comb = (sem(n) for n in ("atf", "sum", "rsum", "hot", "combine"))
        ctx.start()
        block = ctx.enter_context(nc.Block())

        @block.sync
        def _(sp):
            sp.dma_start(rw[:], rw_dram).then_inc(s_ld, 16)
            sp.dma_start(sdb[:], sdb_dram.partition_broadcast(P)).then_inc(s_ld, 16)

        @block.gpsimd
        def _(pool):
            pool.iota(expert[:], pattern=[[1, E]], base=0, channel_multiplier=0,
                      allow_small_or_imprecise_dtypes=True).then_inc(s_const, 1)
            pool.memset(combine[:, :, E:], 1.0).then_inc(s_const, 1)
            pool.wait_ge(s_ld, at(32))
            with pool.Fori(0, T) as t:
                pool.wait_ge(s_xn, at(t + 1))
                row = X[:, bass.ds(t, 1), :]
                pool.tensor_tensor(row, row, sdb[:].rearrange("p (a n) -> p a n", a=1), ALU.add).then_inc(s_bias, 1)

        @block.scalar
        def _(act):
            act.wait_ge(s_mv, at(T))
            act.activation(std[:], mv[:, :, 1], ACT.Sqrt, bias=eps[:]).then_inc(s_std, 1)
            with act.Fori(0, T // 2) as i:
                for j in range(2):
                    act.wait_ge(s_tr, at(i * 2 + j + 1))
                    act.wait_ge(s_log, at(i * 2))
                    act.wait_ge(s_lo, at(i * 2))
                    act.activation(xt[j][:], tb[j][:].rearrange("p (k s) -> p k s", k=KD), ACT.Copy).then_inc(s_xt, 1)
                    act.wait_ge(s_xt, at(i * 2 + j + 1))
                    act.wait_ge(s_std, at(1))
                    act.activation(xT.hi[:, :, bass.ds(i * 2 * P + j * P, P)], xt[j][:], ACT.Copy).then_inc(s_hi, 1)
            act.wait_ge(s_sub, at(1))
            act.activation(ex[:], logits[:], ACT.Exp).then_inc(s_exp, 1)

        @block.vector
        def _(dve):
            layernorm_stats(dve, (s_stats, s_mv), X, stats, mv, T)
            dve.wait_ge(s_std, at(1))
            dve.reciprocal(rstd[:], std[:]).then_inc(s_rstd, 1)
            dve.wait_ge(s_rstd, at(1))

            def norm(t, j, first=False):
                col = bass.ds(t, 1)
                if not first:
                    dve.wait_ge(s_tr, at(t - 1))
                dve.tensor_scalar(xn[j][:].rearrange("p (a n) -> p a n", a=1), X[:, col, :], mv[:, col, 0], rstd[:, col],
                                  ALU.subtract, ALU.mult).then_inc(s_xn, 1)

            def rest(t, j):
                dve.wait_ge(s_hi, at(t + 1))
                cols = bass.ds(t * P, P)
                dve.tensor_tensor(xT.lo[:, :, cols], xt[j][:], f32(xT.hi[:, :, cols]), ALU.subtract).then_inc(s_lo, 1)
                dve.wait_ge(s_log, at(t + 1))
                dve.tensor_copy(logits[:, bass.ds(t, 1), :], lb[j][:, 0:E].rearrange("p (a n) -> p a n", a=1))\
                   .then_inc(s_logc, 1)

            norm(0, 0, True)
            norm(1, 1, True)
            with dve.Fori(0, T // 2 - 1) as i:
                for j in range(2):
                    norm(i * 2 + 2 + j, j)
                    rest(i * 2 + j, j)
            for j in range(2):
                rest(T - 2 + j, j)
            dve.wait_ge(s_logc, at(T))
            dve.tensor_reduce(nmax[:], logits[:], AX.X, ALU.max).then_inc(s_nmax, 1)
            dve.wait_ge(s_nmax, at(1))
            dve.tensor_tensor(logits[:], logits[:], nmax[:].unsqueeze(2).broadcast_to([P, T, E]),
                              ALU.subtract).then_inc(s_sub, 1)
            dve.wait_ge(s_exp, at(1))
            for t in range(T):
                dve.max(top[:, t, :], ex[:, t, :]).then_inc(s_top, 1)
            for t in range(T):
                dve.wait_ge(s_top, at(t + 1))
                dve.max_index(topi[:, t, :], top[:, t, :], ex[:, t, :]).then_inc(s_at, 1)
            dve.wait_ge(s_at, at(T))
            dve.tensor_copy(atf[:], topi[:]).then_inc(s_atf, 1)
            dve.tensor_tensor(tsum[:], top[:, :, 0], top[:, :, 1], ALU.add).then_inc(s_sum, 1)
            dve.wait_ge(s_sum, at(1))
            dve.reciprocal(rsum[:], tsum[:]).then_inc(s_rsum, 1)
            dve.wait_ge(s_atf, at(1))
            dve.wait_ge(s_const, at(2))
            for n in range(TOP):
                dve.tensor_tensor(hot[:, :, n, :], expert[:].unsqueeze(1).broadcast_to([P, T, E]),
                                  atf[:, :, n:n + 1].broadcast_to([P, T, E]), ALU.is_equal).then_inc(s_hot, 1)
            dve.wait_ge(s_hot, at(2))
            dve.tensor_tensor(hot[:, :, 0, :], hot[:, :, 0, :], hot[:, :, 1, :], ALU.add).then_inc(s_hot, 1)
            dve.wait_ge(s_hot, at(3))
            dve.tensor_tensor(hot[:, :, 0, :], hot[:, :, 0, :], ex[:], ALU.mult).then_inc(s_hot, 1)
            dve.wait_ge(s_hot, at(4))
            dve.wait_ge(s_rsum, at(1))
            dve.tensor_tensor(combine[:, :, 0:E], hot[:, :, 0, :], rsum[:].unsqueeze(2).broadcast_to([P, T, E]),
                              ALU.mult).then_inc(s_comb, 1)

        @block.tensor
        def _(pe):
            pe.wait_ge(s_ld, at(32))
            with pe.Fori(0, T // 2) as i:
                for j in range(2):
                    t = i * 2 + j
                    pe.wait_ge(s_xn, at(t + 1))
                    pe.wait_ge(s_hi, at(i * 2))
                    for c in range(KD):
                        last = pe.transpose(tb[j][:, c * P:(c + 1) * P], xn[j][:, c * P:(c + 1) * P], ident[:])
                    last.then_inc(s_tr, 1)
                for j in range(2):
                    t = i * 2 + j
                    pe.wait_ge(s_xt, at(t + 1))
                    pe.wait_ge(s_logc, at(i * 2))
                    for c in range(KD):
                        last = pe.matmul(lb[j][:, 0:E], xt[j][:, c, :], rw[:, c, :], start=c == 0, stop=c == KD - 1)
                    last.then_inc(s_log, 1)


def experts(nc, banks, X, xT, combine, gw_dram, uw_dram, dw_dram, gb_dram, ub_dram, T, E, I):
    C = 512
    NC = T * P // C
    CT = C // P
    MT = [(m, min(P, I - m)) for m in range(0, I, P)]
    M = len(MT)
    with Phase(nc) as ctx:
        def sb(name, shape, dt=F32):
            return ctx.enter_context(nc.sbuf_tensor("e_" + name, shape, dt))

        def sem(name):
            return ctx.semaphore("e_" + name)

        wg, wu = ([Pair(ctx, nc, f"e_{n}{j}", [P, KD, I]) for j in range(2)] for n in ("wg", "wu"))
        wd = [Pair(ctx, nc, f"e_wd{j}", [P, M, D]) for j in range(2)]
        graw, uraw, draw = sb("graw", [P, KD, I]), sb("uraw", [P, KD, I]), sb("draw", [P, M, D])
        gbias, ubias = sb("gbias", [P, E, M]), sb("ubias", [P, E, M])
        gbe, ube = ([sb(f"{n}{j}", [P, M]) for j in range(2)] for n in ("gbe", "ube"))
        ce = sb("ce", [P, 2, T])
        sg = [sb(f"sg{j}", [P, C]) for j in range(2)]
        hf = [sb(f"hf{j}", [P, C]) for j in range(2)]
        h = Pair(ctx, nc, "e_h", [P, M, C])
        gb, ub, yb = banks[0:2], banks[2:4], banks[4:8]
        s_small, s_raw, s_whi, s_wlo, s_be, s_ce = (sem(n) for n in (
            "biases_loaded", "w_loaded", "w_hi", "w_lo", "expert_bias", "expert_combine"))
        s_g, s_sg, s_u, s_h, s_hi, s_lo, s_y, s_add = (sem(n) for n in (
            "gate", "silu", "up", "h", "h_hi", "h_lo", "down", "added"))
        W = 2 * NC
        ctx.start()
        block = ctx.enter_context(nc.Block())

        LAST = MT[-1]
        full = I // P

        @block.sync
        def _(sp):
            sp.dma_start(gbias[:], gb_dram).then_inc(s_small, 16)
            sp.dma_start(ubias[:], ub_dram).then_inc(s_small, 16)
            with sp.Fori(0, E) as e:
                sp.wait_ge(s_wlo, at(e * 3))
                sp.wait_ge(s_small, at(32))
                one = bass.ds(e, 1)
                src = lambda w: w[one].rearrange("a (k p) n -> p (a k) n", p=P)
                sp.dma_start(graw[:], src(gw_dram)).then_inc(s_raw, 16)
                sp.dma_start(uraw[:], src(uw_dram)).then_inc(s_raw, 16)
                sp.dma_start(draw[:, 0:full, :], dw_dram[one, 0:full * P, :].rearrange("a (k p) n -> p (a k) n", p=P))\
                  .then_inc(s_raw, 16)
                sp.dma_start(draw[0:LAST[1], full:M, :], dw_dram[one, LAST[0]:I, :].rearrange("a p n -> p a n"))\
                  .then_inc(s_raw, 16)

        @block.gpsimd
        def _(pool):
            with pool.Fori(0, E // 2) as i:
                for j in range(2):
                    e = i * 2 + j
                    for n, (w, raw) in enumerate(((wg, graw), (wu, uraw), (wd, draw))):
                        pool.wait_ge(s_whi, at(e * 3 + n + 1))
                        if n < 2:
                            ins = pool.tensor_tensor(w[j].lo[:], raw[:], f32(w[j].hi[:]), ALU.subtract)
                        else:
                            pool.tensor_tensor(w[j].lo[:, 0:full, :], raw[:, 0:full, :], f32(w[j].hi[:, 0:full, :]),
                                               ALU.subtract)
                            r = (slice(0, LAST[1]), full)
                            ins = pool.tensor_tensor(w[j].lo[r], raw[r], f32(w[j].hi[r]), ALU.subtract)
                        ins.then_inc(s_wlo, 1)

        @block.scalar
        def _(act):
            def split(e, j, first=False):
                act.wait_ge(s_raw, at(e * 64 + 64))
                if not first:
                    act.wait_ge(s_add, at((e - 1) * NC * CT))
                act.activation(wg[j].hi[:], graw[:], ACT.Copy).then_inc(s_whi, 1)
                act.activation(wu[j].hi[:], uraw[:], ACT.Copy).then_inc(s_whi, 1)
                act.activation(wd[j].hi[:, 0:full, :], draw[:, 0:full, :], ACT.Copy)
                r = (slice(0, LAST[1]), full)
                act.activation(wd[j].hi[r], draw[r], ACT.Copy).then_inc(s_whi, 1)
                for dst, b in ((gbe, gbias), (ube, ubias)):
                    act.activation(dst[j][:].rearrange("p (a m) -> p a m", a=1), b[:, bass.ds(e, 1), :],
                                   ACT.Copy).then_inc(s_be, 1)
                act.activation(ce[:, j, :].unsqueeze(2), combine[:, :, bass.ds(e, 1)], ACT.Copy).then_inc(s_ce, 1)

            def unit(w, e, j):
                for m in range(M):
                    n, q = w * M + m, (m + w_par[0]) % 2
                    act.wait_ge(s_g, at(n + 1))
                    act.wait_ge(s_h, at(w * M + max(m - 1, 0)))
                    r = slice(0, MT[m][1])
                    act.activation(sg[q][r, :], gb[q][r, :], ACT.Silu, bias=gbe[j][r, m:m + 1]).then_inc(s_sg, 1)
                    act.wait_ge(s_h, at(n + 1))
                    if m == 0:
                        act.wait_ge(s_y, at(w * CT))
                    act.activation(h.hi[r, m, :], hf[q][r, :], ACT.Copy).then_inc(s_hi, 1)
                w_par[0] += M

            w_par = [0]
            act.wait_ge(s_small, at(32))
            split(0, 0, True)

            def turn(i, more):
                for j in range(2):
                    for c in range(NC):
                        act.wait_ge(s_be, at(i * 4 + 2 * (j + 1)))
                        unit(i * W + j * NC + c, None, j)
                        if c == 0 and (j == 0 or more):
                            split(i * 2 + j + 1, 1 - j)

            with act.Fori(0, E // 2 - 1) as i:
                turn(i, True)
            turn(E // 2 - 1, False)

        @block.vector
        def _(dve):
            par = [0]

            def add(w, c, j):
                for t in range(CT):
                    dve.wait_ge(s_y, at(w * CT + t + 1))
                    row = X[:, c * CT + t, :]
                    dve.scalar_tensor_tensor(row, yb[t][:], ce[:, j, c * CT + t:c * CT + t + 1], row, ALU.mult,
                                             ALU.add).then_inc(s_add, 1)

            def unit(w, c, j, first=False):
                for m in range(M):
                    n, q = w * M + m, (m + par[0]) % 2
                    r = slice(0, MT[m][1])
                    dve.wait_ge(s_sg, at(n + 1))
                    dve.wait_ge(s_u, at(n + 1))
                    dve.wait_ge(s_lo, at(w * M + max(m - 1, 0)))
                    dve.scalar_tensor_tensor(hf[q][r, :], ub[q][r, :], ube[j][r, m:m + 1], sg[q][r, :], ALU.add,
                                             ALU.mult).then_inc(s_h, 1)
                    dve.wait_ge(s_hi, at(n + 1))
                    dve.tensor_tensor(h.lo[r, m, :], hf[q][r, :], f32(h.hi[r, m, :]), ALU.subtract).then_inc(s_lo, 1)
                par[0] += M
                add(w, c, j)

            with dve.Fori(0, E // 2) as i:
                for j in range(2):
                    dve.wait_ge(s_be, at(i * 4 + 2 * (j + 1)))
                    dve.wait_ge(s_ce, at(i * 2 + j + 1))
                    for c in range(NC):
                        unit(i * W + j * NC + c, c, j)

        @block.tensor
        def _(pe):
            par = [0]

            def unit(w, c, j):
                cols = slice(c * C, (c + 1) * C)
                for m, (m0, mn) in enumerate(MT):
                    q = (m + par[0]) % 2
                    for weights, dst, s_free, s_done in ((wg, gb, s_sg, s_g), (wu, ub, s_h, s_u)):
                        pe.wait_ge(s_free, at(w * M + max(m - 1, 0)))
                        for k in range(KD):
                            last = matmul3(pe, dst[q][0:mn, :], part(weights[j], slice(None), k, slice(m0, m0 + mn)),
                                           part(xT, slice(None), k, cols), k == 0, k == KD - 1)
                        last.then_inc(s_done, 1)
                par[0] += M
                for ms in (range(M - 1), range(M - 1, M)):
                    for t in range(CT):
                        pe.wait_ge(s_lo, at(w * M + max(ms) + 1))
                        pe.wait_ge(s_add, at(w * CT))
                        for m in ms:
                            r = slice(0, MT[m][1])
                            last = matmul3(pe, yb[t][:], part(h, r, m, slice(t * P, (t + 1) * P)),
                                           part(wd[j], r, m), m == 0, m == M - 1)
                        if M - 1 in ms:
                            last.then_inc(s_y, 1)

            with pe.Fori(0, E // 2) as i:
                for j in range(2):
                    pe.wait_ge(s_wlo, at(i * 6 + 3 * (j + 1)))
                    for c in range(NC):
                        unit(i * W + j * NC + c, c, j)


def program(nc, a, out, stop=4, start=0):
    B, S, _ = a["x"].shape
    T = B * S // P
    with ExitStack() as ctx:
        X = ctx.enter_context(nc.sbuf_tensor("X", [P, T, D], F32))
        eps = ctx.enter_context(nc.sbuf_tensor("eps", [P, 1], F32))
        ident = ctx.enter_context(nc.sbuf_tensor("ident", [P, P], F32))
        eps_rms = ctx.enter_context(nc.sbuf_tensor("eps_rms", [P, 1], F32))
        ones = ctx.enter_context(nc.sbuf_tensor("ones", [P, P], F32))
        banks = [ctx.enter_context(nc.psum_tensor(f"bank{j}", [P, 512], F32)) for j in range(8)]
        s_const = ctx.enter_context(nc.semaphore("constants"))
        s_out = ctx.enter_context(nc.semaphore("stored"))
        with nc.Block() as block:
            @block.gpsimd
            def _(pool):
                pool.memset(eps[:], LN_EPS).then_inc(s_const, 1)
                pool.memset(ident[:], 0.0).then_inc(s_const, 1)
                pool.memset(ones[:], 1.0).then_inc(s_const, 1)
                pool.memset(eps_rms[:], 1e-6).then_inc(s_const, 1)
                pool.wait_ge(s_const, 2)
                pool.affine_select(out=ident[:], in_=ident[:], compare_op=ALU.not_equal, fill=1.0, base=0,
                                   pattern=[[-1, P]], channel_multiplier=1).then_inc(s_const, 1)
        tok = lambda ap: ap.rearrange("b s d -> (b s) d").rearrange("(t p) d -> p t d", p=P)
        ktile = lambda ap: ap.rearrange("(k p) n -> p k n", p=P)
        if start:
            with nc.Block() as block:
                @block.sync
                def _(sp):
                    sp.dma_start(X[:], tok(a["x"])).then_inc(s_const, 16)
                    sp.wait_ge(s_const, 21)
        if start < 1:
          attention0(nc, banks, X, eps, ident, tok(a["x"]), tok(a["ctx"]), ktile(a["ctxT"]),
                   [ktile(a[n]) for n in ("wqT", "wkT", "wvT", "woT")], B, S)
        if start < 2 and stop >= 2:
            ffn0(nc, banks, X, eps, ident, ones, [ktile(a[n]) for n in ("gwT", "vwT", "owT")], [a[n] for n in ("gb", "vb", "ob")], T)
        if start < 3 and stop >= 3:
            G = 4
            k_dram = [nc.dram_tensor(f"K_{n}", (P, G, B * S), F32, kind="Internal").ap() for n in ("hi", "lo")]
            v_dram = [nc.dram_tensor(f"V_{n}", (P, T, D), F32, kind="Internal").ap() for n in ("hi", "lo")]
            with ExitStack() as cx:
                xT = Pair(cx, nc, "x1T", [P, KD, B * S])
                keys_values1(nc, banks, X, eps, eps_rms, ident, ones, xT, ktile(a["ctxT"]), ktile(a["Wk"]), ktile(a["Wv"]),
                             a["bkT"], a["bv"], a["qn"], a["kn"], k_dram, v_dram, B, S, G)
                attention1(nc, banks, X, ident, ones, xT, a["mask"].rearrange("(t p) s -> p t s", p=P), ktile(a["Wq"]),
                           ktile(a["Wo"]), a["bqT"], k_dram, v_dram, B, S, G)
        if stop >= 4:
            E = a["rwT"].shape[1]
            EA, _, I = a["egw"].shape
            with ExitStack() as cx:
                xT = Pair(cx, nc, "x2T", [P, KD, B * S])
                combine = cx.enter_context(nc.sbuf_tensor("combine", [P, T, EA], F32))
                router(nc, banks, X, eps, ident, xT, combine, ktile(a["rwT"]), a["sdb"], T, E)
                experts(nc, banks, X, xT, combine, a["egw"], a["euw"], a["edw"], a["egb"], a["eub"], T, EA, I)
        with nc.Block() as block:
            @block.sync
            def _(sp):
                sp.dma_start(tok(out), X[:]).then_inc(s_out, 16)
                sp.wait_ge(s_out, 16)


def _layout(inputs):
    import numpy as np
    g = lambda n: np.asarray(inputs[n])
    t = lambda n: np.ascontiguousarray(g(n).T)
    E, _, I = g("L1_ffn_gate_w").shape

    def experts_in(n):
        shared = g(f"L1_ffn_s_{n}_w").reshape(512, 2, I).transpose(1, 0, 2)
        return np.concatenate([g(f"L1_ffn_{n}_w"), shared])

    def bias(n):
        b = np.zeros((E + 2, -(-I // 128) * 128), np.float32)
        b[E:, :I] = g(f"L1_ffn_s_{n}_b").reshape(2, I)
        return b.reshape(E + 2, -1, 128).transpose(2, 0, 1)

    return {
        "x": g("x"), "ctx": g("ctx_2048"),
        "ctxT": np.ascontiguousarray(g("ctx_2048").reshape(-1, 512).T),
        "rwT": t("L1_ffn_router_w"), "sdb": g("L1_ffn_s_down_b"),
        "egw": experts_in("gate"), "euw": experts_in("up"),
        "edw": np.concatenate([g("L1_ffn_down_w"), g("L1_ffn_s_down_w").reshape(2, I, 512)]),
        "egb": bias("gate"), "eub": bias("up"),
        "Wq": g("L1_xattn_Wq"), "Wk": g("L1_xattn_Wk"), "Wv": g("L1_xattn_Wv"), "Wo": g("L1_xattn_Wo"),
        "bqT": g("L1_xattn_bq").reshape(-1, 128).T, "bkT": g("L1_xattn_bk").reshape(-1, 128).T, "bv": g("L1_xattn_bv"),
        "qn": g("L1_xattn_qn_w").reshape(128, 1), "kn": g("L1_xattn_kn_w").reshape(128, 1),
        "mask": g("mask_1xSxS2_ff0")[0],
        "gwT": t("L0_ffn_gate_w"), "vwT": t("L0_ffn_val_w"), "owT": t("L0_ffn_out_w"),
        "gb": g("L0_ffn_gate_b"), "vb": g("L0_ffn_val_b"), "ob": g("L0_ffn_out_b"),
        "wqT": t("L0_xattn_wq"), "wkT": t("L0_xattn_wk"), "wvT": t("L0_xattn_wv"), "woT": t("L0_xattn_wo"),
    }


def kernel(**inputs):
    import numpy as np
    import concourse.bacc as bacc
    from concourse.bass_utils import run_bass_kernel_spmd

    nc = bacc.Bacc("TRN2", target_bir_lowering=False, num_devices=1)
    arrays, args = {}, {}
    for name, a in _layout(inputs).items():
        a = np.ascontiguousarray(a)
        arrays["in_" + name] = a
        args[name] = nc.dram_tensor("in_" + name, a.shape, mybir.dt.from_np(a.dtype), kind="ExternalInput").ap()
    out = nc.dram_tensor("out", (8, 256, 512), F32, kind="ExternalOutput").ap()
    program(nc, args, out)
    r = run_bass_kernel_spmd(nc, [arrays], core_ids=[0])
    return r.results[0]["out"]
```

```python
from contextlib import ExitStack

import concourse.bass as bass
from concourse import mybir

ALU = mybir.AluOpType
ACT = mybir.ActivationFunctionType
AX = mybir.AxisListType
F32 = mybir.dt.float32
F32R = mybir.dt.float32r
BF16 = mybir.dt.bfloat16
U32 = mybir.dt.uint32

P = 128
D = 512
KD = D // P
ROUND = 12582912.0
LN_EPS = 1e-5


def at(count):
    return count + 1


class Phase(ExitStack):

    def __init__(self, nc):
        super().__init__()
        self.nc, self.semaphores, self.from_zero = nc, [], []

    def semaphore(self, name):
        self.semaphores.append(self.nc.alloc_semaphore(name=name))
        return self.semaphores[-1]

    def queue_semaphore(self, name):
        self.from_zero.append(self.nc.alloc_semaphore(name=name))
        return self.from_zero[-1]

    def start(self):
        for s in self.semaphores:
            self.nc.gpsimd.sem_inc(s, 1)
        self.nc.all_engine_barrier()

    def __exit__(self, *exc):
        super().__exit__(*exc)
        self.nc.clear_and_free_semaphores(self.semaphores + self.from_zero)


class Pair:

    def __init__(self, ctx, nc, name, shape):
        self.hi = ctx.enter_context(nc.sbuf_tensor(name + "_hi", shape, F32R))
        self.lo = ctx.enter_context(nc.sbuf_tensor(name + "_lo", shape, F32R))


def f32(ap):
    return ap.bitcast(F32)


def matmul3(pe, out, w, x, first, last):
    pe.matmul(out, w[1], x[0], start=first, stop=False)
    pe.matmul(out, w[0], x[1], start=False, stop=False)
    return pe.matmul(out, w[0], x[0], start=False, stop=last)


def part(pair, *index):
    return pair.hi[index], pair.lo[index]


class Flow:

    def __init__(self, ctx, nc, name):
        self.mm = ctx.semaphore(name + "_product")
        self.hi = ctx.semaphore(name + "_hi_written")
        self.lo = ctx.semaphore(name + "_lo_written")


def layernorm_stats(dve, ctx_sems, X, stats, mv, tiles):
    s_stats, s_mv = ctx_sems
    for t in range(tiles):
        dve.bn_stats(stats[:, t, :], X[:, t, :]).then_inc(s_stats, 1)
    for t in range(tiles):
        dve.wait_ge(s_stats, at(t + 1))
        dve.bn_aggr(mv[:, t, :], stats[:, t, :]).then_inc(s_mv, 1)


def attention0(nc, banks, X, eps, ident, x_dram, ctx_dram, ctxT_dram, w_dram, B, S):
    T = B * S // P
    QT = S // P
    KT = 2 * QT
    SCALE = float(D) ** -0.5
    with Phase(nc) as ctx:
        def sb(name, shape, dt=F32):
            return ctx.enter_context(nc.sbuf_tensor("a0_" + name, shape, dt))

        def sem(name):
            return ctx.semaphore("a0_" + name)

        def pair(name, shape):
            return Pair(ctx, nc, "a0_" + name, shape)

        def flow(name):
            return Flow(ctx, nc, "a0_" + name)

        W = [pair(n, [P, KD, D]) for n in ("wq", "wk", "wv", "wo")]
        wq, wk, wv, wo = W
        wraw = [sb(f"wraw{j}", [P, KD, D]) for j in range(2)]
        stats = sb("stats", [P, T, 6])
        mv = sb("mv", [P, T, 2])
        std = sb("std", [P, T])
        rstd = sb("rstd", [P, T])
        xn = sb("xn", [P, QT, D])
        xT = pair("xT", [P, KD, S])
        qT = pair("qT", [P, KD, S])
        kT = pair("kT", [P, KD, 2 * S])
        V = pair("V", [P, KT, D])
        cTraw = sb("cTraw", [P, KD, S])
        craw = sb("craw", [P, QT, D])
        probs = sb("probs", [P, QT, 2 * S])
        pT = pair("pT", [P, KT, S])
        oT = pair("oT", [P, KD, S])
        nmax = sb("nmax", [P, QT])
        den = sb("den", [P, QT])
        rden = sb("rden", [P, QT])
        bank = banks

        s_x = sem("x_loaded")
        s_w = [sem(f"w{j}_loaded") for j in range(4)]
        s_whi = sem("w_hi_written")
        s_wlo = sem("w_lo_written")
        s_stats, s_mv, s_std, s_rstd = sem("stats"), sem("mean_var"), sem("std"), sem("rstd")
        s_cT, s_c = sem("ctxT_loaded"), sem("ctx_loaded")
        s_cThi, s_cTlo = sem("ctxT_hi"), sem("ctxT_lo")
        s_chi, s_clo = sem("ctx_hi"), sem("ctx_lo")
        s_xn = sem("xn")
        tr, q, k, v, o, pt = (flow(n) for n in ("xT", "q", "k", "v", "o", "pT"))
        s_scores, s_nmax, s_exp, s_rden = sem("scores"), sem("nmax"), sem("exp"), sem("rden")
        s_proj, s_added = sem("projected"), sem("added")

        ctx.start()
        block = ctx.enter_context(nc.Block())

        @block.sync
        def _(sp):
            for j in (0, 1):
                sp.dma_start(wraw[j][:], w_dram[j]).then_inc(s_w[j], 16)
            sp.dma_start(X[:], x_dram).then_inc(s_x, 16)
            for j in (2, 3):
                sp.wait_ge(s_wlo, at(j - 1))
                sp.dma_start(wraw[j - 2][:], w_dram[j]).then_inc(s_w[j], 16)
            with sp.Fori(0, B) as i:
                sp.wait_ge(s_cTlo, at(i))
                sp.dma_start(cTraw[:], ctxT_dram[:, :, bass.ds(i * S, S)]).then_inc(s_cT, 16)
                sp.wait_ge(s_clo, at(i))
                sp.dma_start(craw[:], ctx_dram[:, bass.ds(i * QT, QT), :]).then_inc(s_c, 16)

        @block.gpsimd
        def _(pool):
            with pool.Fori(0, B) as i:
                pool.wait_ge(s_cThi, at(i + 1))
                pool.tensor_tensor(kT.lo[:, :, 0:S], cTraw[:], f32(kT.hi[:, :, 0:S]), ALU.subtract).then_inc(s_cTlo, 1)
                pool.wait_ge(s_chi, at(i + 1))
                pool.tensor_tensor(V.lo[:, 0:QT, :], craw[:], f32(V.hi[:, 0:QT, :]), ALU.subtract).then_inc(s_clo, 1)

        @block.scalar
        def _(act):
            for j in range(4):
                act.wait_ge(s_w[j], at(16))
                act.activation(W[j].hi[:], wraw[j % 2][:], ACT.Copy).then_inc(s_whi, 1)
                if j == 0:
                    act.wait_ge(s_mv, at(T))
                    act.activation(std[:], mv[:, :, 1], ACT.Sqrt, bias=eps[:]).then_inc(s_std, 1)
            with act.Fori(0, B) as i:
                act.wait_ge(s_cT, at(i * 16 + 16))
                act.activation(kT.hi[:, :, 0:S], cTraw[:], ACT.Copy).then_inc(s_cThi, 1)
                act.wait_ge(s_c, at(i * 16 + 16))
                act.activation(V.hi[:, 0:QT, :], craw[:], ACT.Copy).then_inc(s_chi, 1)
                for t in range(QT):
                    act.wait_ge(tr.mm, at(i * QT + t + 1))
                    act.activation(xT.hi[:, :, t * P:(t + 1) * P],
                                   bank[t][:].rearrange("p (k s) -> p k s", k=KD), ACT.Copy).then_inc(tr.hi, 1)
                for n, (f, dst, b0, scale) in enumerate(((q, qT.hi, 2, SCALE), (k, kT.hi, 4, 1.0))):
                    for m in range(2):
                        act.wait_ge(f.mm, at(i * 2 + m + 1))
                        dd = dst[:, 2 * m:2 * m + 2, 0:S] if n == 0 else dst[:, 2 * m:2 * m + 2, S:2 * S]
                        act.activation(dd, bank[b0 + m][:].rearrange("p (k s) -> p k s", k=2), ACT.Copy,
                                       scale=scale).then_inc(f.hi, 1)
                for t in range(QT):
                    act.wait_ge(v.mm, at(i * QT + t + 1))
                    act.activation(V.hi[:, QT + t, :], bank[6 + t][:], ACT.Copy).then_inc(v.hi, 1)
                for t in range(QT):
                    act.wait_ge(s_nmax, at(i * QT + t + 1))
                    act.activation(probs[:, t, :], bank[t][:], ACT.Exp, bias=nmax[:, t:t + 1],
                                   accum_out=den[:, t:t + 1]).then_inc(s_exp, 1)
                for t in range(QT):
                    act.wait_ge(pt.mm, at(i * QT + t + 1))
                    act.activation(pT.hi[:, :, t * P:(t + 1) * P],
                                   bank[2 + t][:].rearrange("p (k s) -> p k s", k=KT), ACT.Copy).then_inc(pt.hi, 1)
                for m in range(2):
                    act.wait_ge(o.mm, at(i * 2 + m + 1))
                    if m == 0:
                        act.wait_ge(s_proj, at(i * QT))
                    act.activation(oT.hi[:, 2 * m:2 * m + 2, :],
                                   bank[4 + m][:].rearrange("p (k s) -> p k s", k=2), ACT.Copy).then_inc(o.hi, 1)

        @block.vector
        def _(dve):
            dve.wait_ge(s_x, at(16))
            layernorm_stats(dve, (s_stats, s_mv), X, stats, mv, T)
            dve.wait_ge(s_std, at(1))
            dve.reciprocal(rstd[:], std[:]).then_inc(s_rstd, 1)
            for j in range(4):
                dve.wait_ge(s_whi, at(j + 1))
                dve.tensor_tensor(W[j].lo[:], wraw[j % 2][:], f32(W[j].hi[:]), ALU.subtract).then_inc(s_wlo, 1)
            dve.wait_ge(s_rstd, at(1))
            with dve.Fori(0, B) as i:
                for t in range(QT):
                    dve.tensor_scalar(xn[:, t, :], X[:, bass.ds(i * QT + t, 1), :], mv[:, bass.ds(i * QT + t, 1), 0],
                                      rstd[:, bass.ds(i * QT + t, 1)], ALU.subtract, ALU.mult).then_inc(s_xn, 1)
                for t in range(QT):
                    dve.wait_ge(tr.hi, at(i * QT + t + 1))
                    dst = slice(t * P, (t + 1) * P)
                    dve.tensor_tensor(xT.lo[:, :, dst], bank[t][:].rearrange("p (k s) -> p k s", k=KD),
                                      f32(xT.hi[:, :, dst]), ALU.subtract).then_inc(tr.lo, 1)
                for n, (f, dst, b0, scale) in enumerate(((q, qT, 2, SCALE), (k, kT, 4, 1.0))):
                    for m in range(2):
                        dve.wait_ge(f.hi, at(i * 2 + m + 1))
                        cols = slice(0, S) if n == 0 else slice(S, 2 * S)
                        dve.scalar_tensor_tensor(dst.lo[:, 2 * m:2 * m + 2, cols],
                                                 bank[b0 + m][:].rearrange("p (k s) -> p k s", k=2), scale,
                                                 f32(dst.hi[:, 2 * m:2 * m + 2, cols]), ALU.mult,
                                                 ALU.subtract).then_inc(f.lo, 1)
                for t in range(QT):
                    dve.wait_ge(v.hi, at(i * QT + t + 1))
                    dve.tensor_tensor(V.lo[:, QT + t, :], bank[6 + t][:], f32(V.hi[:, QT + t, :]),
                                      ALU.subtract).then_inc(v.lo, 1)
                for t in range(QT):
                    dve.wait_ge(s_scores, at(i * QT + t + 1))
                    dve.tensor_reduce(nmax[:, t:t + 1], bank[t][:], AX.X, ALU.max, negate=True).then_inc(s_nmax, 1)
                for t in range(QT):
                    dve.wait_ge(s_exp, at(i * QT + t + 1))
                    dve.reciprocal(rden[:, t:t + 1], den[:, t:t + 1]).then_inc(s_rden, 1)
                for t in range(QT):
                    dve.wait_ge(pt.hi, at(i * QT + t + 1))
                    dst = slice(t * P, (t + 1) * P)
                    dve.tensor_tensor(pT.lo[:, :, dst], bank[2 + t][:].rearrange("p (k s) -> p k s", k=KT),
                                      f32(pT.hi[:, :, dst]), ALU.subtract).then_inc(pt.lo, 1)
                for m in range(2):
                    dve.wait_ge(o.hi, at(i * 2 + m + 1))
                    dve.tensor_tensor(oT.lo[:, 2 * m:2 * m + 2, :],
                                      bank[4 + m][:].rearrange("p (k s) -> p k s", k=2),
                                      f32(oT.hi[:, 2 * m:2 * m + 2, :]), ALU.subtract).then_inc(o.lo, 1)
                for t in range(QT):
                    dve.wait_ge(s_proj, at(i * QT + t + 1))
                    dve.wait_ge(s_rden, at(i * QT + t + 1))
                    row = X[:, bass.ds(i * QT + t, 1), :]
                    dve.scalar_tensor_tensor(row, bank[6 + t][:].rearrange("p (a n) -> p a n", a=1),
                                             rden[:, t:t + 1], row, ALU.mult, ALU.add).then_inc(s_added, 1)

        @block.tensor
        def _(pe):
            with pe.Fori(0, B) as i:
                for t in range(QT):
                    pe.wait_ge(s_xn, at(i * QT + t + 1))
                    for c in range(KD):
                        last = pe.transpose(bank[t][:, c * P:(c + 1) * P], xn[:, t, c * P:(c + 1) * P], ident[:])
                    last.then_inc(tr.mm, 1)
                pe.wait_ge(tr.lo, at(i * QT + QT))
                for n, (f, w, b0) in enumerate(((q, wq, 2), (k, wk, 4))):
                    pe.wait_ge(s_wlo, at(n + 1))
                    for m in range(2):
                        for h in range(2):
                            e = 2 * m + h
                            for c in range(KD):
                                last = matmul3(pe, bank[b0 + m][:, h * S:(h + 1) * S],
                                               part(w, slice(None), c, slice(e * P, (e + 1) * P)),
                                               part(xT, slice(None), c), c == 0, c == KD - 1)
                        last.then_inc(f.mm, 1)
                pe.wait_ge(s_wlo, at(3))
                pe.wait_ge(s_added, at(i * QT))
                for t in range(QT):
                    for c in range(KD):
                        last = matmul3(pe, bank[6 + t][:], part(xT, slice(None), c, slice(t * P, (t + 1) * P)),
                                       part(wv, slice(None), c), c == 0, c == KD - 1)
                    last.then_inc(v.mm, 1)
                pe.wait_ge(q.lo, at(i * 2 + 2))
                pe.wait_ge(k.lo, at(i * 2 + 2))
                pe.wait_ge(s_cTlo, at(i + 1))
                for t in range(QT):
                    for c in range(KD):
                        last = matmul3(pe, bank[t][:], part(qT, slice(None), c, slice(t * P, (t + 1) * P)),
                                       part(kT, slice(None), c), c == 0, c == KD - 1)
                    last.then_inc(s_scores, 1)
                for t in range(QT):
                    pe.wait_ge(s_exp, at(i * QT + t + 1))
                    for c in range(KT):
                        last = pe.transpose(bank[2 + t][:, c * P:(c + 1) * P], probs[:, t, c * P:(c + 1) * P],
                                            ident[:])
                    last.then_inc(pt.mm, 1)
                pe.wait_ge(pt.lo, at(i * QT + QT))
                pe.wait_ge(v.lo, at(i * QT + QT))
                pe.wait_ge(s_clo, at(i + 1))
                for m in range(2):
                    for h in range(2):
                        e = 2 * m + h
                        for c in range(KT):
                            last = matmul3(pe, bank[4 + m][:, h * S:(h + 1) * S],
                                           part(V, slice(None), c, slice(e * P, (e + 1) * P)),
                                           part(pT, slice(None), c), c == 0, c == KT - 1)
                    last.then_inc(o.mm, 1)
                pe.wait_ge(o.lo, at(i * 2 + 2))
                pe.wait_ge(s_wlo, at(4))
                for t in range(QT):
                    for c in range(KD):
                        last = matmul3(pe, bank[6 + t][:], part(oT, slice(None), c, slice(t * P, (t + 1) * P)),
                                       part(wo, slice(None), c), c == 0, c == KD - 1)
                    last.then_inc(s_proj, 1)


def bitlinear_weights(nc, banks, eps, ones, w_dram, wq, gamma):
    N = 3
    FR = w_dram[0].shape[1] * w_dram[0].shape[2]
    CH = 4
    C = FR // CH
    with Phase(nc) as ctx:
        def sb(name, shape, dt=F32):
            return ctx.enter_context(nc.sbuf_tensor("bw_" + name, shape, dt))

        def sem(name):
            return ctx.semaphore("bw_" + name)

        raw = [sb(f"raw{j}", [P, FR]) for j in range(N)]
        junk = sb("junk", [P, FR], BF16)
        magic = sb("magic", [P, 1])
        asum = sb("asum", [P, N])
        rgamma = sb("rgamma", [P, N])
        tot = banks[0]
        s_raw = [sem(f"raw{j}_loaded") for j in range(N)]
        s_magic, s_asum, s_tot, s_g, s_rg = (sem(n) for n in ("magic", "abs_sum", "total", "gamma", "rgamma"))
        s_sc, s_min, s_done = sem("scaled"), sem("min"), sem("ternary")
        ctx.start()
        block = ctx.enter_context(nc.Block())

        @block.sync
        def _(sp):
            for j in range(N):
                sp.dma_start(raw[j][:].rearrange("p (k n) -> p k n", k=w_dram[j].shape[1]),
                             w_dram[j]).then_inc(s_raw[j], 16)

        @block.scalar
        def _(act):
            for j in range(N):
                act.wait_ge(s_raw[j], at(16))
                if j:
                    act.wait_ge(s_asum, at(j))
                act.activation(junk[:], raw[j][:], ACT.Abs, accum_out=asum[:, j:j + 1]).then_inc(s_asum, 1)

        @block.tensor
        def _(pe):
            for j in range(N):
                pe.wait_ge(s_asum, at(j + 1))
                pe.wait_ge(s_g, at(j))
                pe.matmul(tot[:, j:j + 1], ones[:], asum[:, j:j + 1], start=True, stop=True).then_inc(s_tot, 1)

        @block.gpsimd
        def _(pool):
            pass

        @block.vector
        def _(dve):
            n = 0
            for j in range(N):
                dve.wait_ge(s_tot, at(j + 1))
                dve.tensor_scalar(gamma[:, j:j + 1], tot[:, j:j + 1], 1.0 / (P * FR), 1e-5, ALU.mult,
                                  ALU.max).then_inc(s_g, 1)
                dve.wait_ge(s_g, at(j + 1))
                dve.reciprocal(rgamma[:, j:j + 1], gamma[:, j:j + 1]).then_inc(s_rg, 1)
                dve.wait_ge(s_rg, at(j + 1))
                w = wq[j][:].rearrange("p k n -> p (k n)")
                dve.tensor_scalar(raw[j][:], raw[j][:], rgamma[:, j:j + 1], ROUND, ALU.mult, ALU.add).then_inc(s_sc, 1)
                dve.wait_ge(s_sc, at(j + 1))
                dve.tensor_scalar(w, raw[j][:], ROUND, 1.0, ALU.subtract, ALU.min).then_inc(s_min, 1)
                dve.wait_ge(s_min, at(j + 1))
                dve.tensor_scalar(w, w, -1.0, None, ALU.max).then_inc(s_done, 1)


def ffn0(nc, banks, X, eps, ident, ones, w_dram, b_dram, T):
    H = w_dram[0].shape[2]
    NH = H // 512
    KH = H // P
    with Phase(nc) as ctx:
        def sb(name, shape, dt=F32):
            return ctx.enter_context(nc.sbuf_tensor("f0_" + name, shape, dt))

        def sem(name):
            return ctx.semaphore("f0_" + name)

        wg, wv = (sb(n, [P, KD, H], BF16) for n in ("wg", "wv"))
        wo = sb("wo", [P, KH, D], BF16)
        gamma = sb("gamma", [P, 3])
        bitlinear_weights(nc, banks, eps, ones, w_dram, (wg, wv, wo), gamma)

        bg, bv = (sb(n, [P, H]) for n in ("bg", "bv"))
        bo = sb("bo", [P, D])
        identb = sb("identb", [P, P], BF16)
        stats = sb("stats", [P, T, 6])
        mv = sb("mv", [P, T, 2])
        std = sb("std", [P, T])
        rstd = sb("rstd", [P, T])
        xn = sb("xn", [P, D])
        xr = sb("xr", [P, D])
        xq = sb("xq", [P, D], BF16)
        xqT = sb("xqT", [P, KD, P], BF16)
        ax = sb("ax", [P, T])
        rx = sb("rx", [P, T])
        sx = sb("sx", [P, T])
        sg = sb("sg", [P, 2, T])
        g = sb("g", [P, 2, 512])
        gs = sb("gs", [P, 2, 512])
        vv = sb("vv", [P, 2, 512])
        h = sb("h", [P, H])
        hr = sb("hr", [P, H])
        hq = sb("hq", [P, H], BF16)
        hqT = sb("hqT", [P, KH, P], BF16)
        ah, rh, sh, so = (sb(n, [P, 1]) for n in ("ah", "rh", "sh", "so"))
        magic = sb("magic", [P, 1])
        gb, vb = banks[0:2], banks[2:4]
        hb = [b[:].bitcast(BF16) for b in banks[4:6]]
        xb, ob = banks[6][:].bitcast(BF16), banks[7]

        s_b = sem("biases_loaded")
        s_id = sem("constants")
        s_stats, s_mv, s_std, s_rstd = sem("stats"), sem("mean_var"), sem("std"), sem("rstd")
        s_xn, s_ax, s_axc, s_rx, s_sx, s_sgv, s_xr, s_xq = (sem(n) for n in (
            "xn", "absmax_x", "absmax_x_clipped", "rx", "sx", "sg", "x_rounded", "xq"))
        s_bo = sem("out_bias_added")
        s_xT, s_xTc = sem("xqT_product"), sem("xqT_copied")
        s_g, s_gb, s_gs, s_v, s_vb, s_h = (sem(n) for n in ("gate", "gate_biased", "silu", "val", "val_biased", "h"))
        s_ah, s_ahc, s_rh, s_sh, s_so, s_hr, s_hq = (sem(n) for n in (
            "absmax_h", "absmax_h_clipped", "rh", "sh", "so", "h_rounded", "hq"))
        s_hT, s_hTc, s_out, s_added = sem("hqT_product"), sem("hqT_copied"), sem("out"), sem("added")

        ctx.start()
        block = ctx.enter_context(nc.Block())

        @block.sync
        def _(sp):
            sp.dma_start(bg[:], b_dram[0].partition_broadcast(P)).then_inc(s_b, 16)
            sp.dma_start(bv[:], b_dram[1].partition_broadcast(P)).then_inc(s_b, 16)
            sp.dma_start(bo[:], b_dram[2].partition_broadcast(P)).then_inc(s_b, 16)

        @block.gpsimd
        def _(pool):
            pool.memset(magic[:], ROUND).then_inc(s_id, 1)
            pool.tensor_copy(identb[:], ident[:]).then_inc(s_id, 1)
            pool.wait_ge(s_b, at(48))

            def out_bias(t):
                pool.wait_ge(s_xn, at(t + 1))
                row = X[:, bass.ds(t, 1), :]
                pool.tensor_tensor(row, row, bo[:].rearrange("p (a n) -> p a n", a=1), ALU.add).then_inc(s_bo, 1)

            def hidden(t):
                for j in range(NH):
                    pool.wait_ge(s_vb, at(t * NH + j + 1))
                    pool.wait_ge(s_gs, at(t * NH + j + 1))
                    if j == 0:
                        pool.wait_ge(s_hr, at(t))
                    pool.tensor_tensor(h[:, j * 512:(j + 1) * 512], vv[:, j % 2, :], gs[:, j % 2, :],
                                       ALU.mult).then_inc(s_h, 1)

            out_bias(0)
            out_bias(1)
            hidden(0)
            with pool.Fori(0, T - 2) as t:
                out_bias(t + 2)
                hidden(t + 1)
            hidden(T - 1)

        @block.scalar
        def _(act):
            act.wait_ge(s_mv, at(T))
            act.activation(std[:], mv[:, :, 1], ACT.Sqrt, bias=eps[:]).then_inc(s_std, 1)
            act.wait_ge(s_id, at(2))

            def xT_copy(t):
                act.wait_ge(s_xT, at(t + 1))
                act.wait_ge(s_v, at(t * NH))
                act.activation(xqT[:], xb[:, 0:D].rearrange("p (k s) -> p k s", k=KD), ACT.Copy).then_inc(s_xTc, 1)

            def silu(t):
                for j in range(NH):
                    act.wait_ge(s_gb, at(t * NH + j + 1))
                    act.wait_ge(s_h, at(t * NH + max(j - 1, 0)))
                    act.activation(gs[:, j % 2, :], g[:, j % 2, :], ACT.Silu).then_inc(s_gs, 1)

            def h_round(t):
                act.wait_ge(s_sh, at(t + 1))
                act.wait_ge(s_hq, at(t))
                act.activation(hr[:], h[:], ACT.Identity, bias=magic[:], scale=sh[:]).then_inc(s_hr, 1)

            def hT_copy(t):
                for j in range(2):
                    act.wait_ge(s_hT, at(t * 2 + j + 1))
                    if j == 0:
                        act.wait_ge(s_out, at(t))
                    act.activation(hqT[:, 8 * j:8 * j + 8, :], hb[j][:].rearrange("p (k s) -> p k s", k=8),
                                   ACT.Copy).then_inc(s_hTc, 1)

            xT_copy(0)
            silu(0)
            xT_copy(1)
            h_round(0)
            with act.Fori(0, T - 2) as t:
                silu(t + 1)
                hT_copy(t)
                xT_copy(t + 2)
                h_round(t + 1)
            silu(T - 1)
            hT_copy(T - 2)
            h_round(T - 1)
            hT_copy(T - 1)

        @block.vector
        def _(dve):
            layernorm_stats(dve, (s_stats, s_mv), X, stats, mv, T)
            dve.wait_ge(s_std, at(1))
            dve.reciprocal(rstd[:], std[:]).then_inc(s_rstd, 1)
            dve.wait_ge(s_rstd, at(1))
            dve.wait_ge(s_b, at(48))

            def quantise_x(t):
                col = bass.ds(t, 1)
                dve.tensor_scalar(xn[:].rearrange("p (a n) -> p a n", a=1), X[:, col, :], mv[:, col, 0], rstd[:, col],
                                  ALU.subtract, ALU.mult).then_inc(s_xn, 1)
                dve.wait_ge(s_xn, at(t + 1))
                dve.tensor_reduce(ax[:, col], xn[:], AX.X, ALU.max, apply_absolute_value=True).then_inc(s_ax, 1)
                dve.wait_ge(s_ax, at(t + 1))
                dve.tensor_scalar(ax[:, col], ax[:, col], 1e-5, None, ALU.max).then_inc(s_axc, 1)
                dve.wait_ge(s_axc, at(t + 1))
                dve.reciprocal(rx[:, col], ax[:, col]).then_inc(s_rx, 1)
                for n in range(2):
                    dve.tensor_scalar(sg[:, n, col], ax[:, col], gamma[:, n:n + 1], 1.0 / 127, ALU.mult,
                                      ALU.mult).then_inc(s_sgv, 1)
                dve.wait_ge(s_rx, at(t + 1))
                dve.tensor_scalar(sx[:, col], rx[:, col], 127.0, None, ALU.mult).then_inc(s_sx, 1)
                dve.wait_ge(s_sx, at(t + 1))
                dve.tensor_scalar(xr[:], xn[:], sx[:, col], ROUND, ALU.mult, ALU.add).then_inc(s_xr, 1)
                dve.wait_ge(s_xr, at(t + 1))
                dve.wait_ge(s_xT, at(t))
                dve.tensor_scalar(xq[:], xr[:], ROUND, 127.0, ALU.subtract, ALU.min).then_inc(s_xq, 1)

            def hidden(t):
                dve.wait_ge(s_sgv, at(2 * t + 2))
                for j in range(NH):
                    cols = slice(j * 512, (j + 1) * 512)
                    for n, (s_in, src, dst, b, s_free, s_done) in enumerate(((s_g, gb, g, bg, s_gs, s_gb),
                                                                             (s_v, vb, vv, bv, s_h, s_vb))):
                        dve.wait_ge(s_in, at(t * NH + j + 1))
                        dve.wait_ge(s_free, at(t * NH + max(j - 1, 0)))
                        dve.scalar_tensor_tensor(dst[:, j % 2, :], src[j % 2][:], sg[:, n, bass.ds(t, 1)], b[:, cols],
                                                 ALU.mult, ALU.add).then_inc(s_done, 1)

            def quantise_h(t):
                dve.wait_ge(s_h, at(t * NH + NH))
                dve.tensor_reduce(ah[:], h[:], AX.X, ALU.max, apply_absolute_value=True).then_inc(s_ah, 1)
                dve.wait_ge(s_ah, at(t + 1))
                dve.tensor_scalar(ah[:], ah[:], 1e-5, None, ALU.max).then_inc(s_ahc, 1)
                dve.wait_ge(s_ahc, at(t + 1))
                dve.reciprocal(rh[:], ah[:]).then_inc(s_rh, 1)
                dve.wait_ge(s_rh, at(t + 1))
                dve.tensor_scalar(sh[:], rh[:], 127.0, None, ALU.mult).then_inc(s_sh, 1)

            def quantised_h(t):
                dve.wait_ge(s_hr, at(t + 1))
                dve.wait_ge(s_hT, at(2 * t))
                dve.tensor_scalar(hq[:], hr[:], ROUND, 127.0, ALU.subtract, ALU.min).then_inc(s_hq, 1)
                dve.wait_ge(s_added, at(t))
                dve.tensor_scalar(so[:], ah[:], gamma[:, 2:3], 1.0 / 127, ALU.mult, ALU.mult).then_inc(s_so, 1)

            def add(t):
                dve.wait_ge(s_out, at(t + 1))
                dve.wait_ge(s_bo, at(t + 1))
                dve.wait_ge(s_so, at(t + 1))
                row = X[:, bass.ds(t, 1), :]
                dve.scalar_tensor_tensor(row, ob[:].rearrange("p (a n) -> p a n", a=1), so[:], row, ALU.mult,
                                         ALU.add).then_inc(s_added, 1)

            quantise_x(0)
            quantise_x(1)
            hidden(0)
            quantise_h(0)
            quantised_h(0)
            with dve.Fori(0, T - 2) as t:
                quantise_x(t + 2)
                hidden(t + 1)
                quantise_h(t + 1)
                add(t)
                quantised_h(t + 1)
            hidden(T - 1)
            quantise_h(T - 1)
            add(T - 2)
            quantised_h(T - 1)
            add(T - 1)

        @block.tensor
        def _(pe):
            pe.wait_ge(s_id, at(2))

            def xT(t):
                pe.wait_ge(s_xq, at(t + 1))
                pe.wait_ge(s_xTc, at(t))
                for c in range(KD):
                    last = pe.transpose(xb[:, c * P:(c + 1) * P], xq[:, c * P:(c + 1) * P], identb[:])
                last.then_inc(s_xT, 1)

            def up(t):
                pe.wait_ge(s_xTc, at(t + 1))
                for j in range(NH):
                    for w, dst, s_free, s_done in ((wg, gb, s_gb, s_g), (wv, vb, s_vb, s_v)):
                        pe.wait_ge(s_free, at(t * NH + max(j - 1, 0)))
                        for c in range(KD):
                            last = pe.matmul(dst[j % 2][:], xqT[:, c, :], w[:, c, j * 512:(j + 1) * 512],
                                             start=c == 0, stop=c == KD - 1)
                        last.then_inc(s_done, 1)

            def hT(t):
                pe.wait_ge(s_hq, at(t + 1))
                for j in range(2):
                    pe.wait_ge(s_hTc, at(t * 2))
                    for c in range(8):
                        last = pe.transpose(hb[j][:, c * P:(c + 1) * P], hq[:, (8 * j + c) * P:(8 * j + c + 1) * P],
                                            identb[:])
                    last.then_inc(s_hT, 1)

            def down(t):
                pe.wait_ge(s_hTc, at(t * 2 + 2))
                pe.wait_ge(s_added, at(t))
                for c in range(KH):
                    last = pe.matmul(ob[:], hqT[:, c, :], wo[:, c, :], start=c == 0, stop=c == KH - 1)
                last.then_inc(s_out, 1)

            xT(0)
            up(0)
            xT(1)
            with pe.Fori(0, T - 2) as t:
                up(t + 1)
                hT(t)
                xT(t + 2)
                down(t)
            up(T - 1)
            hT(T - 2)
            down(T - 2)
            hT(T - 1)
            down(T - 1)


def keys_values1(nc, banks, X, eps, eps_rms, ident, ones, xT, ctxT_dram, wk_dram, wv_dram, bk_dram, bv_dram, qn_dram, kn_dram,
                 k_dram, v_dram, B, S, G):
    T = B * S // P
    QT = S // P
    HD = P
    with Phase(nc) as ctx:
        def sb(name, shape, dt=F32):
            return ctx.enter_context(nc.sbuf_tensor("kv_" + name, shape, dt))

        def sem(name):
            return ctx.semaphore("kv_" + name)

        wk, wv = (Pair(ctx, nc, "kv_" + n, [P, KD, D]) for n in ("wk", "wv"))
        wraw = sb("wraw", [P, KD, D])
        bk = sb("bk", [P, G])
        qn, kn, wn = (sb(n, [P, 1]) for n in ("qn", "kn", "wn"))
        bv = sb("bv", [P, D])
        stats = sb("stats", [P, T, 6])
        mv = sb("mv", [P, T, 2])
        std, rstd = sb("std", [P, T]), sb("rstd", [P, T])
        xn = sb("xn", [P, QT, D])
        cTraw = sb("cTraw", [P, KD, S])
        cT = Pair(ctx, nc, "kv_cT", [P, KD, S])
        kf, ksq, kstd, rk, kw = (sb(n, [P, G, S]) for n in ("kf", "ksq", "kstd", "rk", "kw"))
        vf = sb("vf", [P, QT, D])
        K = Pair(ctx, nc, "kv_K", [P, G, S])
        V = Pair(ctx, nc, "kv_V", [P, QT, D])
        tb, kb, sb2, vb = banks[0:2], banks[2:4], banks[4:6], banks[6:8]

        s_small, s_w, s_whi, s_wlo, s_wn = (sem(n) for n in ("small_loaded", "w_loaded", "w_hi", "w_lo", "norm_weight"))
        s_stats, s_mv, s_std, s_rstd = sem("stats"), sem("mean_var"), sem("std"), sem("rstd")
        s_c, s_chi, s_clo = sem("ctxT_loaded"), sem("ctxT_hi"), sem("ctxT_lo")
        s_xn = sem("xn")
        tr = Flow(ctx, nc, "kv_xT")
        s_k, s_kf, s_ksq, s_sum, s_kstd, s_rk, s_kw = (sem(n) for n in (
            "k_product", "k_biased", "k_squared", "k_sum", "k_std", "k_rstd", "k_normed"))
        s_khi, s_klo, s_v, s_vf, s_vhi, s_vlo = (sem(n) for n in ("k_hi", "k_lo", "v_product", "v_biased", "v_hi", "v_lo"))
        s_kst, s_vst = (ctx.queue_semaphore("kv_" + n) for n in ("k_stored", "v_stored"))
        s_stored = sem("stored")
        ctx.start()
        block = ctx.enter_context(nc.Block())

        @block.sync
        def _(sp):
            sp.dma_start(wraw[:], wk_dram).then_inc(s_w, 16)
            sp.dma_start(bk[:], bk_dram).then_inc(s_small, 16)
            sp.dma_start(qn[:], qn_dram).then_inc(s_small, 16)
            sp.dma_start(kn[:], kn_dram).then_inc(s_small, 16)
            sp.dma_start(bv[:], bv_dram.partition_broadcast(P)).then_inc(s_small, 16)
            sp.dma_start(cTraw[:], ctxT_dram[:, :, 0:S]).then_inc(s_c, 16)
            sp.wait_ge(s_wlo, at(1))
            sp.dma_start(wraw[:], wv_dram).then_inc(s_w, 16)

            with sp.Fori(0, B - 1) as i:
                sp.wait_ge(s_clo, at(i + 1))
                sp.dma_start(cTraw[:], ctxT_dram[:, :, bass.ds(i * S + S, S)]).then_inc(s_c, 16)

        @block.gpsimd
        def _(pool):
            with pool.Fori(0, B) as i:
                pool.wait_ge(s_klo, at(i + 1))
                for n, t in enumerate((K.hi, K.lo)):
                    pool.dma_start(k_dram[n][:, :, bass.ds(i * S, S)], f32(t[:])).then_inc(s_kst, 16)
                pool.wait_ge(s_vlo, at(i + 1))
                for n, t in enumerate((V.hi, V.lo)):
                    pool.dma_start(v_dram[n][:, bass.ds(i * QT, QT), :], f32(t[:])).then_inc(s_vst, 16)
                pool.wait_ge(s_kst, i * 32 + 32)
                pool.wait_ge(s_vst, i * 32 + 32)
                pool.sem_inc(s_stored, 1)

        @block.scalar
        def _(act):
            for j, w in enumerate((wk, wv)):
                act.wait_ge(s_w, at(16 * (j + 1)))
                act.activation(w.hi[:], wraw[:], ACT.Copy).then_inc(s_whi, 1)
                if j == 0:
                    act.wait_ge(s_mv, at(T))
                    act.activation(std[:], mv[:, :, 1], ACT.Sqrt, bias=eps[:]).then_inc(s_std, 1)
            act.wait_ge(s_small, at(64))
            with act.Fori(0, B) as i:
                act.wait_ge(s_c, at(i * 16 + 16))
                act.wait_ge(s_v, at(i * QT))
                act.activation(cT.hi[:], cTraw[:], ACT.Copy).then_inc(s_chi, 1)
                for g in range(G):
                    act.wait_ge(s_kf, at(i * G + g + 1))
                    act.activation(ksq[:, g, :], kf[:, g, :], ACT.Square).then_inc(s_ksq, 1)
                for t in range(QT):
                    act.wait_ge(tr.mm, at(i * QT + t + 1))
                    act.wait_ge(s_small, at(64))
                    act.activation(xT.hi[:, :, bass.ds(i * S + t * P, P)], tb[t][:].rearrange("p (k s) -> p k s", k=KD),
                                   ACT.Copy).then_inc(tr.hi, 1)
                for m in range(2):
                    act.wait_ge(s_sum, at(i * 2 + m + 1))
                    act.activation(kstd[:, 2 * m:2 * m + 2, :], sb2[m][:].rearrange("p (k s) -> p k s", k=2),
                                   ACT.Sqrt, bias=eps_rms[:], scale=1.0 / HD).then_inc(s_kstd, 1)
                act.wait_ge(s_vf, at(i * QT + QT))
                act.wait_ge(s_stored, at(i))
                act.activation(V.hi[:], vf[:], ACT.Copy).then_inc(s_vhi, 1)
                act.wait_ge(s_kw, at(i + 1))
                act.activation(K.hi[:], kw[:], ACT.Copy).then_inc(s_khi, 1)

        @block.vector
        def _(dve):
            layernorm_stats(dve, (s_stats, s_mv), X, stats, mv, T)
            dve.wait_ge(s_std, at(1))
            dve.reciprocal(rstd[:], std[:]).then_inc(s_rstd, 1)
            for j, w in enumerate((wk, wv)):
                dve.wait_ge(s_whi, at(j + 1))
                dve.tensor_tensor(w.lo[:], wraw[:], f32(w.hi[:]), ALU.subtract).then_inc(s_wlo, 1)
            dve.wait_ge(s_rstd, at(1))
            dve.wait_ge(s_small, at(64))
            dve.tensor_tensor(wn[:], qn[:], kn[:], ALU.mult).then_inc(s_wn, 1)
            dve.wait_ge(s_wn, at(1))
            with dve.Fori(0, B) as i:
                dve.wait_ge(s_chi, at(i + 1))
                dve.tensor_tensor(cT.lo[:], cTraw[:], f32(cT.hi[:]), ALU.subtract).then_inc(s_clo, 1)
                for t in range(QT):
                    col = bass.ds(i * QT + t, 1)
                    dve.tensor_scalar(xn[:, t:t + 1, :], X[:, col, :], mv[:, col, 0], rstd[:, col],
                                      ALU.subtract, ALU.mult).then_inc(s_xn, 1)
                for g in range(G):
                    dve.wait_ge(s_k, at(i * 2 + g // 2 + 1))
                    dve.wait_ge(s_kw, at(i))
                    dve.tensor_scalar(kf[:, g, :], kb[g // 2][:, (g % 2) * S:(g % 2 + 1) * S], bk[:, g:g + 1], None,
                                      ALU.add).then_inc(s_kf, 1)
                for t in range(QT):
                    dve.wait_ge(tr.hi, at(i * QT + t + 1))
                    cols = bass.ds(i * S + t * P, P)
                    dve.tensor_tensor(xT.lo[:, :, cols], tb[t][:].rearrange("p (k s) -> p k s", k=KD),
                                      f32(xT.hi[:, :, cols]), ALU.subtract).then_inc(tr.lo, 1)
                for t in range(QT):
                    dve.wait_ge(s_v, at(i * QT + t + 1))
                    dve.wait_ge(s_vlo, at(i))
                    dve.tensor_tensor(vf[:, t, :], vb[t][:], bv[:], ALU.add).then_inc(s_vf, 1)
                dve.wait_ge(s_kstd, at(i * 2 + 2))
                dve.reciprocal(rk[:], kstd[:]).then_inc(s_rk, 1)
                dve.wait_ge(s_rk, at(i + 1))
                dve.wait_ge(s_kf, at(i * G + G))
                dve.wait_ge(s_klo, at(i))
                dve.scalar_tensor_tensor(kw[:], kf[:], wn[:], rk[:], ALU.mult, ALU.mult).then_inc(s_kw, 1)
                dve.wait_ge(s_vhi, at(i + 1))
                dve.wait_ge(s_stored, at(i))
                dve.tensor_tensor(V.lo[:], vf[:], f32(V.hi[:]), ALU.subtract).then_inc(s_vlo, 1)
                dve.wait_ge(s_khi, at(i + 1))
                dve.tensor_tensor(K.lo[:], kw[:], f32(K.hi[:]), ALU.subtract).then_inc(s_klo, 1)

        @block.tensor
        def _(pe):
            with pe.Fori(0, B) as i:
                pe.wait_ge(s_wlo, at(1))
                pe.wait_ge(s_clo, at(i + 1))
                pe.wait_ge(s_kf, at(i * G))
                for g in range(G):
                    for c in range(KD):
                        last = matmul3(pe, kb[g // 2][:, (g % 2) * S:(g % 2 + 1) * S],
                                       part(wk, slice(None), c, slice(g * P, (g + 1) * P)),
                                       part(cT, slice(None), c), c == 0, c == KD - 1)
                    if g % 2:
                        last.then_inc(s_k, 1)
                for t in range(QT):
                    pe.wait_ge(s_xn, at(i * QT + t + 1))
                    for c in range(KD):
                        last = pe.transpose(tb[t][:, c * P:(c + 1) * P], xn[:, t, c * P:(c + 1) * P], ident[:])
                    last.then_inc(tr.mm, 1)
                pe.wait_ge(s_wlo, at(2))
                for t in range(QT):
                    pe.wait_ge(s_vf, at(i * QT + t))
                    for c in range(KD):
                        last = matmul3(pe, vb[t][:], part(cT, slice(None), c, slice(t * P, (t + 1) * P)),
                                       part(wv, slice(None), c), c == 0, c == KD - 1)
                    last.then_inc(s_v, 1)
                for m in range(2):
                    pe.wait_ge(s_ksq, at(i * G + 2 * m + 2))
                    pe.matmul(sb2[m][:], ones[:], ksq[:, 2 * m:2 * m + 2, :].rearrange("p k s -> p (k s)"),
                              start=True, stop=True).then_inc(s_sum, 1)


def attention1(nc, banks, X, ident, ones, xT, mask_dram, wq_dram, wo_dram, bq_dram, k_dram, v_dram, B, S, G):
    QT = S // P
    NB = 2
    C = NB * S
    NC = B // NB
    HG = 4
    CT = C // P
    U = NC * HG
    HD = P
    RMS_EPS = 1e-6
    with Phase(nc) as ctx:
        def sb(name, shape, dt=F32):
            return ctx.enter_context(nc.sbuf_tensor("a1_" + name, shape, dt))

        def sem(name):
            return ctx.semaphore("a1_" + name)

        def pair(name, shape):
            return Pair(ctx, nc, "a1_" + name, shape)

        wq, wo = pair("wq", [P, KD, HG * HD]), pair("wo", [P, HG, D])
        wraw = sb("wraw", [P, KD, D])
        bq = sb("bq", [P, G * HG])
        bqg = sb("bqg", [P, HG])
        mask = sb("mask", [P, QT, S])
        q = [pair(f"q{j}", [P, C]) for j in range(2)]
        sq = [sb(f"sq{j}", [P, C]) for j in range(2)]
        K = [pair(f"K{j}", [P, C]) for j in range(2)]
        V = [pair(f"V{j}", [P, CT, HD]) for j in range(2)]
        sc = [sb(f"scores{j}", [P, CT, S]) for j in range(2)]
        pT = [pair(f"pT{b}", [P, QT, S]) for b in range(NB)]
        oT = pair("oT", [P, HG, C])
        ssq = sb("ssq", [P, HG, CT])
        mhalf = sb("mhalf", [P, CT])
        rq = sb("rq", [P, HG, CT])
        nmax, den, rden = (sb(n, [P, 2, CT]) for n in ("nmax", "den", "rden"))
        qb, scb, ptb, ob, ssb = banks[0:2], banks[2:4], banks[4:6], banks[6], banks[7]

        s_small, s_const, s_bqg = sem("small_loaded"), sem("constants"), sem("group_bias")
        s_wload = ctx.queue_semaphore("a1_w_loaded")
        s_wqhi, s_wqlo, s_wohi, s_wolo = sem("wq_hi"), sem("wq_lo"), sem("wo_hi"), sem("wo_lo")
        s_k, s_v = ([sem(f"{n}{j}_loaded") for j in range(2)] for n in "KV")
        fq, ft, fo = (Flow(ctx, nc, "a1_" + n) for n in ("q", "pT", "oT"))
        s_sq, s_ssq, s_ssqc, s_rq = sem("q_squared"), sem("q_sum"), sem("q_sum_copied"), sem("q_rstd")
        s_sc, s_masked, s_nmax, s_exp, s_rden, s_p = (sem(n) for n in (
            "scores", "masked", "nmax", "exp", "rden", "probs"))
        s_out, s_added = sem("out"), sem("added")
        ctx.start()
        block = ctx.enter_context(nc.Block())


        @block.sync
        def _(sp):
            sp.dma_start(bq[:], bq_dram).then_inc(s_small, 16)
            sp.dma_start(mask[:], mask_dram).then_inc(s_small, 16)

            def load(g, c, wait=None):
                cols = slice(c * C, (c + 1) * C)
                if wait is not None:
                    sp.wait_ge(s_sc, at(wait))
                    sp.wait_ge(s_small, at(32))
                for m, t in enumerate((K[c % 2].hi, K[c % 2].lo)):
                    sp.dma_start(f32(t[:]).rearrange("p (a n) -> p a n", a=1), k_dram[m][:, bass.ds(g, 1), cols]).then_inc(s_k[c % 2], 16)
                if wait is not None:
                    sp.wait_ge(fo.mm, at(wait))
                    sp.wait_ge(s_small, at(32))
                for m, t in enumerate((V[c % 2].hi, V[c % 2].lo)):
                    sp.dma_start(f32(t[:]), v_dram[m][:, c * CT:(c + 1) * CT, bass.ds(g * HD, HD)]).then_inc(s_v[c % 2], 16)

            load(0, 0)

            def group(g, more):
                for c in range(NC):
                    last = c == NC - 1
                    if not last or more:
                        load(g + 1 if last else g, (c + 1) % NC, (g * NC + c) * HG)

            with sp.Fori(0, G - 1) as g:
                group(g, True)
            group(G - 1, False)

        @block.gpsimd
        def _(pool):
            pool.dma_start(wraw[:], wq_dram[:, :, 0:HG * HD]).then_inc(s_wload, 16)
            pool.memset(mhalf[:], -0.5).then_inc(s_const, 1)
            pool.wait_ge(s_const, at(1))

            def rstd(u, h):
                pool.wait_ge(s_ssqc, at(u + 1))
                pool.tensor_tensor(rq[:, h % HG, :], ssq[:, h % HG, :], mhalf[:], ALU.pow).then_inc(s_rq, 1)

            def wq_lo(g):
                pool.wait_ge(s_wqhi, at(g + 1))
                pool.tensor_tensor(wq.lo[:], wraw[:], f32(wq.hi[:]), ALU.subtract).then_inc(s_wqlo, 1)
                pool.wait_ge(s_wqlo, at(g + 1))
                pool.dma_start(wraw[:], wo_dram[:, bass.ds(g * HG, HG), :]).then_inc(s_wload, 16)

            def wo_lo(g, more):
                pool.wait_ge(s_wohi, at(g + 1))
                pool.tensor_tensor(wo.lo[:], wraw[:], f32(wo.hi[:]), ALU.subtract).then_inc(s_wolo, 1)
                if more:
                    pool.wait_ge(s_wolo, at(g + 1))
                    pool.dma_start(wraw[:], wq_dram[:, :, bass.ds((g + 1) * HG * HD, HG * HD)]).then_inc(s_wload, 16)

            def group(g, more):
                for i in range(U):
                    if i + 2 < U or more:
                        rstd(g * U + i + 2, i + 2)
                    if i == 0:
                        wo_lo(g, more)
                    if i == U - 4 and more:
                        wq_lo(g + 1)

            wq_lo(0)
            rstd(0, 0)
            rstd(1, 1)
            with pool.Fori(0, G - 1) as g:
                group(g, True)
            group(G - 1, False)

        @block.scalar
        def _(act):
            def wq_hi(g):
                act.wait_ge(s_wload, g * 32 + 16)
                act.wait_ge(fq.mm, at(g * U))
                act.wait_ge(fq.lo, at(g * U))
                act.activation(wq.hi[:], wraw[:], ACT.Copy).then_inc(s_wqhi, 1)
                act.activation(bqg[:], bq[:, bass.ds(g * HG, HG)], ACT.Copy).then_inc(s_bqg, 1)

            def wo_hi(g):
                act.wait_ge(s_wload, g * 32 + 32)
                act.wait_ge(s_out, at(g * NC * CT))
                act.activation(wo.hi[:], wraw[:], ACT.Copy).then_inc(s_wohi, 1)

            def queries(u, g, i, first=False):
                act.wait_ge(fq.mm, at(u + 1))
                if not first:
                    act.wait_ge(s_ssq, at(u - 1))
                act.wait_ge(s_bqg, at(g + 1))
                b = bqg[:, i % HG:i % HG + 1]
                act.activation(sq[i % 2][:], qb[i % 2][:], ACT.Square, bias=b).then_inc(s_sq, 1)
                act.activation(q[i % 2].hi[:], qb[i % 2][:], ACT.Identity, bias=b).then_inc(fq.hi, 1)

            def exp(u, i):
                for t in range(CT):
                    act.wait_ge(s_nmax, at(u * NB + t // QT + 1))
                    row = sc[i % 2][:, t, :]
                    act.activation(row, row, ACT.Exp, bias=nmax[:, i % 2, t:t + 1],
                                   accum_out=den[:, i % 2, t:t + 1]).then_inc(s_exp, 1)

            def transposed(u):
                for b in range(NB):
                    act.wait_ge(ft.mm, at(u * NB + b + 1))
                    act.activation(pT[b].hi[:], ptb[b][:].rearrange("p (k s) -> p k s", k=QT), ACT.Copy).then_inc(ft.hi, 1)

            def output(u, n, i):
                act.wait_ge(fo.mm, at(u + 1))
                if i % HG == 0:
                    act.wait_ge(s_out, at(n * CT))
                act.activation(oT.hi[:, i % HG, :], ob[:], ACT.Copy).then_inc(fo.hi, 1)

            def group(g, more):
                for i in range(U):
                    u, n = g * U + i, g * NC + i // HG
                    transposed(u)
                    if i + 1 < U or more:
                        exp(u + 1, i + 1)
                    if i + 3 < U or more:
                        queries(u + 3, g + (i + 3) // U, i + 3)
                    if i == 0:
                        wo_hi(g)
                    if i == U - 4 and more:
                        wq_hi(g + 1)
                    output(u, n, i)

            act.wait_ge(s_small, at(32))
            wq_hi(0)
            queries(0, 0, 0, True)
            queries(1, 0, 1, True)
            exp(0, 0)
            queries(2, 0, 2)
            with act.Fori(0, G - 1) as g:
                group(g, True)
            group(G - 1, False)

        @block.vector
        def _(dve):
            def queries(u, i):
                dve.wait_ge(fq.hi, at(u + 1))
                dve.scalar_tensor_tensor(q[i % 2].lo[:], qb[i % 2][:], bqg[:, i % HG:i % HG + 1],
                                         f32(q[i % 2].hi[:]), ALU.add, ALU.subtract).then_inc(fq.lo, 1)

            def square_sums(u, i):
                dve.wait_ge(s_ssq, at(u + 1))
                dve.tensor_scalar(ssq[:, i % HG, :], ssb[:, 0:CT], HD * RMS_EPS, None, ALU.add).then_inc(s_ssqc, 1)

            def scores(u, i):
                dve.wait_ge(s_rq, at(u + 1))
                dve.wait_ge(s_sc, at(u + 1))
                for b in range(NB):
                    for t in range(QT):
                        r = b * QT + t
                        dve.scalar_tensor_tensor(sc[i % 2][:, r, :], scb[b][:, t * S:(t + 1) * S],
                                                 rq[:, i % HG, r:r + 1], mask[:, t, :], ALU.mult,
                                                 ALU.add).then_inc(s_masked, 1)

            def maxima(u, i):
                for b in range(NB):
                    dve.wait_ge(s_masked, at(u * CT + QT * (b + 1)))
                    dve.tensor_reduce(nmax[:, i % 2, b * QT:(b + 1) * QT], sc[i % 2][:, b * QT:(b + 1) * QT, :], AX.X,
                                      ALU.max, negate=True).then_inc(s_nmax, 1)

            def normalise(u, i):
                dve.wait_ge(s_exp, at(u * CT + CT))
                dve.reciprocal(rden[:, i % 2, :], den[:, i % 2, :]).then_inc(s_rden, 1)
                dve.wait_ge(s_rden, at(u + 1))
                for t in range(CT):
                    row = sc[i % 2][:, t, :]
                    dve.tensor_scalar(row, row, rden[:, i % 2, t:t + 1], None, ALU.mult).then_inc(s_p, 1)

            def transposed(u):
                for b in range(NB):
                    dve.wait_ge(ft.hi, at(u * NB + b + 1))
                    dve.tensor_tensor(pT[b].lo[:], ptb[b][:].rearrange("p (k s) -> p k s", k=QT), f32(pT[b].hi[:]),
                                      ALU.subtract).then_inc(ft.lo, 1)

            def output(u, i):
                dve.wait_ge(fo.hi, at(u + 1))
                dve.tensor_tensor(oT.lo[:, i % HG, :], ob[:], f32(oT.hi[:, i % HG, :]), ALU.subtract).then_inc(fo.lo, 1)

            def add(n, c):
                for t in range(CT):
                    dve.wait_ge(s_out, at(n * CT + t + 1))
                    row = X[:, c * CT + t, :]
                    dve.tensor_tensor(row, row, ptb[t % 2][:], ALU.add).then_inc(s_added, 1)

            def group(g, more):
                for i in range(U):
                    u, n = g * U + i, g * NC + i // HG
                    if i + 2 < U or more:
                        square_sums(u + 2, i + 2)
                    transposed(u)
                    if i + 1 < U or more:
                        normalise(u + 1, i + 1)
                    if i + 2 < U or more:
                        scores(u + 2, i + 2)
                    if i + 3 < U or more:
                        queries(u + 3, i + 3)
                    if i + 2 < U or more:
                        maxima(u + 2, i + 2)
                    output(u, i)
                    if i % HG == HG - 1:
                        add(n, i // HG)

            dve.wait_ge(s_small, at(32))
            queries(0, 0)
            queries(1, 1)
            square_sums(0, 0)
            scores(0, 0)
            maxima(0, 0)
            queries(2, 2)
            square_sums(1, 1)
            scores(1, 1)
            maxima(1, 1)
            normalise(0, 0)
            with dve.Fori(0, G - 1) as g:
                group(g, True)
            group(G - 1, False)

        @block.tensor
        def _(pe):
            def queries(u, g, i, first=False):
                c, h = i // HG % NC, i % HG
                if c == 0 and h == 0:
                    pe.wait_ge(s_wqlo, at(g + 1))
                if not first:
                    pe.wait_ge(fq.lo, at(u - 1))
                for k in range(KD):
                    last = matmul3(pe, qb[i % 2][:], part(wq, slice(None), k, slice(h * HD, (h + 1) * HD)),
                                   part(xT, slice(None), k, slice(c * C, (c + 1) * C)), k == 0, k == KD - 1)
                last.then_inc(fq.mm, 1)

            def square_sums(u, i):
                pe.wait_ge(s_sq, at(u + 1))
                pe.wait_ge(s_ssqc, at(u))
                for t in range(CT):
                    last = pe.matmul(ssb[:, t:t + 1], sq[i % 2][:, t * P:(t + 1) * P], ones[:, 0:1], start=True,
                                     stop=True)
                last.then_inc(s_ssq, 1)

            def scores(u, g, i):
                c = i // HG % NC
                pe.wait_ge(fq.lo, at(u + 1))
                pe.wait_ge(s_masked, at(u * CT))
                if i % HG == 0:
                    pe.wait_ge(s_k[c % 2], at((g * (NC // 2) + i // HG // 2) * 32 + 32))
                for b in range(NB):
                    for t in range(QT):
                        r = b * QT + t
                        last = matmul3(pe, scb[b][:, t * S:(t + 1) * S],
                                       part(q[i % 2], slice(None), slice(r * P, (r + 1) * P)),
                                       part(K[c % 2], slice(None), slice(b * S, (b + 1) * S)), True, True)
                last.then_inc(s_sc, 1)

            def transposed(u, n, i):
                if i % HG == 0:
                    pe.wait_ge(s_added, at(n * CT))
                for b in range(NB):
                    for t in range(QT):
                        r = b * QT + t
                        pe.wait_ge(s_p, at(u * CT + r + 1))
                        for k in range(QT):
                            last = pe.transpose(ptb[b][:, k * S + t * P:k * S + (t + 1) * P],
                                                sc[i % 2][:, r, k * P:(k + 1) * P], ident[:])
                    last.then_inc(ft.mm, 1)

            def output(u, g, i):
                v = V[i // HG % 2]
                if i % HG == 0:
                    pe.wait_ge(s_v[i // HG % 2], at((g * (NC // 2) + i // HG // 2) * 32 + 32))
                pe.wait_ge(fo.lo, at(u))
                for b in range(NB):
                    pe.wait_ge(ft.lo, at(u * NB + b + 1))
                    for k in range(QT):
                        last = matmul3(pe, ob[:, b * S:(b + 1) * S], part(v, slice(None), b * QT + k),
                                       part(pT[b], slice(None), k), k == 0, k == QT - 1)
                last.then_inc(fo.mm, 1)

            def project(u, n):
                pe.wait_ge(fo.lo, at(u))
                for t0 in range(0, CT, 2):
                    for heads in (range(HG - 1), range(HG - 1, HG)):
                        for t in (t0, t0 + 1):
                            if t0:
                                pe.wait_ge(s_added, at(n * CT + t - 1))
                            pe.wait_ge(fo.lo, at(u + (1 if HG - 1 in heads else 0)))
                            for k in heads:
                                last = matmul3(pe, ptb[t % 2][:], part(oT, slice(None), k, slice(t * P, (t + 1) * P)),
                                               part(wo, slice(None), k), k == 0, k == HG - 1)
                            if HG - 1 in heads:
                                last.then_inc(s_out, 1)

            def group(g, more):
                for i in range(U):
                    u, n = g * U + i, g * NC + i // HG
                    transposed(u, n, i)
                    if i + 2 < U or more:
                        square_sums(u + 2, i + 2)
                    if i + 3 < U or more:
                        queries(u + 3, g + (i + 3) // U, i + 3)
                    if i + 2 < U or more:
                        scores(u + 2, g, i + 2)
                    output(u, g, i)
                    if i % HG == HG - 1:
                        if i == HG - 1:
                            pe.wait_ge(s_wolo, at(g + 1))
                        project(u, n)

            queries(0, 0, 0, True)
            queries(1, 0, 1, True)
            square_sums(0, 0)
            scores(0, 0, 0)
            queries(2, 0, 2)
            square_sums(1, 1)
            scores(1, 0, 1)
            with pe.Fori(0, G - 1) as g:
                group(g, True)
            group(G - 1, False)


def router(nc, banks, X, eps, ident, xT, combine, rw_dram, sdb_dram, T, E):
    TOP = 2
    with Phase(nc) as ctx:
        def sb(name, shape, dt=F32):
            return ctx.enter_context(nc.sbuf_tensor("r_" + name, shape, dt))

        def sem(name):
            return ctx.semaphore("r_" + name)

        rw = sb("rw", [P, KD, E])
        sdb = sb("sdb", [P, D])
        stats = sb("stats", [P, T, 6])
        mv = sb("mv", [P, T, 2])
        std, rstd = sb("std", [P, T]), sb("rstd", [P, T])
        xn = [sb(f"xn{j}", [P, D]) for j in range(2)]
        xt = [sb(f"xt{j}", [P, KD, P]) for j in range(2)]
        logits = sb("logits", [P, T, E])
        nmax = sb("nmax", [P, T])
        ex = sb("ex", [P, T, E])
        top = sb("top", [P, T, 8])
        topi = sb("topi", [P, T, 8], U32)
        atf = sb("atf", [P, T, 8])
        expert = sb("expert", [P, E])
        hot = sb("hot", [P, T, TOP, E])
        tsum, rsum = sb("tsum", [P, T]), sb("rsum", [P, T])
        tb, lb = banks[0:2], banks[2:4]
        s_ld, s_const = sem("loaded"), sem("constants")
        s_stats, s_mv, s_std, s_rstd = sem("stats"), sem("mean_var"), sem("std"), sem("rstd")
        s_xn, s_bias, s_tr, s_xt, s_hi, s_lo = (sem(n) for n in ("xn", "bias_added", "transposed", "xt", "xT_hi", "xT_lo"))
        s_log, s_logc, s_nmax, s_sub, s_exp, s_top, s_at = (sem(n) for n in (
            "logits", "logits_copied", "nmax", "sub", "exp", "top", "at"))
        s_atf, s_sum, s_rsum, s_hot, s_comb = (sem(n) for n in ("atf", "sum", "rsum", "hot", "combine"))
        ctx.start()
        block = ctx.enter_context(nc.Block())

        @block.sync
        def _(sp):
            sp.dma_start(rw[:], rw_dram).then_inc(s_ld, 16)
            sp.dma_start(sdb[:], sdb_dram.partition_broadcast(P)).then_inc(s_ld, 16)

        @block.gpsimd
        def _(pool):
            pool.iota(expert[:], pattern=[[1, E]], base=0, channel_multiplier=0,
                      allow_small_or_imprecise_dtypes=True).then_inc(s_const, 1)
            pool.memset(combine[:, :, E:], 1.0).then_inc(s_const, 1)
            pool.wait_ge(s_ld, at(32))
            with pool.Fori(0, T) as t:
                pool.wait_ge(s_xn, at(t + 1))
                row = X[:, bass.ds(t, 1), :]
                pool.tensor_tensor(row, row, sdb[:].rearrange("p (a n) -> p a n", a=1), ALU.add).then_inc(s_bias, 1)

        @block.scalar
        def _(act):
            act.wait_ge(s_mv, at(T))
            act.activation(std[:], mv[:, :, 1], ACT.Sqrt, bias=eps[:]).then_inc(s_std, 1)
            with act.Fori(0, T // 2) as i:
                for j in range(2):
                    act.wait_ge(s_tr, at(i * 2 + j + 1))
                    act.wait_ge(s_log, at(i * 2))
                    act.wait_ge(s_lo, at(i * 2))
                    act.activation(xt[j][:], tb[j][:].rearrange("p (k s) -> p k s", k=KD), ACT.Copy).then_inc(s_xt, 1)
                    act.wait_ge(s_xt, at(i * 2 + j + 1))
                    act.wait_ge(s_std, at(1))
                    act.activation(xT.hi[:, :, bass.ds(i * 2 * P + j * P, P)], xt[j][:], ACT.Copy).then_inc(s_hi, 1)
            act.wait_ge(s_sub, at(1))
            act.activation(ex[:], logits[:], ACT.Exp).then_inc(s_exp, 1)

        @block.vector
        def _(dve):
            layernorm_stats(dve, (s_stats, s_mv), X, stats, mv, T)
            dve.wait_ge(s_std, at(1))
            dve.reciprocal(rstd[:], std[:]).then_inc(s_rstd, 1)
            dve.wait_ge(s_rstd, at(1))

            def norm(t, j, first=False):
                col = bass.ds(t, 1)
                if not first:
                    dve.wait_ge(s_tr, at(t - 1))
                dve.tensor_scalar(xn[j][:].rearrange("p (a n) -> p a n", a=1), X[:, col, :], mv[:, col, 0], rstd[:, col],
                                  ALU.subtract, ALU.mult).then_inc(s_xn, 1)

            def rest(t, j):
                dve.wait_ge(s_hi, at(t + 1))
                cols = bass.ds(t * P, P)
                dve.tensor_tensor(xT.lo[:, :, cols], xt[j][:], f32(xT.hi[:, :, cols]), ALU.subtract).then_inc(s_lo, 1)
                dve.wait_ge(s_log, at(t + 1))
                dve.tensor_copy(logits[:, bass.ds(t, 1), :], lb[j][:, 0:E].rearrange("p (a n) -> p a n", a=1))\
                   .then_inc(s_logc, 1)

            norm(0, 0, True)
            norm(1, 1, True)
            with dve.Fori(0, T // 2 - 1) as i:
                for j in range(2):
                    norm(i * 2 + 2 + j, j)
                    rest(i * 2 + j, j)
            for j in range(2):
                rest(T - 2 + j, j)
            dve.wait_ge(s_logc, at(T))
            dve.tensor_reduce(nmax[:], logits[:], AX.X, ALU.max).then_inc(s_nmax, 1)
            dve.wait_ge(s_nmax, at(1))
            dve.tensor_tensor(logits[:], logits[:], nmax[:].unsqueeze(2).broadcast_to([P, T, E]),
                              ALU.subtract).then_inc(s_sub, 1)
            dve.wait_ge(s_exp, at(1))
            for t in range(T):
                dve.max(top[:, t, :], ex[:, t, :]).then_inc(s_top, 1)
            for t in range(T):
                dve.wait_ge(s_top, at(t + 1))
                dve.max_index(topi[:, t, :], top[:, t, :], ex[:, t, :]).then_inc(s_at, 1)
            dve.wait_ge(s_at, at(T))
            dve.tensor_copy(atf[:], topi[:]).then_inc(s_atf, 1)
            dve.tensor_tensor(tsum[:], top[:, :, 0], top[:, :, 1], ALU.add).then_inc(s_sum, 1)
            dve.wait_ge(s_sum, at(1))
            dve.reciprocal(rsum[:], tsum[:]).then_inc(s_rsum, 1)
            dve.wait_ge(s_atf, at(1))
            dve.wait_ge(s_const, at(2))
            for n in range(TOP):
                dve.tensor_tensor(hot[:, :, n, :], expert[:].unsqueeze(1).broadcast_to([P, T, E]),
                                  atf[:, :, n:n + 1].broadcast_to([P, T, E]), ALU.is_equal).then_inc(s_hot, 1)
            dve.wait_ge(s_hot, at(2))
            dve.tensor_tensor(hot[:, :, 0, :], hot[:, :, 0, :], hot[:, :, 1, :], ALU.add).then_inc(s_hot, 1)
            dve.wait_ge(s_hot, at(3))
            dve.tensor_tensor(hot[:, :, 0, :], hot[:, :, 0, :], ex[:], ALU.mult).then_inc(s_hot, 1)
            dve.wait_ge(s_hot, at(4))
            dve.wait_ge(s_rsum, at(1))
            dve.tensor_tensor(combine[:, :, 0:E], hot[:, :, 0, :], rsum[:].unsqueeze(2).broadcast_to([P, T, E]),
                              ALU.mult).then_inc(s_comb, 1)

        @block.tensor
        def _(pe):
            pe.wait_ge(s_ld, at(32))
            with pe.Fori(0, T // 2) as i:
                for j in range(2):
                    t = i * 2 + j
                    pe.wait_ge(s_xn, at(t + 1))
                    pe.wait_ge(s_hi, at(i * 2))
                    for c in range(KD):
                        last = pe.transpose(tb[j][:, c * P:(c + 1) * P], xn[j][:, c * P:(c + 1) * P], ident[:])
                    last.then_inc(s_tr, 1)
                for j in range(2):
                    t = i * 2 + j
                    pe.wait_ge(s_xt, at(t + 1))
                    pe.wait_ge(s_logc, at(i * 2))
                    for c in range(KD):
                        last = pe.matmul(lb[j][:, 0:E], xt[j][:, c, :], rw[:, c, :], start=c == 0, stop=c == KD - 1)
                    last.then_inc(s_log, 1)


def experts(nc, banks, X, xT, combine, gw_dram, uw_dram, dw_dram, gb_dram, ub_dram, T, E, I):
    C = 512
    NC = T * P // C
    CT = C // P
    MT = [(m, min(P, I - m)) for m in range(0, I, P)]
    M = len(MT)
    with Phase(nc) as ctx:
        def sb(name, shape, dt=F32):
            return ctx.enter_context(nc.sbuf_tensor("e_" + name, shape, dt))

        def sem(name):
            return ctx.semaphore("e_" + name)

        wg, wu = ([Pair(ctx, nc, f"e_{n}{j}", [P, KD, I]) for j in range(2)] for n in ("wg", "wu"))
        wd = [Pair(ctx, nc, f"e_wd{j}", [P, M, D]) for j in range(2)]
        graw, uraw, draw = sb("graw", [P, KD, I]), sb("uraw", [P, KD, I]), sb("draw", [P, M, D])
        gbias, ubias = sb("gbias", [P, E, M]), sb("ubias", [P, E, M])
        gbe, ube = ([sb(f"{n}{j}", [P, M]) for j in range(2)] for n in ("gbe", "ube"))
        ce = sb("ce", [P, 2, T])
        sg = [sb(f"sg{j}", [P, C]) for j in range(2)]
        hf = [sb(f"hf{j}", [P, C]) for j in range(2)]
        h = Pair(ctx, nc, "e_h", [P, M, C])
        gb, ub, yb = banks[0:2], banks[2:4], banks[4:8]
        s_small, s_raw, s_whi, s_wlo, s_be, s_ce = (sem(n) for n in (
            "biases_loaded", "w_loaded", "w_hi", "w_lo", "expert_bias", "expert_combine"))
        s_g, s_sg, s_u, s_h, s_hi, s_lo, s_y, s_add = (sem(n) for n in (
            "gate", "silu", "up", "h", "h_hi", "h_lo", "down", "added"))
        W = 2 * NC
        ctx.start()
        block = ctx.enter_context(nc.Block())

        LAST = MT[-1]
        full = I // P

        @block.sync
        def _(sp):
            sp.dma_start(gbias[:], gb_dram).then_inc(s_small, 16)
            sp.dma_start(ubias[:], ub_dram).then_inc(s_small, 16)
            with sp.Fori(0, E) as e:
                sp.wait_ge(s_wlo, at(e * 3))
                sp.wait_ge(s_small, at(32))
                one = bass.ds(e, 1)
                src = lambda w: w[one].rearrange("a (k p) n -> p (a k) n", p=P)
                sp.dma_start(graw[:], src(gw_dram)).then_inc(s_raw, 16)
                sp.dma_start(uraw[:], src(uw_dram)).then_inc(s_raw, 16)
                sp.dma_start(draw[:, 0:full, :], dw_dram[one, 0:full * P, :].rearrange("a (k p) n -> p (a k) n", p=P))\
                  .then_inc(s_raw, 16)
                sp.dma_start(draw[0:LAST[1], full:M, :], dw_dram[one, LAST[0]:I, :].rearrange("a p n -> p a n"))\
                  .then_inc(s_raw, 16)

        @block.gpsimd
        def _(pool):
            with pool.Fori(0, E // 2) as i:
                for j in range(2):
                    e = i * 2 + j
                    for n, (w, raw) in enumerate(((wg, graw), (wu, uraw), (wd, draw))):
                        pool.wait_ge(s_whi, at(e * 3 + n + 1))
                        if n < 2:
                            ins = pool.tensor_tensor(w[j].lo[:], raw[:], f32(w[j].hi[:]), ALU.subtract)
                        else:
                            pool.tensor_tensor(w[j].lo[:, 0:full, :], raw[:, 0:full, :], f32(w[j].hi[:, 0:full, :]),
                                               ALU.subtract)
                            r = (slice(0, LAST[1]), full)
                            ins = pool.tensor_tensor(w[j].lo[r], raw[r], f32(w[j].hi[r]), ALU.subtract)
                        ins.then_inc(s_wlo, 1)

        @block.scalar
        def _(act):
            def split(e, j, first=False):
                act.wait_ge(s_raw, at(e * 64 + 64))
                if not first:
                    act.wait_ge(s_add, at((e - 1) * NC * CT))
                act.activation(wg[j].hi[:], graw[:], ACT.Copy).then_inc(s_whi, 1)
                act.activation(wu[j].hi[:], uraw[:], ACT.Copy).then_inc(s_whi, 1)
                act.activation(wd[j].hi[:, 0:full, :], draw[:, 0:full, :], ACT.Copy)
                r = (slice(0, LAST[1]), full)
                act.activation(wd[j].hi[r], draw[r], ACT.Copy).then_inc(s_whi, 1)
                for dst, b in ((gbe, gbias), (ube, ubias)):
                    act.activation(dst[j][:].rearrange("p (a m) -> p a m", a=1), b[:, bass.ds(e, 1), :],
                                   ACT.Copy).then_inc(s_be, 1)
                act.activation(ce[:, j, :].unsqueeze(2), combine[:, :, bass.ds(e, 1)], ACT.Copy).then_inc(s_ce, 1)

            def unit(w, e, j):
                for m in range(M):
                    n, q = w * M + m, (m + w_par[0]) % 2
                    act.wait_ge(s_g, at(n + 1))
                    act.wait_ge(s_h, at(w * M + max(m - 1, 0)))
                    r = slice(0, MT[m][1])
                    act.activation(sg[q][r, :], gb[q][r, :], ACT.Silu, bias=gbe[j][r, m:m + 1]).then_inc(s_sg, 1)
                    act.wait_ge(s_h, at(n + 1))
                    if m == 0:
                        act.wait_ge(s_y, at(w * CT))
                    act.activation(h.hi[r, m, :], hf[q][r, :], ACT.Copy).then_inc(s_hi, 1)
                w_par[0] += M

            w_par = [0]
            act.wait_ge(s_small, at(32))
            split(0, 0, True)

            def turn(i, more):
                for j in range(2):
                    for c in range(NC):
                        act.wait_ge(s_be, at(i * 4 + 2 * (j + 1)))
                        unit(i * W + j * NC + c, None, j)
                        if c == 0 and (j == 0 or more):
                            split(i * 2 + j + 1, 1 - j)

            with act.Fori(0, E // 2 - 1) as i:
                turn(i, True)
            turn(E // 2 - 1, False)

        @block.vector
        def _(dve):
            par = [0]

            def add(w, c, j):
                for t in range(CT):
                    dve.wait_ge(s_y, at(w * CT + t + 1))
                    row = X[:, c * CT + t, :]
                    dve.scalar_tensor_tensor(row, yb[t][:], ce[:, j, c * CT + t:c * CT + t + 1], row, ALU.mult,
                                             ALU.add).then_inc(s_add, 1)

            def unit(w, c, j, first=False):
                for m in range(M):
                    n, q = w * M + m, (m + par[0]) % 2
                    r = slice(0, MT[m][1])
                    dve.wait_ge(s_sg, at(n + 1))
                    dve.wait_ge(s_u, at(n + 1))
                    dve.wait_ge(s_lo, at(w * M + max(m - 1, 0)))
                    dve.scalar_tensor_tensor(hf[q][r, :], ub[q][r, :], ube[j][r, m:m + 1], sg[q][r, :], ALU.add,
                                             ALU.mult).then_inc(s_h, 1)
                    dve.wait_ge(s_hi, at(n + 1))
                    dve.tensor_tensor(h.lo[r, m, :], hf[q][r, :], f32(h.hi[r, m, :]), ALU.subtract).then_inc(s_lo, 1)
                par[0] += M
                add(w, c, j)

            with dve.Fori(0, E // 2) as i:
                for j in range(2):
                    dve.wait_ge(s_be, at(i * 4 + 2 * (j + 1)))
                    dve.wait_ge(s_ce, at(i * 2 + j + 1))
                    for c in range(NC):
                        unit(i * W + j * NC + c, c, j)

        @block.tensor
        def _(pe):
            par = [0]

            def unit(w, c, j):
                cols = slice(c * C, (c + 1) * C)
                for m, (m0, mn) in enumerate(MT):
                    q = (m + par[0]) % 2
                    for weights, dst, s_free, s_done in ((wg, gb, s_sg, s_g), (wu, ub, s_h, s_u)):
                        pe.wait_ge(s_free, at(w * M + max(m - 1, 0)))
                        for k in range(KD):
                            last = matmul3(pe, dst[q][0:mn, :], part(weights[j], slice(None), k, slice(m0, m0 + mn)),
                                           part(xT, slice(None), k, cols), k == 0, k == KD - 1)
                        last.then_inc(s_done, 1)
                par[0] += M
                for ms in (range(M - 1), range(M - 1, M)):
                    for t in range(CT):
                        pe.wait_ge(s_lo, at(w * M + max(ms) + 1))
                        pe.wait_ge(s_add, at(w * CT))
                        for m in ms:
                            r = slice(0, MT[m][1])
                            last = matmul3(pe, yb[t][:], part(h, r, m, slice(t * P, (t + 1) * P)),
                                           part(wd[j], r, m), m == 0, m == M - 1)
                        if M - 1 in ms:
                            last.then_inc(s_y, 1)

            with pe.Fori(0, E // 2) as i:
                for j in range(2):
                    pe.wait_ge(s_wlo, at(i * 6 + 3 * (j + 1)))
                    for c in range(NC):
                        unit(i * W + j * NC + c, c, j)


def program(nc, a, out, stop=4, start=0):
    B, S, _ = a["x"].shape
    T = B * S // P
    with ExitStack() as ctx:
        X = ctx.enter_context(nc.sbuf_tensor("X", [P, T, D], F32))
        eps = ctx.enter_context(nc.sbuf_tensor("eps", [P, 1], F32))
        ident = ctx.enter_context(nc.sbuf_tensor("ident", [P, P], F32))
        eps_rms = ctx.enter_context(nc.sbuf_tensor("eps_rms", [P, 1], F32))
        ones = ctx.enter_context(nc.sbuf_tensor("ones", [P, P], F32))
        banks = [ctx.enter_context(nc.psum_tensor(f"bank{j}", [P, 512], F32)) for j in range(8)]
        s_const = ctx.enter_context(nc.semaphore("constants"))
        s_out = ctx.enter_context(nc.semaphore("stored"))
        with nc.Block() as block:
            @block.gpsimd
            def _(pool):
                pool.memset(eps[:], LN_EPS).then_inc(s_const, 1)
                pool.memset(ident[:], 0.0).then_inc(s_const, 1)
                pool.memset(ones[:], 1.0).then_inc(s_const, 1)
                pool.memset(eps_rms[:], 1e-6).then_inc(s_const, 1)
                pool.wait_ge(s_const, 2)
                pool.affine_select(out=ident[:], in_=ident[:], compare_op=ALU.not_equal, fill=1.0, base=0,
                                   pattern=[[-1, P]], channel_multiplier=1).then_inc(s_const, 1)
        tok = lambda ap: ap.rearrange("b s d -> (b s) d").rearrange("(t p) d -> p t d", p=P)
        ktile = lambda ap: ap.rearrange("(k p) n -> p k n", p=P)
        if start:
            with nc.Block() as block:
                @block.sync
                def _(sp):
                    sp.dma_start(X[:], tok(a["x"])).then_inc(s_const, 16)
                    sp.wait_ge(s_const, 21)
        if start < 1:
          attention0(nc, banks, X, eps, ident, tok(a["x"]), tok(a["ctx"]), ktile(a["ctxT"]),
                   [ktile(a[n]) for n in ("wqT", "wkT", "wvT", "woT")], B, S)
        if start < 2 and stop >= 2:
            ffn0(nc, banks, X, eps, ident, ones, [ktile(a[n]) for n in ("gwT", "vwT", "owT")], [a[n] for n in ("gb", "vb", "ob")], T)
        if start < 3 and stop >= 3:
            G = 4
            k_dram = [nc.dram_tensor(f"K_{n}", (P, G, B * S), F32, kind="Internal").ap() for n in ("hi", "lo")]
            v_dram = [nc.dram_tensor(f"V_{n}", (P, T, D), F32, kind="Internal").ap() for n in ("hi", "lo")]
            with ExitStack() as cx:
                xT = Pair(cx, nc, "x1T", [P, KD, B * S])
                keys_values1(nc, banks, X, eps, eps_rms, ident, ones, xT, ktile(a["ctxT"]), ktile(a["Wk"]), ktile(a["Wv"]),
                             a["bkT"], a["bv"], a["qn"], a["kn"], k_dram, v_dram, B, S, G)
                attention1(nc, banks, X, ident, ones, xT, a["mask"].rearrange("(t p) s -> p t s", p=P), ktile(a["Wq"]),
                           ktile(a["Wo"]), a["bqT"], k_dram, v_dram, B, S, G)
        if stop >= 4:
            E = a["rwT"].shape[1]
            EA, _, I = a["egw"].shape
            with ExitStack() as cx:
                xT = Pair(cx, nc, "x2T", [P, KD, B * S])
                combine = cx.enter_context(nc.sbuf_tensor("combine", [P, T, EA], F32))
                router(nc, banks, X, eps, ident, xT, combine, ktile(a["rwT"]), a["sdb"], T, E)
                experts(nc, banks, X, xT, combine, a["egw"], a["euw"], a["edw"], a["egb"], a["eub"], T, EA, I)
        with nc.Block() as block:
            @block.sync
            def _(sp):
                sp.dma_start(tok(out), X[:]).then_inc(s_out, 16)
                sp.wait_ge(s_out, 16)


def _layout(inputs):
    import numpy as np
    g = lambda n: np.asarray(inputs[n])
    t = lambda n: np.ascontiguousarray(g(n).T)
    E, _, I = g("L1_ffn_gate_w").shape

    def experts_in(n):
        shared = g(f"L1_ffn_s_{n}_w").reshape(512, 2, I).transpose(1, 0, 2)
        return np.concatenate([g(f"L1_ffn_{n}_w"), shared])

    def bias(n):
        b = np.zeros((E + 2, -(-I // 128) * 128), np.float32)
        b[E:, :I] = g(f"L1_ffn_s_{n}_b").reshape(2, I)
        return b.reshape(E + 2, -1, 128).transpose(2, 0, 1)

    return {
        "x": g("x"), "ctx": g("ctx_2048"),
        "ctxT": np.ascontiguousarray(g("ctx_2048").reshape(-1, 512).T),
        "rwT": t("L1_ffn_router_w"), "sdb": g("L1_ffn_s_down_b"),
        "egw": experts_in("gate"), "euw": experts_in("up"),
        "edw": np.concatenate([g("L1_ffn_down_w"), g("L1_ffn_s_down_w").reshape(2, I, 512)]),
        "egb": bias("gate"), "eub": bias("up"),
        "Wq": g("L1_xattn_Wq"), "Wk": g("L1_xattn_Wk"), "Wv": g("L1_xattn_Wv"), "Wo": g("L1_xattn_Wo"),
        "bqT": g("L1_xattn_bq").reshape(-1, 128).T, "bkT": g("L1_xattn_bk").reshape(-1, 128).T, "bv": g("L1_xattn_bv"),
        "qn": g("L1_xattn_qn_w").reshape(128, 1), "kn": g("L1_xattn_kn_w").reshape(128, 1),
        "mask": g("mask_1xSxS2_ff0")[0],
        "gwT": t("L0_ffn_gate_w"), "vwT": t("L0_ffn_val_w"), "owT": t("L0_ffn_out_w"),
        "gb": g("L0_ffn_gate_b"), "vb": g("L0_ffn_val_b"), "ob": g("L0_ffn_out_b"),
        "wqT": t("L0_xattn_wq"), "wkT": t("L0_xattn_wk"), "wvT": t("L0_xattn_wv"), "woT": t("L0_xattn_wo"),
    }


def kernel(**inputs):
    import numpy as np
    import concourse.bacc as bacc
    from concourse.bass_utils import run_bass_kernel_spmd

    nc = bacc.Bacc("TRN2", target_bir_lowering=False, num_devices=1)
    arrays, args = {}, {}
    for name, a in _layout(inputs).items():
        a = np.ascontiguousarray(a)
        arrays["in_" + name] = a
        args[name] = nc.dram_tensor("in_" + name, a.shape, mybir.dt.from_np(a.dtype), kind="ExternalInput").ap()
    out = nc.dram_tensor("out", (8, 256, 512), F32, kind="ExternalOutput").ap()
    program(nc, args, out)
    r = run_bass_kernel_spmd(nc, [arrays], core_ids=[0])
    return r.results[0]["out"]
```

```python
from contextlib import ExitStack

import concourse.bass as bass
from concourse import mybir

ALU = mybir.AluOpType
ACT = mybir.ActivationFunctionType
AX = mybir.AxisListType
F32 = mybir.dt.float32
F32R = mybir.dt.float32r
BF16 = mybir.dt.bfloat16
U32 = mybir.dt.uint32

P = 128
D = 512
KD = D // P
ROUND = 12582912.0
LN_EPS = 1e-5


def at(count):
    return count + 1


class Phase(ExitStack):

    def __init__(self, nc):
        super().__init__()
        self.nc, self.semaphores, self.from_zero = nc, [], []

    def semaphore(self, name):
        self.semaphores.append(self.nc.alloc_semaphore(name=name))
        return self.semaphores[-1]

    def queue_semaphore(self, name):
        self.from_zero.append(self.nc.alloc_semaphore(name=name))
        return self.from_zero[-1]

    def start(self):
        for s in self.semaphores:
            self.nc.gpsimd.sem_inc(s, 1)
        self.nc.all_engine_barrier()

    def __exit__(self, *exc):
        super().__exit__(*exc)
        self.nc.clear_and_free_semaphores(self.semaphores + self.from_zero)


class Pair:

    def __init__(self, ctx, nc, name, shape):
        self.hi = ctx.enter_context(nc.sbuf_tensor(name + "_hi", shape, F32R))
        self.lo = ctx.enter_context(nc.sbuf_tensor(name + "_lo", shape, F32R))


def f32(ap):
    return ap.bitcast(F32)


def matmul3(pe, out, w, x, first, last):
    pe.matmul(out, w[1], x[0], start=first, stop=False)
    pe.matmul(out, w[0], x[1], start=False, stop=False)
    return pe.matmul(out, w[0], x[0], start=False, stop=last)


def part(pair, *index):
    return pair.hi[index], pair.lo[index]


class Flow:

    def __init__(self, ctx, nc, name):
        self.mm = ctx.semaphore(name + "_product")
        self.hi = ctx.semaphore(name + "_hi_written")
        self.lo = ctx.semaphore(name + "_lo_written")


def layernorm_stats(dve, ctx_sems, X, stats, mv, tiles):
    s_stats, s_mv = ctx_sems
    for t in range(tiles):
        dve.bn_stats(stats[:, t, :], X[:, t, :]).then_inc(s_stats, 1)
    for t in range(tiles):
        dve.wait_ge(s_stats, at(t + 1))
        dve.bn_aggr(mv[:, t, :], stats[:, t, :]).then_inc(s_mv, 1)


def attention0(nc, banks, X, eps, ident, x_dram, ctx_dram, ctxT_dram, w_dram, B, S):
    T = B * S // P
    QT = S // P
    KT = 2 * QT
    SCALE = float(D) ** -0.5
    with Phase(nc) as ctx:
        def sb(name, shape, dt=F32):
            return ctx.enter_context(nc.sbuf_tensor("a0_" + name, shape, dt))

        def sem(name):
            return ctx.semaphore("a0_" + name)

        def pair(name, shape):
            return Pair(ctx, nc, "a0_" + name, shape)

        def flow(name):
            return Flow(ctx, nc, "a0_" + name)

        W = [pair(n, [P, KD, D]) for n in ("wq", "wk", "wv", "wo")]
        wq, wk, wv, wo = W
        wraw = [sb(f"wraw{j}", [P, KD, D]) for j in range(2)]
        stats = sb("stats", [P, T, 6])
        mv = sb("mv", [P, T, 2])
        std = sb("std", [P, T])
        rstd = sb("rstd", [P, T])
        xn = sb("xn", [P, QT, D])
        xT = pair("xT", [P, KD, S])
        qT = pair("qT", [P, KD, S])
        kT = pair("kT", [P, KD, 2 * S])
        V = pair("V", [P, KT, D])
        cTraw = sb("cTraw", [P, KD, S])
        craw = sb("craw", [P, QT, D])
        probs = sb("probs", [P, QT, 2 * S])
        pT = pair("pT", [P, KT, S])
        oT = pair("oT", [P, KD, S])
        nmax = sb("nmax", [P, QT])
        den = sb("den", [P, QT])
        rden = sb("rden", [P, QT])
        bank = banks

        s_x = sem("x_loaded")
        s_w = [sem(f"w{j}_loaded") for j in range(4)]
        s_whi = sem("w_hi_written")
        s_wlo = sem("w_lo_written")
        s_stats, s_mv, s_std, s_rstd = sem("stats"), sem("mean_var"), sem("std"), sem("rstd")
        s_cT, s_c = sem("ctxT_loaded"), sem("ctx_loaded")
        s_cThi, s_cTlo = sem("ctxT_hi"), sem("ctxT_lo")
        s_chi, s_clo = sem("ctx_hi"), sem("ctx_lo")
        s_xn = sem("xn")
        tr, q, k, v, o, pt = (flow(n) for n in ("xT", "q", "k", "v", "o", "pT"))
        s_scores, s_nmax, s_exp, s_rden = sem("scores"), sem("nmax"), sem("exp"), sem("rden")
        s_proj, s_added = sem("projected"), sem("added")

        ctx.start()
        block = ctx.enter_context(nc.Block())

        @block.sync
        def _(sp):
            for j in (0, 1):
                sp.dma_start(wraw[j][:], w_dram[j]).then_inc(s_w[j], 16)
            sp.dma_start(X[:], x_dram).then_inc(s_x, 16)
            for j in (2, 3):
                sp.wait_ge(s_wlo, at(j - 1))
                sp.dma_start(wraw[j - 2][:], w_dram[j]).then_inc(s_w[j], 16)
            with sp.Fori(0, B) as i:
                sp.wait_ge(s_cTlo, at(i))
                sp.dma_start(cTraw[:], ctxT_dram[:, :, bass.ds(i * S, S)]).then_inc(s_cT, 16)
                sp.wait_ge(s_clo, at(i))
                sp.dma_start(craw[:], ctx_dram[:, bass.ds(i * QT, QT), :]).then_inc(s_c, 16)

        @block.gpsimd
        def _(pool):
            with pool.Fori(0, B) as i:
                pool.wait_ge(s_cThi, at(i + 1))
                pool.tensor_tensor(kT.lo[:, :, 0:S], cTraw[:], f32(kT.hi[:, :, 0:S]), ALU.subtract).then_inc(s_cTlo, 1)
                pool.wait_ge(s_chi, at(i + 1))
                pool.tensor_tensor(V.lo[:, 0:QT, :], craw[:], f32(V.hi[:, 0:QT, :]), ALU.subtract).then_inc(s_clo, 1)

        @block.scalar
        def _(act):
            for j in range(4):
                act.wait_ge(s_w[j], at(16))
                act.activation(W[j].hi[:], wraw[j % 2][:], ACT.Copy).then_inc(s_whi, 1)
                if j == 0:
                    act.wait_ge(s_mv, at(T))
                    act.activation(std[:], mv[:, :, 1], ACT.Sqrt, bias=eps[:]).then_inc(s_std, 1)
            with act.Fori(0, B) as i:
                act.wait_ge(s_cT, at(i * 16 + 16))
                act.activation(kT.hi[:, :, 0:S], cTraw[:], ACT.Copy).then_inc(s_cThi, 1)
                act.wait_ge(s_c, at(i * 16 + 16))
                act.activation(V.hi[:, 0:QT, :], craw[:], ACT.Copy).then_inc(s_chi, 1)
                for t in range(QT):
                    act.wait_ge(tr.mm, at(i * QT + t + 1))
                    act.activation(xT.hi[:, :, t * P:(t + 1) * P],
                                   bank[t][:].rearrange("p (k s) -> p k s", k=KD), ACT.Copy).then_inc(tr.hi, 1)
                for n, (f, dst, b0, scale) in enumerate(((q, qT.hi, 2, SCALE), (k, kT.hi, 4, 1.0))):
                    for m in range(2):
                        act.wait_ge(f.mm, at(i * 2 + m + 1))
                        dd = dst[:, 2 * m:2 * m + 2, 0:S] if n == 0 else dst[:, 2 * m:2 * m + 2, S:2 * S]
                        act.activation(dd, bank[b0 + m][:].rearrange("p (k s) -> p k s", k=2), ACT.Copy,
                                       scale=scale).then_inc(f.hi, 1)
                for t in range(QT):
                    act.wait_ge(v.mm, at(i * QT + t + 1))
                    act.activation(V.hi[:, QT + t, :], bank[6 + t][:], ACT.Copy).then_inc(v.hi, 1)
                for t in range(QT):
                    act.wait_ge(s_nmax, at(i * QT + t + 1))
                    act.activation(probs[:, t, :], bank[t][:], ACT.Exp, bias=nmax[:, t:t + 1],
                                   accum_out=den[:, t:t + 1]).then_inc(s_exp, 1)
                for t in range(QT):
                    act.wait_ge(pt.mm, at(i * QT + t + 1))
                    act.activation(pT.hi[:, :, t * P:(t + 1) * P],
                                   bank[2 + t][:].rearrange("p (k s) -> p k s", k=KT), ACT.Copy).then_inc(pt.hi, 1)
                for m in range(2):
                    act.wait_ge(o.mm, at(i * 2 + m + 1))
                    if m == 0:
                        act.wait_ge(s_proj, at(i * QT))
                    act.activation(oT.hi[:, 2 * m:2 * m + 2, :],
                                   bank[4 + m][:].rearrange("p (k s) -> p k s", k=2), ACT.Copy).then_inc(o.hi, 1)

        @block.vector
        def _(dve):
            dve.wait_ge(s_x, at(16))
            layernorm_stats(dve, (s_stats, s_mv), X, stats, mv, T)
            dve.wait_ge(s_std, at(1))
            dve.reciprocal(rstd[:], std[:]).then_inc(s_rstd, 1)
            for j in range(4):
                dve.wait_ge(s_whi, at(j + 1))
                dve.tensor_tensor(W[j].lo[:], wraw[j % 2][:], f32(W[j].hi[:]), ALU.subtract).then_inc(s_wlo, 1)
            dve.wait_ge(s_rstd, at(1))
            with dve.Fori(0, B) as i:
                for t in range(QT):
                    dve.tensor_scalar(xn[:, t, :], X[:, bass.ds(i * QT + t, 1), :], mv[:, bass.ds(i * QT + t, 1), 0],
                                      rstd[:, bass.ds(i * QT + t, 1)], ALU.subtract, ALU.mult).then_inc(s_xn, 1)
                for t in range(QT):
                    dve.wait_ge(tr.hi, at(i * QT + t + 1))
                    dst = slice(t * P, (t + 1) * P)
                    dve.tensor_tensor(xT.lo[:, :, dst], bank[t][:].rearrange("p (k s) -> p k s", k=KD),
                                      f32(xT.hi[:, :, dst]), ALU.subtract).then_inc(tr.lo, 1)
                for n, (f, dst, b0, scale) in enumerate(((q, qT, 2, SCALE), (k, kT, 4, 1.0))):
                    for m in range(2):
                        dve.wait_ge(f.hi, at(i * 2 + m + 1))
                        cols = slice(0, S) if n == 0 else slice(S, 2 * S)
                        dve.scalar_tensor_tensor(dst.lo[:, 2 * m:2 * m + 2, cols],
                                                 bank[b0 + m][:].rearrange("p (k s) -> p k s", k=2), scale,
                                                 f32(dst.hi[:, 2 * m:2 * m + 2, cols]), ALU.mult,
                                                 ALU.subtract).then_inc(f.lo, 1)
                for t in range(QT):
                    dve.wait_ge(v.hi, at(i * QT + t + 1))
                    dve.tensor_tensor(V.lo[:, QT + t, :], bank[6 + t][:], f32(V.hi[:, QT + t, :]),
                                      ALU.subtract).then_inc(v.lo, 1)
                for t in range(QT):
                    dve.wait_ge(s_scores, at(i * QT + t + 1))
                    dve.tensor_reduce(nmax[:, t:t + 1], bank[t][:], AX.X, ALU.max, negate=True).then_inc(s_nmax, 1)
                for t in range(QT):
                    dve.wait_ge(s_exp, at(i * QT + t + 1))
                    dve.reciprocal(rden[:, t:t + 1], den[:, t:t + 1]).then_inc(s_rden, 1)
                for t in range(QT):
                    dve.wait_ge(pt.hi, at(i * QT + t + 1))
                    dst = slice(t * P, (t + 1) * P)
                    dve.tensor_tensor(pT.lo[:, :, dst], bank[2 + t][:].rearrange("p (k s) -> p k s", k=KT),
                                      f32(pT.hi[:, :, dst]), ALU.subtract).then_inc(pt.lo, 1)
                for m in range(2):
                    dve.wait_ge(o.hi, at(i * 2 + m + 1))
                    dve.tensor_tensor(oT.lo[:, 2 * m:2 * m + 2, :],
                                      bank[4 + m][:].rearrange("p (k s) -> p k s", k=2),
                                      f32(oT.hi[:, 2 * m:2 * m + 2, :]), ALU.subtract).then_inc(o.lo, 1)
                for t in range(QT):
                    dve.wait_ge(s_proj, at(i * QT + t + 1))
                    dve.wait_ge(s_rden, at(i * QT + t + 1))
                    row = X[:, bass.ds(i * QT + t, 1), :]
                    dve.scalar_tensor_tensor(row, bank[6 + t][:].rearrange("p (a n) -> p a n", a=1),
                                             rden[:, t:t + 1], row, ALU.mult, ALU.add).then_inc(s_added, 1)

        @block.tensor
        def _(pe):
            with pe.Fori(0, B) as i:
                for t in range(QT):
                    pe.wait_ge(s_xn, at(i * QT + t + 1))
                    for c in range(KD):
                        last = pe.transpose(bank[t][:, c * P:(c + 1) * P], xn[:, t, c * P:(c + 1) * P], ident[:])
                    last.then_inc(tr.mm, 1)
                pe.wait_ge(tr.lo, at(i * QT + QT))
                for n, (f, w, b0) in enumerate(((q, wq, 2), (k, wk, 4))):
                    pe.wait_ge(s_wlo, at(n + 1))
                    for m in range(2):
                        for h in range(2):
                            e = 2 * m + h
                            for c in range(KD):
                                last = matmul3(pe, bank[b0 + m][:, h * S:(h + 1) * S],
                                               part(w, slice(None), c, slice(e * P, (e + 1) * P)),
                                               part(xT, slice(None), c), c == 0, c == KD - 1)
                        last.then_inc(f.mm, 1)
                pe.wait_ge(s_wlo, at(3))
                pe.wait_ge(s_added, at(i * QT))
                for t in range(QT):
                    for c in range(KD):
                        last = matmul3(pe, bank[6 + t][:], part(xT, slice(None), c, slice(t * P, (t + 1) * P)),
                                       part(wv, slice(None), c), c == 0, c == KD - 1)
                    last.then_inc(v.mm, 1)
                pe.wait_ge(q.lo, at(i * 2 + 2))
                pe.wait_ge(k.lo, at(i * 2 + 2))
                pe.wait_ge(s_cTlo, at(i + 1))
                for t in range(QT):
                    for c in range(KD):
                        last = matmul3(pe, bank[t][:], part(qT, slice(None), c, slice(t * P, (t + 1) * P)),
                                       part(kT, slice(None), c), c == 0, c == KD - 1)
                    last.then_inc(s_scores, 1)
                for t in range(QT):
                    pe.wait_ge(s_exp, at(i * QT + t + 1))
                    for c in range(KT):
                        last = pe.transpose(bank[2 + t][:, c * P:(c + 1) * P], probs[:, t, c * P:(c + 1) * P],
                                            ident[:])
                    last.then_inc(pt.mm, 1)
                pe.wait_ge(pt.lo, at(i * QT + QT))
                pe.wait_ge(v.lo, at(i * QT + QT))
                pe.wait_ge(s_clo, at(i + 1))
                for m in range(2):
                    for h in range(2):
                        e = 2 * m + h
                        for c in range(KT):
                            last = matmul3(pe, bank[4 + m][:, h * S:(h + 1) * S],
                                           part(V, slice(None), c, slice(e * P, (e + 1) * P)),
                                           part(pT, slice(None), c), c == 0, c == KT - 1)
                    last.then_inc(o.mm, 1)
                pe.wait_ge(o.lo, at(i * 2 + 2))
                pe.wait_ge(s_wlo, at(4))
                for t in range(QT):
                    for c in range(KD):
                        last = matmul3(pe, bank[6 + t][:], part(oT, slice(None), c, slice(t * P, (t + 1) * P)),
                                       part(wo, slice(None), c), c == 0, c == KD - 1)
                    last.then_inc(s_proj, 1)


def bitlinear_weights(nc, banks, eps, ones, w_dram, wq, gamma):
    N = 3
    FR = w_dram[0].shape[1] * w_dram[0].shape[2]
    CH = 4
    C = FR // CH
    with Phase(nc) as ctx:
        def sb(name, shape, dt=F32):
            return ctx.enter_context(nc.sbuf_tensor("bw_" + name, shape, dt))

        def sem(name):
            return ctx.semaphore("bw_" + name)

        raw = [sb(f"raw{j}", [P, FR]) for j in range(N)]
        junk = sb("junk", [P, FR], BF16)
        magic = sb("magic", [P, 1])
        asum = sb("asum", [P, N])
        rgamma = sb("rgamma", [P, N])
        tot = banks[0]
        s_raw = [sem(f"raw{j}_loaded") for j in range(N)]
        s_magic, s_asum, s_tot, s_g, s_rg = (sem(n) for n in ("magic", "abs_sum", "total", "gamma", "rgamma"))
        s_sc, s_min, s_done = sem("scaled"), sem("min"), sem("ternary")
        ctx.start()
        block = ctx.enter_context(nc.Block())

        @block.sync
        def _(sp):
            for j in range(N):
                sp.dma_start(raw[j][:].rearrange("p (k n) -> p k n", k=w_dram[j].shape[1]),
                             w_dram[j]).then_inc(s_raw[j], 16)

        @block.scalar
        def _(act):
            for j in range(N):
                act.wait_ge(s_raw[j], at(16))
                if j:
                    act.wait_ge(s_asum, at(j))
                act.activation(junk[:], raw[j][:], ACT.Abs, accum_out=asum[:, j:j + 1]).then_inc(s_asum, 1)

        @block.tensor
        def _(pe):
            for j in range(N):
                pe.wait_ge(s_asum, at(j + 1))
                pe.wait_ge(s_g, at(j))
                pe.matmul(tot[:, j:j + 1], ones[:], asum[:, j:j + 1], start=True, stop=True).then_inc(s_tot, 1)

        @block.gpsimd
        def _(pool):
            pass

        @block.vector
        def _(dve):
            n = 0
            for j in range(N):
                dve.wait_ge(s_tot, at(j + 1))
                dve.tensor_scalar(gamma[:, j:j + 1], tot[:, j:j + 1], 1.0 / (P * FR), 1e-5, ALU.mult,
                                  ALU.max).then_inc(s_g, 1)
                dve.wait_ge(s_g, at(j + 1))
                dve.reciprocal(rgamma[:, j:j + 1], gamma[:, j:j + 1]).then_inc(s_rg, 1)
                dve.wait_ge(s_rg, at(j + 1))
                w = wq[j][:].rearrange("p k n -> p (k n)")
                dve.tensor_scalar(raw[j][:], raw[j][:], rgamma[:, j:j + 1], ROUND, ALU.mult, ALU.add).then_inc(s_sc, 1)
                dve.wait_ge(s_sc, at(j + 1))
                dve.tensor_scalar(w, raw[j][:], ROUND, 1.0, ALU.subtract, ALU.min).then_inc(s_min, 1)
                dve.wait_ge(s_min, at(j + 1))
                dve.tensor_scalar(w, w, -1.0, None, ALU.max).then_inc(s_done, 1)


def ffn0(nc, banks, X, eps, ident, ones, w_dram, b_dram, T):
    H = w_dram[0].shape[2]
    NH = H // 512
    KH = H // P
    with Phase(nc) as ctx:
        def sb(name, shape, dt=F32):
            return ctx.enter_context(nc.sbuf_tensor("f0_" + name, shape, dt))

        def sem(name):
            return ctx.semaphore("f0_" + name)

        wg, wv = (sb(n, [P, KD, H], BF16) for n in ("wg", "wv"))
        wo = sb("wo", [P, KH, D], BF16)
        gamma = sb("gamma", [P, 3])
        bitlinear_weights(nc, banks, eps, ones, w_dram, (wg, wv, wo), gamma)

        bg, bv = (sb(n, [P, H]) for n in ("bg", "bv"))
        bo = sb("bo", [P, D])
        identb = sb("identb", [P, P], BF16)
        stats = sb("stats", [P, T, 6])
        mv = sb("mv", [P, T, 2])
        std = sb("std", [P, T])
        rstd = sb("rstd", [P, T])
        xn = sb("xn", [P, D])
        xr = sb("xr", [P, D])
        xq = sb("xq", [P, D], BF16)
        xqT = sb("xqT", [P, KD, P], BF16)
        ax = sb("ax", [P, T])
        rx = sb("rx", [P, T])
        sx = sb("sx", [P, T])
        sg = sb("sg", [P, 2, T])
        g = sb("g", [P, 2, 512])
        gs = sb("gs", [P, 2, 512])
        vv = sb("vv", [P, 2, 512])
        h = sb("h", [P, H])
        hr = sb("hr", [P, H])
        hq = sb("hq", [P, H], BF16)
        hqT = sb("hqT", [P, KH, P], BF16)
        ah, rh, sh, so = (sb(n, [P, 1]) for n in ("ah", "rh", "sh", "so"))
        magic = sb("magic", [P, 1])
        gb, vb = banks[0:2], banks[2:4]
        hb = [b[:].bitcast(BF16) for b in banks[4:6]]
        xb, ob = banks[6][:].bitcast(BF16), banks[7]

        s_b = sem("biases_loaded")
        s_id = sem("constants")
        s_stats, s_mv, s_std, s_rstd = sem("stats"), sem("mean_var"), sem("std"), sem("rstd")
        s_xn, s_ax, s_axc, s_rx, s_sx, s_sgv, s_xr, s_xq = (sem(n) for n in (
            "xn", "absmax_x", "absmax_x_clipped", "rx", "sx", "sg", "x_rounded", "xq"))
        s_bo = sem("out_bias_added")
        s_xT, s_xTc = sem("xqT_product"), sem("xqT_copied")
        s_g, s_gb, s_gs, s_v, s_vb, s_h = (sem(n) for n in ("gate", "gate_biased", "silu", "val", "val_biased", "h"))
        s_ah, s_ahc, s_rh, s_sh, s_so, s_hr, s_hq = (sem(n) for n in (
            "absmax_h", "absmax_h_clipped", "rh", "sh", "so", "h_rounded", "hq"))
        s_hT, s_hTc, s_out, s_added = sem("hqT_product"), sem("hqT_copied"), sem("out"), sem("added")

        ctx.start()
        block = ctx.enter_context(nc.Block())

        @block.sync
        def _(sp):
            sp.dma_start(bg[:], b_dram[0].partition_broadcast(P)).then_inc(s_b, 16)
            sp.dma_start(bv[:], b_dram[1].partition_broadcast(P)).then_inc(s_b, 16)
            sp.dma_start(bo[:], b_dram[2].partition_broadcast(P)).then_inc(s_b, 16)

        @block.gpsimd
        def _(pool):
            pool.memset(magic[:], ROUND).then_inc(s_id, 1)
            pool.tensor_copy(identb[:], ident[:]).then_inc(s_id, 1)
            pool.wait_ge(s_b, at(48))

            def out_bias(t):
                pool.wait_ge(s_xn, at(t + 1))
                row = X[:, bass.ds(t, 1), :]
                pool.tensor_tensor(row, row, bo[:].rearrange("p (a n) -> p a n", a=1), ALU.add).then_inc(s_bo, 1)

            def hidden(t):
                for j in range(NH):
                    pool.wait_ge(s_vb, at(t * NH + j + 1))
                    pool.wait_ge(s_gs, at(t * NH + j + 1))
                    if j == 0:
                        pool.wait_ge(s_hr, at(t))
                    pool.tensor_tensor(h[:, j * 512:(j + 1) * 512], vv[:, j % 2, :], gs[:, j % 2, :],
                                       ALU.mult).then_inc(s_h, 1)

            out_bias(0)
            out_bias(1)
            hidden(0)
            with pool.Fori(0, T - 2) as t:
                out_bias(t + 2)
                hidden(t + 1)
            hidden(T - 1)

        @block.scalar
        def _(act):
            act.wait_ge(s_mv, at(T))
            act.activation(std[:], mv[:, :, 1], ACT.Sqrt, bias=eps[:]).then_inc(s_std, 1)
            act.wait_ge(s_id, at(2))

            def xT_copy(t):
                act.wait_ge(s_xT, at(t + 1))
                act.wait_ge(s_v, at(t * NH))
                act.activation(xqT[:], xb[:, 0:D].rearrange("p (k s) -> p k s", k=KD), ACT.Copy).then_inc(s_xTc, 1)

            def silu(t):
                for j in range(NH):
                    act.wait_ge(s_gb, at(t * NH + j + 1))
                    act.wait_ge(s_h, at(t * NH + max(j - 1, 0)))
                    act.activation(gs[:, j % 2, :], g[:, j % 2, :], ACT.Silu).then_inc(s_gs, 1)

            def h_round(t):
                act.wait_ge(s_sh, at(t + 1))
                act.wait_ge(s_hq, at(t))
                act.activation(hr[:], h[:], ACT.Identity, bias=magic[:], scale=sh[:]).then_inc(s_hr, 1)

            def hT_copy(t):
                for j in range(2):
                    act.wait_ge(s_hT, at(t * 2 + j + 1))
                    if j == 0:
                        act.wait_ge(s_out, at(t))
                    act.activation(hqT[:, 8 * j:8 * j + 8, :], hb[j][:].rearrange("p (k s) -> p k s", k=8),
                                   ACT.Copy).then_inc(s_hTc, 1)

            xT_copy(0)
            silu(0)
            xT_copy(1)
            h_round(0)
            with act.Fori(0, T - 2) as t:
                silu(t + 1)
                hT_copy(t)
                xT_copy(t + 2)
                h_round(t + 1)
            silu(T - 1)
            hT_copy(T - 2)
            h_round(T - 1)
            hT_copy(T - 1)

        @block.vector
        def _(dve):
            layernorm_stats(dve, (s_stats, s_mv), X, stats, mv, T)
            dve.wait_ge(s_std, at(1))
            dve.reciprocal(rstd[:], std[:]).then_inc(s_rstd, 1)
            dve.wait_ge(s_rstd, at(1))
            dve.wait_ge(s_b, at(48))

            def quantise_x(t):
                col = bass.ds(t, 1)
                dve.tensor_scalar(xn[:].rearrange("p (a n) -> p a n", a=1), X[:, col, :], mv[:, col, 0], rstd[:, col],
                                  ALU.subtract, ALU.mult).then_inc(s_xn, 1)
                dve.wait_ge(s_xn, at(t + 1))
                dve.tensor_reduce(ax[:, col], xn[:], AX.X, ALU.max, apply_absolute_value=True).then_inc(s_ax, 1)
                dve.wait_ge(s_ax, at(t + 1))
                dve.tensor_scalar(ax[:, col], ax[:, col], 1e-5, None, ALU.max).then_inc(s_axc, 1)
                dve.wait_ge(s_axc, at(t + 1))
                dve.reciprocal(rx[:, col], ax[:, col]).then_inc(s_rx, 1)
                for n in range(2):
                    dve.tensor_scalar(sg[:, n, col], ax[:, col], gamma[:, n:n + 1], 1.0 / 127, ALU.mult,
                                      ALU.mult).then_inc(s_sgv, 1)
                dve.wait_ge(s_rx, at(t + 1))
                dve.tensor_scalar(sx[:, col], rx[:, col], 127.0, None, ALU.mult).then_inc(s_sx, 1)
                dve.wait_ge(s_sx, at(t + 1))
                dve.tensor_scalar(xr[:], xn[:], sx[:, col], ROUND, ALU.mult, ALU.add).then_inc(s_xr, 1)
                dve.wait_ge(s_xr, at(t + 1))
                dve.wait_ge(s_xT, at(t))
                dve.tensor_scalar(xq[:], xr[:], ROUND, 127.0, ALU.subtract, ALU.min).then_inc(s_xq, 1)

            def hidden(t):
                dve.wait_ge(s_sgv, at(2 * t + 2))
                for j in range(NH):
                    cols = slice(j * 512, (j + 1) * 512)
                    for n, (s_in, src, dst, b, s_free, s_done) in enumerate(((s_g, gb, g, bg, s_gs, s_gb),
                                                                             (s_v, vb, vv, bv, s_h, s_vb))):
                        dve.wait_ge(s_in, at(t * NH + j + 1))
                        dve.wait_ge(s_free, at(t * NH + max(j - 1, 0)))
                        dve.scalar_tensor_tensor(dst[:, j % 2, :], src[j % 2][:], sg[:, n, bass.ds(t, 1)], b[:, cols],
                                                 ALU.mult, ALU.add).then_inc(s_done, 1)

            def quantise_h(t):
                dve.wait_ge(s_h, at(t * NH + NH))
                dve.tensor_reduce(ah[:], h[:], AX.X, ALU.max, apply_absolute_value=True).then_inc(s_ah, 1)
                dve.wait_ge(s_ah, at(t + 1))
                dve.tensor_scalar(ah[:], ah[:], 1e-5, None, ALU.max).then_inc(s_ahc, 1)
                dve.wait_ge(s_ahc, at(t + 1))
                dve.reciprocal(rh[:], ah[:]).then_inc(s_rh, 1)
                dve.wait_ge(s_rh, at(t + 1))
                dve.tensor_scalar(sh[:], rh[:], 127.0, None, ALU.mult).then_inc(s_sh, 1)

            def quantised_h(t):
                dve.wait_ge(s_hr, at(t + 1))
                dve.wait_ge(s_hT, at(2 * t))
                dve.tensor_scalar(hq[:], hr[:], ROUND, 127.0, ALU.subtract, ALU.min).then_inc(s_hq, 1)
                dve.wait_ge(s_added, at(t))
                dve.tensor_scalar(so[:], ah[:], gamma[:, 2:3], 1.0 / 127, ALU.mult, ALU.mult).then_inc(s_so, 1)

            def add(t):
                dve.wait_ge(s_out, at(t + 1))
                dve.wait_ge(s_bo, at(t + 1))
                dve.wait_ge(s_so, at(t + 1))
                row = X[:, bass.ds(t, 1), :]
                dve.scalar_tensor_tensor(row, ob[:].rearrange("p (a n) -> p a n", a=1), so[:], row, ALU.mult,
                                         ALU.add).then_inc(s_added, 1)

            quantise_x(0)
            quantise_x(1)
            hidden(0)
            quantise_h(0)
            quantised_h(0)
            with dve.Fori(0, T - 2) as t:
                quantise_x(t + 2)
                hidden(t + 1)
                quantise_h(t + 1)
                add(t)
                quantised_h(t + 1)
            hidden(T - 1)
            quantise_h(T - 1)
            add(T - 2)
            quantised_h(T - 1)
            add(T - 1)

        @block.tensor
        def _(pe):
            pe.wait_ge(s_id, at(2))

            def xT(t):
                pe.wait_ge(s_xq, at(t + 1))
                pe.wait_ge(s_xTc, at(t))
                for c in range(KD):
                    last = pe.transpose(xb[:, c * P:(c + 1) * P], xq[:, c * P:(c + 1) * P], identb[:])
                last.then_inc(s_xT, 1)

            def up(t):
                pe.wait_ge(s_xTc, at(t + 1))
                for j in range(NH):
                    for w, dst, s_free, s_done in ((wg, gb, s_gb, s_g), (wv, vb, s_vb, s_v)):
                        pe.wait_ge(s_free, at(t * NH + max(j - 1, 0)))
                        for c in range(KD):
                            last = pe.matmul(dst[j % 2][:], xqT[:, c, :], w[:, c, j * 512:(j + 1) * 512],
                                             start=c == 0, stop=c == KD - 1)
                        last.then_inc(s_done, 1)

            def hT(t):
                pe.wait_ge(s_hq, at(t + 1))
                for j in range(2):
                    pe.wait_ge(s_hTc, at(t * 2))
                    for c in range(8):
                        last = pe.transpose(hb[j][:, c * P:(c + 1) * P], hq[:, (8 * j + c) * P:(8 * j + c + 1) * P],
                                            identb[:])
                    last.then_inc(s_hT, 1)

            def down(t):
                pe.wait_ge(s_hTc, at(t * 2 + 2))
                pe.wait_ge(s_added, at(t))
                for c in range(KH):
                    last = pe.matmul(ob[:], hqT[:, c, :], wo[:, c, :], start=c == 0, stop=c == KH - 1)
                last.then_inc(s_out, 1)

            xT(0)
            up(0)
            xT(1)
            with pe.Fori(0, T - 2) as t:
                up(t + 1)
                hT(t)
                xT(t + 2)
                down(t)
            up(T - 1)
            hT(T - 2)
            down(T - 2)
            hT(T - 1)
            down(T - 1)


def keys_values1(nc, banks, X, eps, ident, ones, xT, ctxT_dram, wk_dram, wv_dram, bk_dram, bv_dram, qn_dram, kn_dram,
                 k_dram, v_dram, B, S, G):
    T = B * S // P
    QT = S // P
    HD = P
    RMS_EPS = 1e-6
    with Phase(nc) as ctx:
        def sb(name, shape, dt=F32):
            return ctx.enter_context(nc.sbuf_tensor("kv_" + name, shape, dt))

        def sem(name):
            return ctx.semaphore("kv_" + name)

        wk, wv = (Pair(ctx, nc, "kv_" + n, [P, KD, D]) for n in ("wk", "wv"))
        wraw = sb("wraw", [P, KD, D])
        bk = sb("bk", [P, D])
        qn, kn, wn = (sb(n, [P, 1]) for n in ("qn", "kn", "wn"))
        bv = sb("bv", [P, D])
        stats = sb("stats", [P, T, 6])
        mv = sb("mv", [P, T, 2])
        std, rstd = sb("std", [P, T]), sb("rstd", [P, T])
        xn = sb("xn", [P, QT, D])
        cTraw = [sb(f"cTraw{j}", [P, KD, S]) for j in range(2)]
        cT = [Pair(ctx, nc, f"kv_cT{j}", [P, KD, S]) for j in range(2)]
        kf = sb("kf", [P, QT, G, HD])
        junk = sb("junk", [P, HD])
        eps_rms = sb("eps_rms", [P, 1])
        ksum, krms, rk = (sb(n, [P, QT * G]) for n in ("ksum", "krms", "rk"))
        vf = sb("vf", [P, QT, D])
        K = Pair(ctx, nc, "kv_K", [P, G, S])
        V = Pair(ctx, nc, "kv_V", [P, QT, D])
        tb, kb, ktb, vb = banks[0:2], banks[2:4], banks[4:6], banks[6:8]

        s_const = sem("constants")
        s_small, s_w, s_whi, s_wlo, s_wn = (sem(n) for n in ("small_loaded", "w_loaded", "w_hi", "w_lo", "norm_weight"))
        s_stats, s_mv, s_std, s_rstd = sem("stats"), sem("mean_var"), sem("std"), sem("rstd")
        s_c, s_chi, s_clo = [sem(f"ctxT{j}_loaded") for j in range(2)], sem("ctxT_hi"), sem("ctxT_lo")
        s_xn = sem("xn")
        tr = Flow(ctx, nc, "kv_xT")
        s_k, s_kf, s_ksq, s_krms, s_rk, s_kn, s_kt = (sem(n) for n in (
            "k_product", "k_biased", "k_squares_summed", "k_rms", "k_rrms", "k_normed", "k_transposed"))
        s_khi, s_klo, s_v, s_vf, s_vhi, s_vlo = (sem(n) for n in ("k_hi", "k_lo", "v_product", "v_biased", "v_hi", "v_lo"))
        s_kst, s_vst = (ctx.queue_semaphore("kv_" + n) for n in ("k_stored", "v_stored"))
        s_stored = sem("stored")
        ctx.start()
        block = ctx.enter_context(nc.Block())

        @block.sync
        def _(sp):
            def context(i, j):
                sp.dma_start(cTraw[j][:], ctxT_dram[:, :, bass.ds(i * S, S)]).then_inc(s_c[j], 16)

            context(0, 0)
            sp.dma_start(wraw[:], wk_dram).then_inc(s_w, 16)
            sp.dma_start(bk[:], bk_dram.partition_broadcast(P)).then_inc(s_small, 16)
            sp.dma_start(qn[:], qn_dram).then_inc(s_small, 16)
            sp.dma_start(kn[:], kn_dram).then_inc(s_small, 16)
            sp.dma_start(bv[:], bv_dram.partition_broadcast(P)).then_inc(s_small, 16)
            context(1, 1)
            sp.wait_ge(s_wlo, at(1))
            sp.dma_start(wraw[:], wv_dram).then_inc(s_w, 16)
            with sp.Fori(0, B // 2 - 1) as p:
                for j in range(2):
                    sp.wait_ge(s_clo, at(p * 2 + j + 1))
                    context(p * 2 + j + 2, j)

        @block.gpsimd
        def _(pool):
            pool.wait_ge(s_chi, at(1))
            pool.tensor_tensor(cT[0].lo[:], cTraw[0][:], f32(cT[0].hi[:]), ALU.subtract).then_inc(s_clo, 1)
            for j, w in enumerate((wk, wv)):
                pool.wait_ge(s_whi, at(j + 1))
                pool.tensor_tensor(w.lo[:], wraw[:], f32(w.hi[:]), ALU.subtract).then_inc(s_wlo, 1)
            pool.memset(eps_rms[:], RMS_EPS).then_inc(s_const, 1)
            with pool.Fori(0, B) as i:
                pool.wait_ge(s_vlo, at(i + 1))
                for n, t in enumerate((V.hi, V.lo)):
                    pool.dma_start(v_dram[n][:, bass.ds(i * QT, QT), :], f32(t[:])).then_inc(s_vst, 16)
                pool.wait_ge(s_klo, at(i * 2 + 2))
                for n, t in enumerate((K.hi, K.lo)):
                    pool.dma_start(k_dram[n][:, :, bass.ds(i * S, S)], f32(t[:])).then_inc(s_kst, 16)
                pool.wait_ge(s_vst, i * 32 + 32)
                pool.wait_ge(s_kst, i * 32 + 32)
                pool.sem_inc(s_stored, 1)

        @block.scalar
        def _(act):
            def context(i, j):
                act.wait_ge(s_c[j], at((i - j) * 8 + 16))
                act.activation(cT[j].hi[:], cTraw[j][:], ACT.Copy).then_inc(s_chi, 1)

            def batch(i, j, more):
                if more:
                    act.wait_ge(s_v, at(i * QT))
                    context(i + 1, 1 - j)
                for t in range(QT):
                    act.wait_ge(s_kf, at(i * QT + t + 1))
                    for g in range(G):
                        n = t * G + g
                        act.wait_ge(s_ksq, at(i * QT * G + n))
                        act.activation(junk[:], kf[:, t, g, :], ACT.Square, accum_out=ksum[:, n:n + 1]).then_inc(s_ksq, 1)
                act.wait_ge(s_ksq, at((i + 1) * QT * G))
                act.activation(krms[:], ksum[:], ACT.Sqrt, bias=eps_rms[:], scale=1.0 / HD).then_inc(s_krms, 1)
                for t in range(QT):
                    act.wait_ge(tr.mm, at(i * QT + t + 1))
                    act.activation(xT.hi[:, :, bass.ds(i * S + t * P, P)], tb[t][:].rearrange("p (k s) -> p k s", k=KD),
                                   ACT.Copy).then_inc(tr.hi, 1)
                act.wait_ge(s_vf, at(i * QT + QT))
                act.wait_ge(s_stored, at(i))
                act.activation(V.hi[:], vf[:], ACT.Copy).then_inc(s_vhi, 1)
                for m in range(2):
                    act.wait_ge(s_kt, at(i * 2 + m + 1))
                    act.activation(K.hi[:, 2 * m:2 * m + 2, :], ktb[m][:].rearrange("p (g s) -> p g s", g=2), ACT.Copy,
                                   scale=wn[:]).then_inc(s_khi, 1)

            context(0, 0)
            for j, w in enumerate((wk, wv)):
                act.wait_ge(s_w, at(16 * (j + 1)))
                act.activation(w.hi[:], wraw[:], ACT.Copy).then_inc(s_whi, 1)
                if j == 0:
                    act.wait_ge(s_mv, at(T))
                    act.activation(std[:], mv[:, :, 1], ACT.Sqrt, bias=eps[:]).then_inc(s_std, 1)
            act.wait_ge(s_small, at(64))
            act.wait_ge(s_const, at(1))
            act.wait_ge(s_wn, at(1))
            with act.Fori(0, B // 2 - 1) as p:
                for j in range(2):
                    batch(p * 2 + j, j, True)
            batch(B - 2, 0, True)
            batch(B - 1, 1, False)

        @block.vector
        def _(dve):
            def batch(i, j, more):
                if more:
                    dve.wait_ge(s_chi, at(i + 2))
                    dve.tensor_tensor(cT[1 - j].lo[:], cTraw[1 - j][:], f32(cT[1 - j].hi[:]),
                                      ALU.subtract).then_inc(s_clo, 1)
                for t in range(QT):
                    col = bass.ds(i * QT + t, 1)
                    dve.tensor_scalar(xn[:, t:t + 1, :], X[:, col, :], mv[:, col, 0], rstd[:, col],
                                      ALU.subtract, ALU.mult).then_inc(s_xn, 1)
                for t in range(QT):
                    dve.wait_ge(s_k, at(i * QT + t + 1))
                    dve.wait_ge(s_kt, at(i * 2))
                    dve.tensor_tensor(kf[:, t, :, :].rearrange("p g n -> p (g n)"), kb[t][:], bk[:], ALU.add).then_inc(s_kf, 1)
                for t in range(QT):
                    dve.wait_ge(tr.hi, at(i * QT + t + 1))
                    cols = bass.ds(i * S + t * P, P)
                    dve.tensor_tensor(xT.lo[:, :, cols], tb[t][:].rearrange("p (k s) -> p k s", k=KD),
                                      f32(xT.hi[:, :, cols]), ALU.subtract).then_inc(tr.lo, 1)
                dve.wait_ge(s_krms, at(i + 1))
                dve.reciprocal(rk[:], krms[:]).then_inc(s_rk, 1)
                dve.wait_ge(s_rk, at(i + 1))
                k2 = kf[:].rearrange("p t g n -> p (t g) n")
                dve.tensor_tensor(k2, k2, rk[:].unsqueeze(2).broadcast_to([P, QT * G, HD]), ALU.mult).then_inc(s_kn, 1)
                for t in range(QT):
                    dve.wait_ge(s_v, at(i * QT + t + 1))
                    dve.wait_ge(s_vlo, at(i))
                    dve.tensor_tensor(vf[:, t, :], vb[t][:], bv[:], ALU.add).then_inc(s_vf, 1)

            def finish(i):
                dve.wait_ge(s_vhi, at(i + 1))
                dve.wait_ge(s_stored, at(i))
                dve.tensor_tensor(V.lo[:], vf[:], f32(V.hi[:]), ALU.subtract).then_inc(s_vlo, 1)
                for m in range(2):
                    dve.wait_ge(s_khi, at(i * 2 + m + 1))
                    half = slice(2 * m, 2 * m + 2)
                    dve.scalar_tensor_tensor(K.lo[:, half, :], ktb[m][:].rearrange("p (g s) -> p g s", g=2), wn[:],
                                             f32(K.hi[:, half, :]), ALU.mult, ALU.subtract).then_inc(s_klo, 1)

            layernorm_stats(dve, (s_stats, s_mv), X, stats, mv, T)
            dve.wait_ge(s_std, at(1))
            dve.reciprocal(rstd[:], std[:]).then_inc(s_rstd, 1)
            dve.wait_ge(s_rstd, at(1))
            dve.wait_ge(s_small, at(64))
            dve.tensor_tensor(wn[:], qn[:], kn[:], ALU.mult).then_inc(s_wn, 1)
            batch(0, 0, True)
            with dve.Fori(0, B // 2 - 1) as p:
                for j in range(2):
                    finish(p * 2 + j)
                    batch(p * 2 + j + 1, 1 - j, True)
            finish(B - 2)
            batch(B - 1, 1, False)
            finish(B - 1)

        @block.tensor
        def _(pe):
            def batch(i, j, first=False):
                c = cT[j]
                pe.wait_ge(s_clo, at(i + 1))
                if first:
                    pe.wait_ge(s_wlo, at(1))
                for t in range(QT):
                    pe.wait_ge(s_kf, at(i * QT))
                    for k in range(KD):
                        last = matmul3(pe, kb[t][:], part(c, slice(None), k, slice(t * P, (t + 1) * P)),
                                       part(wk, slice(None), k), k == 0, k == KD - 1)
                    last.then_inc(s_k, 1)
                for t in range(QT):
                    pe.wait_ge(s_xn, at(i * QT + t + 1))
                    pe.wait_ge(tr.lo, at(i * QT))
                    for k in range(KD):
                        last = pe.transpose(tb[t][:, k * P:(k + 1) * P], xn[:, t, k * P:(k + 1) * P], ident[:])
                    last.then_inc(tr.mm, 1)
                if first:
                    pe.wait_ge(s_wlo, at(2))
                for t in range(QT):
                    pe.wait_ge(s_vf, at(i * QT))
                    for k in range(KD):
                        last = matmul3(pe, vb[t][:], part(c, slice(None), k, slice(t * P, (t + 1) * P)),
                                       part(wv, slice(None), k), k == 0, k == KD - 1)
                    last.then_inc(s_v, 1)
                pe.wait_ge(s_kn, at(i + 1))
                pe.wait_ge(s_klo, at(i * 2))
                for m in range(2):
                    for g in range(2):
                        for t in range(QT):
                            last = pe.transpose(ktb[m][:, g * S + t * P:g * S + (t + 1) * P], kf[:, t, 2 * m + g, :], ident[:])
                    last.then_inc(s_kt, 1)

            batch(0, 0, True)
            batch(1, 1)
            with pe.Fori(1, B // 2) as p:
                for j in range(2):
                    batch(p * 2 + j, j)


def attention1(nc, banks, X, ident, ones, xT, mask_dram, wq_dram, wo_dram, bq_dram, k_dram, v_dram, B, S, G):
    QT = S // P
    NB = 2
    C = NB * S
    NC = B // NB
    HG = 4
    CT = C // P
    U = NC * HG
    HD = P
    RMS_EPS = 1e-6
    with Phase(nc) as ctx:
        def sb(name, shape, dt=F32):
            return ctx.enter_context(nc.sbuf_tensor("a1_" + name, shape, dt))

        def sem(name):
            return ctx.semaphore("a1_" + name)

        def pair(name, shape):
            return Pair(ctx, nc, "a1_" + name, shape)

        wq, wo = pair("wq", [P, KD, HG * HD]), pair("wo", [P, HG, D])
        wraw = sb("wraw", [P, KD, D])
        bq = sb("bq", [P, G * HG])
        bqg = sb("bqg", [P, HG])
        mask = sb("mask", [P, QT, S])
        q = [pair(f"q{j}", [P, C]) for j in range(2)]
        sq = [sb(f"sq{j}", [P, C]) for j in range(2)]
        K = [pair(f"K{j}", [P, C]) for j in range(2)]
        V = [pair(f"V{j}", [P, CT, HD]) for j in range(2)]
        sc = [sb(f"scores{j}", [P, CT, S]) for j in range(2)]
        pT = [pair(f"pT{b}", [P, QT, S]) for b in range(NB)]
        oT = pair("oT", [P, HG, C])
        ssq = sb("ssq", [P, HG, CT])
        mhalf = sb("mhalf", [P, CT])
        rq = sb("rq", [P, HG, CT])
        nmax, den, rden = (sb(n, [P, 2, CT]) for n in ("nmax", "den", "rden"))
        qb, scb, ptb, ob, ssb = banks[0:2], banks[2:4], banks[4:6], banks[6], banks[7]

        s_small, s_const, s_bqg = sem("small_loaded"), sem("constants"), sem("group_bias")
        s_wload = ctx.queue_semaphore("a1_w_loaded")
        s_wqhi, s_wqlo, s_wohi, s_wolo = sem("wq_hi"), sem("wq_lo"), sem("wo_hi"), sem("wo_lo")
        s_k, s_v = ([sem(f"{n}{j}_loaded") for j in range(2)] for n in "KV")
        fq, ft, fo = (Flow(ctx, nc, "a1_" + n) for n in ("q", "pT", "oT"))
        s_sq, s_ssq, s_ssqc, s_rq = sem("q_squared"), sem("q_sum"), sem("q_sum_copied"), sem("q_rstd")
        s_sc, s_masked, s_nmax, s_exp, s_rden, s_p = (sem(n) for n in (
            "scores", "masked", "nmax", "exp", "rden", "probs"))
        s_out, s_added = sem("out"), sem("added")
        ctx.start()
        block = ctx.enter_context(nc.Block())


        @block.sync
        def _(sp):
            sp.dma_start(bq[:], bq_dram).then_inc(s_small, 16)
            sp.dma_start(mask[:], mask_dram).then_inc(s_small, 16)

            def load(g, c, wait=None):
                cols = slice(c * C, (c + 1) * C)
                if wait is not None:
                    sp.wait_ge(s_sc, at(wait))
                    sp.wait_ge(s_small, at(32))
                for m, t in enumerate((K[c % 2].hi, K[c % 2].lo)):
                    sp.dma_start(f32(t[:]).rearrange("p (a n) -> p a n", a=1), k_dram[m][:, bass.ds(g, 1), cols]).then_inc(s_k[c % 2], 16)
                if wait is not None:
                    sp.wait_ge(fo.mm, at(wait))
                    sp.wait_ge(s_small, at(32))
                for m, t in enumerate((V[c % 2].hi, V[c % 2].lo)):
                    sp.dma_start(f32(t[:]), v_dram[m][:, c * CT:(c + 1) * CT, bass.ds(g * HD, HD)]).then_inc(s_v[c % 2], 16)

            load(0, 0)

            def group(g, more):
                for c in range(NC):
                    last = c == NC - 1
                    if not last or more:
                        load(g + 1 if last else g, (c + 1) % NC, (g * NC + c) * HG)

            with sp.Fori(0, G - 1) as g:
                group(g, True)
            group(G - 1, False)

        @block.gpsimd
        def _(pool):
            pool.dma_start(wraw[:], wq_dram[:, :, 0:HG * HD]).then_inc(s_wload, 16)
            pool.memset(mhalf[:], -0.5).then_inc(s_const, 1)
            pool.wait_ge(s_const, at(1))

            def rstd(u, h):
                pool.wait_ge(s_ssqc, at(u + 1))
                pool.tensor_tensor(rq[:, h % HG, :], ssq[:, h % HG, :], mhalf[:], ALU.pow).then_inc(s_rq, 1)

            def wq_lo(g):
                pool.wait_ge(s_wqhi, at(g + 1))
                pool.tensor_tensor(wq.lo[:], wraw[:], f32(wq.hi[:]), ALU.subtract).then_inc(s_wqlo, 1)
                pool.wait_ge(s_wqlo, at(g + 1))
                pool.dma_start(wraw[:], wo_dram[:, bass.ds(g * HG, HG), :]).then_inc(s_wload, 16)

            def wo_lo(g, more):
                pool.wait_ge(s_wohi, at(g + 1))
                pool.tensor_tensor(wo.lo[:], wraw[:], f32(wo.hi[:]), ALU.subtract).then_inc(s_wolo, 1)
                if more:
                    pool.wait_ge(s_wolo, at(g + 1))
                    pool.dma_start(wraw[:], wq_dram[:, :, bass.ds((g + 1) * HG * HD, HG * HD)]).then_inc(s_wload, 16)

            def group(g, more):
                for i in range(U):
                    if i + 2 < U or more:
                        rstd(g * U + i + 2, i + 2)
                    if i == 0:
                        wo_lo(g, more)
                    if i == U - 4 and more:
                        wq_lo(g + 1)

            wq_lo(0)
            rstd(0, 0)
            rstd(1, 1)
            with pool.Fori(0, G - 1) as g:
                group(g, True)
            group(G - 1, False)

        @block.scalar
        def _(act):
            def wq_hi(g):
                act.wait_ge(s_wload, g * 32 + 16)
                act.wait_ge(fq.mm, at(g * U))
                act.wait_ge(fq.lo, at(g * U))
                act.activation(wq.hi[:], wraw[:], ACT.Copy).then_inc(s_wqhi, 1)
                act.activation(bqg[:], bq[:, bass.ds(g * HG, HG)], ACT.Copy).then_inc(s_bqg, 1)

            def wo_hi(g):
                act.wait_ge(s_wload, g * 32 + 32)
                act.wait_ge(s_out, at(g * NC * CT))
                act.activation(wo.hi[:], wraw[:], ACT.Copy).then_inc(s_wohi, 1)

            def queries(u, g, i, first=False):
                act.wait_ge(fq.mm, at(u + 1))
                if not first:
                    act.wait_ge(s_ssq, at(u - 1))
                act.wait_ge(s_bqg, at(g + 1))
                b = bqg[:, i % HG:i % HG + 1]
                act.activation(sq[i % 2][:], qb[i % 2][:], ACT.Square, bias=b).then_inc(s_sq, 1)
                act.activation(q[i % 2].hi[:], qb[i % 2][:], ACT.Identity, bias=b).then_inc(fq.hi, 1)

            def exp(u, i):
                for t in range(CT):
                    act.wait_ge(s_nmax, at(u * NB + t // QT + 1))
                    row = sc[i % 2][:, t, :]
                    act.activation(row, row, ACT.Exp, bias=nmax[:, i % 2, t:t + 1],
                                   accum_out=den[:, i % 2, t:t + 1]).then_inc(s_exp, 1)

            def transposed(u):
                for b in range(NB):
                    act.wait_ge(ft.mm, at(u * NB + b + 1))
                    act.activation(pT[b].hi[:], ptb[b][:].rearrange("p (k s) -> p k s", k=QT), ACT.Copy).then_inc(ft.hi, 1)

            def output(u, n, i):
                act.wait_ge(fo.mm, at(u + 1))
                if i % HG == 0:
                    act.wait_ge(s_out, at(n * CT))
                act.activation(oT.hi[:, i % HG, :], ob[:], ACT.Copy).then_inc(fo.hi, 1)

            def group(g, more):
                for i in range(U):
                    u, n = g * U + i, g * NC + i // HG
                    transposed(u)
                    if i + 1 < U or more:
                        exp(u + 1, i + 1)
                    if i + 3 < U or more:
                        queries(u + 3, g + (i + 3) // U, i + 3)
                    if i == 0:
                        wo_hi(g)
                    if i == U - 4 and more:
                        wq_hi(g + 1)
                    output(u, n, i)

            act.wait_ge(s_small, at(32))
            wq_hi(0)
            queries(0, 0, 0, True)
            queries(1, 0, 1, True)
            exp(0, 0)
            queries(2, 0, 2)
            with act.Fori(0, G - 1) as g:
                group(g, True)
            group(G - 1, False)

        @block.vector
        def _(dve):
            def queries(u, i):
                dve.wait_ge(fq.hi, at(u + 1))
                dve.scalar_tensor_tensor(q[i % 2].lo[:], qb[i % 2][:], bqg[:, i % HG:i % HG + 1],
                                         f32(q[i % 2].hi[:]), ALU.add, ALU.subtract).then_inc(fq.lo, 1)

            def square_sums(u, i):
                dve.wait_ge(s_ssq, at(u + 1))
                dve.tensor_scalar(ssq[:, i % HG, :], ssb[:, 0:CT], HD * RMS_EPS, None, ALU.add).then_inc(s_ssqc, 1)

            def scores(u, i):
                dve.wait_ge(s_rq, at(u + 1))
                dve.wait_ge(s_sc, at(u + 1))
                for b in range(NB):
                    for t in range(QT):
                        r = b * QT + t
                        dve.scalar_tensor_tensor(sc[i % 2][:, r, :], scb[b][:, t * S:(t + 1) * S],
                                                 rq[:, i % HG, r:r + 1], mask[:, t, :], ALU.mult,
                                                 ALU.add).then_inc(s_masked, 1)

            def maxima(u, i):
                for b in range(NB):
                    dve.wait_ge(s_masked, at(u * CT + QT * (b + 1)))
                    dve.tensor_reduce(nmax[:, i % 2, b * QT:(b + 1) * QT], sc[i % 2][:, b * QT:(b + 1) * QT, :], AX.X,
                                      ALU.max, negate=True).then_inc(s_nmax, 1)

            def normalise(u, i):
                dve.wait_ge(s_exp, at(u * CT + CT))
                dve.reciprocal(rden[:, i % 2, :], den[:, i % 2, :]).then_inc(s_rden, 1)
                dve.wait_ge(s_rden, at(u + 1))
                for t in range(CT):
                    row = sc[i % 2][:, t, :]
                    dve.tensor_scalar(row, row, rden[:, i % 2, t:t + 1], None, ALU.mult).then_inc(s_p, 1)

            def transposed(u):
                for b in range(NB):
                    dve.wait_ge(ft.hi, at(u * NB + b + 1))
                    dve.tensor_tensor(pT[b].lo[:], ptb[b][:].rearrange("p (k s) -> p k s", k=QT), f32(pT[b].hi[:]),
                                      ALU.subtract).then_inc(ft.lo, 1)

            def output(u, i):
                dve.wait_ge(fo.hi, at(u + 1))
                dve.tensor_tensor(oT.lo[:, i % HG, :], ob[:], f32(oT.hi[:, i % HG, :]), ALU.subtract).then_inc(fo.lo, 1)

            def add(n, c):
                for t in range(CT):
                    dve.wait_ge(s_out, at(n * CT + t + 1))
                    row = X[:, c * CT + t, :]
                    dve.tensor_tensor(row, row, ptb[t % 2][:], ALU.add).then_inc(s_added, 1)

            def group(g, more):
                for i in range(U):
                    u, n = g * U + i, g * NC + i // HG
                    if i + 2 < U or more:
                        square_sums(u + 2, i + 2)
                    transposed(u)
                    if i + 1 < U or more:
                        normalise(u + 1, i + 1)
                    if i + 2 < U or more:
                        scores(u + 2, i + 2)
                    if i + 3 < U or more:
                        queries(u + 3, i + 3)
                    if i + 2 < U or more:
                        maxima(u + 2, i + 2)
                    output(u, i)
                    if i % HG == HG - 1:
                        add(n, i // HG)

            dve.wait_ge(s_small, at(32))
            queries(0, 0)
            queries(1, 1)
            square_sums(0, 0)
            scores(0, 0)
            maxima(0, 0)
            queries(2, 2)
            square_sums(1, 1)
            scores(1, 1)
            maxima(1, 1)
            normalise(0, 0)
            with dve.Fori(0, G - 1) as g:
                group(g, True)
            group(G - 1, False)

        @block.tensor
        def _(pe):
            def queries(u, g, i, first=False):
                c, h = i // HG % NC, i % HG
                if c == 0 and h == 0:
                    pe.wait_ge(s_wqlo, at(g + 1))
                if not first:
                    pe.wait_ge(fq.lo, at(u - 1))
                for k in range(KD):
                    last = matmul3(pe, qb[i % 2][:], part(wq, slice(None), k, slice(h * HD, (h + 1) * HD)),
                                   part(xT, slice(None), k, slice(c * C, (c + 1) * C)), k == 0, k == KD - 1)
                last.then_inc(fq.mm, 1)

            def square_sums(u, i):
                pe.wait_ge(s_sq, at(u + 1))
                pe.wait_ge(s_ssqc, at(u))
                for t in range(CT):
                    last = pe.matmul(ssb[:, t:t + 1], sq[i % 2][:, t * P:(t + 1) * P], ones[:, 0:1], start=True,
                                     stop=True)
                last.then_inc(s_ssq, 1)

            def scores(u, g, i):
                c = i // HG % NC
                pe.wait_ge(fq.lo, at(u + 1))
                pe.wait_ge(s_masked, at(u * CT))
                if i % HG == 0:
                    pe.wait_ge(s_k[c % 2], at((g * (NC // 2) + i // HG // 2) * 32 + 32))
                for b in range(NB):
                    for t in range(QT):
                        r = b * QT + t
                        last = matmul3(pe, scb[b][:, t * S:(t + 1) * S],
                                       part(q[i % 2], slice(None), slice(r * P, (r + 1) * P)),
                                       part(K[c % 2], slice(None), slice(b * S, (b + 1) * S)), True, True)
                last.then_inc(s_sc, 1)

            def transposed(u, n, i):
                if i % HG == 0:
                    pe.wait_ge(s_added, at(n * CT))
                for b in range(NB):
                    for t in range(QT):
                        r = b * QT + t
                        pe.wait_ge(s_p, at(u * CT + r + 1))
                        for k in range(QT):
                            last = pe.transpose(ptb[b][:, k * S + t * P:k * S + (t + 1) * P],
                                                sc[i % 2][:, r, k * P:(k + 1) * P], ident[:])
                    last.then_inc(ft.mm, 1)

            def output(u, g, i):
                v = V[i // HG % 2]
                if i % HG == 0:
                    pe.wait_ge(s_v[i // HG % 2], at((g * (NC // 2) + i // HG // 2) * 32 + 32))
                pe.wait_ge(fo.lo, at(u))
                for b in range(NB):
                    pe.wait_ge(ft.lo, at(u * NB + b + 1))
                    for k in range(QT):
                        last = matmul3(pe, ob[:, b * S:(b + 1) * S], part(v, slice(None), b * QT + k),
                                       part(pT[b], slice(None), k), k == 0, k == QT - 1)
                last.then_inc(fo.mm, 1)

            def project(u, n):
                pe.wait_ge(fo.lo, at(u))
                for t0 in range(0, CT, 2):
                    for heads in (range(HG - 1), range(HG - 1, HG)):
                        for t in (t0, t0 + 1):
                            if t0:
                                pe.wait_ge(s_added, at(n * CT + t - 1))
                            pe.wait_ge(fo.lo, at(u + (1 if HG - 1 in heads else 0)))
                            for k in heads:
                                last = matmul3(pe, ptb[t % 2][:], part(oT, slice(None), k, slice(t * P, (t + 1) * P)),
                                               part(wo, slice(None), k), k == 0, k == HG - 1)
                            if HG - 1 in heads:
                                last.then_inc(s_out, 1)

            def group(g, more):
                for i in range(U):
                    u, n = g * U + i, g * NC + i // HG
                    transposed(u, n, i)
                    if i + 2 < U or more:
                        square_sums(u + 2, i + 2)
                    if i + 3 < U or more:
                        queries(u + 3, g + (i + 3) // U, i + 3)
                    if i + 2 < U or more:
                        scores(u + 2, g, i + 2)
                    output(u, g, i)
                    if i % HG == HG - 1:
                        if i == HG - 1:
                            pe.wait_ge(s_wolo, at(g + 1))
                        project(u, n)

            queries(0, 0, 0, True)
            queries(1, 0, 1, True)
            square_sums(0, 0)
            scores(0, 0, 0)
            queries(2, 0, 2)
            square_sums(1, 1)
            scores(1, 0, 1)
            with pe.Fori(0, G - 1) as g:
                group(g, True)
            group(G - 1, False)


def router(nc, banks, X, eps, ident, ones, weight, slot, tile_expert, token, rw_dram, sdb_dram, xn_dram, table_dram, T, E,
           NT, TT):
    TOP = 2
    with Phase(nc) as ctx:
        def sb(name, shape, dt=F32):
            return ctx.enter_context(nc.sbuf_tensor("r_" + name, shape, dt))

        def sem(name):
            return ctx.semaphore("r_" + name)

        rw = sb("rw", [P, KD, E])
        sdb = sb("sdb", [P, D])
        stats = sb("stats", [P, T, 6])
        mv = sb("mv", [P, T, 2])
        std, rstd = sb("std", [P, T]), sb("rstd", [P, T])
        xn = [sb(f"xn{j}", [P, D]) for j in range(2)]
        xt = [sb(f"xt{j}", [P, KD, P]) for j in range(2)]
        position = sb("position", [P, T, TOP], U32)
        ids = sb("ids", [P, T], U32)
        zeros = sb("zeros", [P, NT * TT // P], U32)
        tiles = sb("tiles", [P, NT])
        before = sb("before", [P, P])
        cnt, scan0, scan1, base = (sb(n, [P, T, E]) for n in ("cnt", "scan0", "scan1", "base"))
        nt0, nt1, first = sb("nt0", [P, E]), sb("nt1", [P, E]), sb("first", [P, E])
        prod = sb("prod", [P, T, TOP, E])
        slotf, rowf, colf, posf = (sb(n, [P, T, TOP]) for n in ("slotf", "rowf", "colf", "posf"))
        le = sb("le", [P, NT, E])
        tef = sb("tef", [P, NT])
        logits = sb("logits", [P, T, E])
        nmax = sb("nmax", [P, T])
        ex = sb("ex", [P, T, E])
        top = sb("top", [P, T, 8])
        topi = sb("topi", [P, T, 8], U32)
        atf = sb("atf", [P, T, 8])
        expert = sb("expert", [P, E])
        hot = sb("hot", [P, T, TOP, E])
        tsum, rsum = sb("tsum", [P, T]), sb("rsum", [P, T])
        tb, lb = banks[0:2], banks[2:4]
        s_ld, s_const = sem("loaded"), sem("constants")
        s_stats, s_mv, s_std, s_rstd = sem("stats"), sem("mean_var"), sem("std"), sem("rstd")
        s_xn, s_bias, s_tr, s_xt, s_hi, s_lo = (sem(n) for n in ("xn", "bias_added", "transposed", "xt", "xT_hi", "xT_lo"))
        s_log, s_logc, s_nmax, s_sub, s_exp, s_top, s_at = (sem(n) for n in (
            "logits", "logits_copied", "nmax", "sub", "exp", "top", "at"))
        s_atf, s_sum, s_rsum, s_hot, s_comb = (sem(n) for n in ("atf", "sum", "rsum", "hot", "combine"))
        s_cnt, s_before, s_step, s_pos = (sem(n) for n in ("counted", "sums_before", "slot_steps", "positions"))
        s_xst = [sem(f"xn{j}_stored") for j in range(2)]
        s_zero, s_scat, s_tok = (ctx.queue_semaphore("r_" + n) for n in ("table_zeroed", "scattered", "tokens_loaded"))
        ctx.start()
        block = ctx.enter_context(nc.Block())

        @block.sync
        def _(sp):
            sp.dma_start(rw[:], rw_dram).then_inc(s_ld, 16)
            sp.dma_start(sdb[:], sdb_dram.partition_broadcast(P)).then_inc(s_ld, 16)
            with sp.Fori(0, T // 2) as i:
                for j in range(2):
                    sp.wait_ge(s_xn, at(i * 2 + j + 1))
                    sp.dma_start(xn_dram[:, bass.ds(i * 2 + j, 1), :], xn[j][:].rearrange("p (a n) -> p a n", a=1))\
                      .then_inc(s_xst[j], 16)
            for j in range(2):
                sp.wait_ge(s_xst[j], at(T // 2 * 16))

        @block.gpsimd
        def _(pool):
            pool.iota(expert[:], pattern=[[1, E]], base=0, channel_multiplier=0,
                      allow_small_or_imprecise_dtypes=True).then_inc(s_const, 1)
            pool.iota(tiles[:], pattern=[[1, NT]], base=0, channel_multiplier=0,
                      allow_small_or_imprecise_dtypes=True).then_inc(s_const, 1)
            pool.iota(ids[:], pattern=[[P, T]], base=0, channel_multiplier=1).then_inc(s_const, 1)
            pool.affine_select(out=before[:], in_=ones[:], compare_op=ALU.is_gt, fill=0.0, base=0,
                               pattern=[[1, P]], channel_multiplier=-1).then_inc(s_const, 1)
            pool.memset(zeros[:], 0).then_inc(s_const, 1)
            pool.wait_ge(s_const, at(5))
            pool.dma_start(table_dram.rearrange("(p c) a -> p (c a)", p=P), zeros[:]).then_inc(s_zero, 16)
            pool.wait_ge(s_ld, at(32))
            with pool.Fori(0, T) as t:
                pool.wait_ge(s_xn, at(t + 1))
                row = X[:, bass.ds(t, 1), :]
                pool.tensor_tensor(row, row, sdb[:].rearrange("p (a n) -> p a n", a=1), ALU.add).then_inc(s_bias, 1)
            pool.wait_ge(s_zero, 16)
            pool.wait_ge(s_pos, at(1))
            for t in range(T):
                for n in range(TOP):
                    pool.indirect_dma_start(out=table_dram, out_offset=bass.IndirectOffsetOnAxis(
                        ap=position[:, t, n:n + 1], axis=0), in_=ids[:, t:t + 1], in_offset=None).then_inc(s_scat, 16)
            pool.wait_ge(s_scat, 16 * T * TOP)
            pool.dma_start(token[:], table_dram.rearrange("(p c) a -> p (c a)", p=P)).then_inc(s_tok, 16)
            pool.wait_ge(s_tok, 16)

        @block.scalar
        def _(act):
            act.wait_ge(s_mv, at(T))
            act.activation(std[:], mv[:, :, 1], ACT.Sqrt, bias=eps[:]).then_inc(s_std, 1)
            with act.Fori(0, T // 2) as i:
                for j in range(2):
                    act.wait_ge(s_tr, at(i * 2 + j + 1))
                    act.wait_ge(s_log, at(i * 2))
                    act.activation(xt[j][:], tb[j][:].rearrange("p (k s) -> p k s", k=KD), ACT.Copy).then_inc(s_xt, 1)
            act.wait_ge(s_sub, at(1))
            act.activation(ex[:], logits[:], ACT.Exp).then_inc(s_exp, 1)

        @block.vector
        def _(dve):
            layernorm_stats(dve, (s_stats, s_mv), X, stats, mv, T)
            dve.wait_ge(s_std, at(1))
            dve.reciprocal(rstd[:], std[:]).then_inc(s_rstd, 1)
            dve.wait_ge(s_rstd, at(1))

            def norm(t, j, first=False):
                col = bass.ds(t, 1)
                if not first:
                    dve.wait_ge(s_tr, at(t - 1))
                    dve.wait_ge(s_xst[j], at((t - j) * 8))
                dve.tensor_scalar(xn[j][:].rearrange("p (a n) -> p a n", a=1), X[:, col, :], mv[:, col, 0], rstd[:, col],
                                  ALU.subtract, ALU.mult).then_inc(s_xn, 1)

            def rest(t, j):
                dve.wait_ge(s_log, at(t + 1))
                dve.tensor_copy(logits[:, bass.ds(t, 1), :], lb[j][:, 0:E].rearrange("p (a n) -> p a n", a=1))\
                   .then_inc(s_logc, 1)

            norm(0, 0, True)
            norm(1, 1, True)
            with dve.Fori(0, T // 2 - 1) as i:
                for j in range(2):
                    norm(i * 2 + 2 + j, j)
                    rest(i * 2 + j, j)
            for j in range(2):
                rest(T - 2 + j, j)
            dve.wait_ge(s_logc, at(T))
            dve.tensor_reduce(nmax[:], logits[:], AX.X, ALU.max).then_inc(s_nmax, 1)
            dve.wait_ge(s_nmax, at(1))
            dve.tensor_tensor(logits[:], logits[:], nmax[:].unsqueeze(2).broadcast_to([P, T, E]),
                              ALU.subtract).then_inc(s_sub, 1)
            dve.wait_ge(s_exp, at(1))
            for t in range(T):
                dve.max(top[:, t, :], ex[:, t, :]).then_inc(s_top, 1)
            for t in range(T):
                dve.wait_ge(s_top, at(t + 1))
                dve.max_index(topi[:, t, :], top[:, t, :], ex[:, t, :]).then_inc(s_at, 1)
            dve.wait_ge(s_at, at(T))
            dve.tensor_copy(atf[:], topi[:]).then_inc(s_atf, 1)
            dve.tensor_tensor(tsum[:], top[:, :, 0], top[:, :, 1], ALU.add).then_inc(s_sum, 1)
            dve.wait_ge(s_sum, at(1))
            dve.reciprocal(rsum[:], tsum[:]).then_inc(s_rsum, 1)
            dve.wait_ge(s_atf, at(1))
            dve.wait_ge(s_const, at(5))
            for n in range(TOP):
                dve.tensor_tensor(hot[:, :, n, :], expert[:].unsqueeze(1).broadcast_to([P, T, E]),
                                  atf[:, :, n:n + 1].broadcast_to([P, T, E]), ALU.is_equal).then_inc(s_hot, 1)
            dve.wait_ge(s_hot, at(2))
            dve.tensor_tensor(cnt[:], hot[:, :, 0, :], hot[:, :, 1, :], ALU.add).then_inc(s_cnt, 1)
            dve.wait_ge(s_rsum, at(1))
            dve.tensor_tensor(weight[:], top[:, :, 0:TOP], rsum[:].unsqueeze(2).broadcast_to([P, T, TOP]),
                              ALU.mult).then_inc(s_comb, 1)

            steps = [0]

            def step(ins):
                ins.then_inc(s_step, 1)
                steps[0] += 1
                dve.wait_ge(s_step, at(steps[0]))

            dve.wait_ge(s_before, at(2))
            totals = lb[1][:, 0:T * E].rearrange("p (t e) -> p t e", t=T)
            step(dve.tensor_copy(scan0[:], totals))
            a, b = scan0, scan1
            d = 1
            while d < T:
                step(dve.tensor_copy(b[:, 0:d, :], a[:, 0:d, :]))
                step(dve.tensor_tensor(b[:, d:T, :], a[:, d:T, :], a[:, 0:T - d, :], ALU.add))
                a, b, d = b, a, 2 * d
            step(dve.tensor_scalar(nt0[:], a[:, T - 1, :], 1.0 / TT, 0.5 - 0.5 / TT, ALU.mult, ALU.add))
            step(dve.tensor_scalar(nt1[:], nt0[:], ROUND, None, ALU.add))
            step(dve.tensor_scalar(nt0[:], nt1[:], ROUND, None, ALU.subtract))
            step(dve.tensor_copy(first[:], nt0[:]))
            c, e, d = nt0, nt1, 1
            while d < E:
                step(dve.tensor_copy(e[:, 0:d], c[:, 0:d]))
                step(dve.tensor_tensor(e[:, d:E], c[:, d:E], c[:, 0:E - d], ALU.add))
                c, e, d = e, c, 2 * d
            step(dve.tensor_tensor(first[:], c[:], first[:], ALU.subtract))
            step(dve.tensor_tensor(base[:], a[:], totals, ALU.subtract))
            step(dve.tensor_tensor(base[:], base[:], lb[0][:, 0:T * E].rearrange("p (t e) -> p t e", t=T), ALU.add))
            step(dve.scalar_tensor_tensor(base[:], first[:].unsqueeze(1).broadcast_to([P, T, E]), float(TT), base[:],
                                          ALU.mult, ALU.add))
            for n in range(TOP):
                step(dve.tensor_tensor(prod[:, :, n, :], hot[:, :, n, :], base[:], ALU.mult))
            step(dve.tensor_reduce(slotf[:], prod[:], AX.X, ALU.add))
            step(dve.tensor_copy(slot[:], slotf[:]))
            step(dve.tensor_scalar(rowf[:], slotf[:], 1.0 / P, 0.5 / P - 0.5, ALU.mult, ALU.add))
            step(dve.tensor_scalar(posf[:], rowf[:], ROUND, None, ALU.add))
            step(dve.tensor_scalar(colf[:], posf[:], ROUND, None, ALU.subtract))
            step(dve.scalar_tensor_tensor(rowf[:], colf[:], -float(P), slotf[:], ALU.mult, ALU.add))
            step(dve.scalar_tensor_tensor(posf[:], rowf[:], float(NT * TT // P), colf[:], ALU.mult, ALU.add))
            dve.tensor_copy(position[:], posf[:]).then_inc(s_pos, 1)
            step(dve.tensor_tensor(le[:], first[:].unsqueeze(1).broadcast_to([P, NT, E]),
                                   tiles[:].unsqueeze(2).broadcast_to([P, NT, E]), ALU.is_le))
            step(dve.tensor_reduce(tef[:], le[:], AX.X, ALU.add))
            step(dve.tensor_scalar(tile_expert[:], tef[:], 1.0, None, ALU.subtract))

        @block.tensor
        def _(pe):
            pe.wait_ge(s_ld, at(32))
            with pe.Fori(0, T // 2) as i:
                for j in range(2):
                    t = i * 2 + j
                    pe.wait_ge(s_xn, at(t + 1))
                    pe.wait_ge(s_xt, at(i * 2))
                    for c in range(KD):
                        last = pe.transpose(tb[j][:, c * P:(c + 1) * P], xn[j][:, c * P:(c + 1) * P], ident[:])
                    last.then_inc(s_tr, 1)
                for j in range(2):
                    t = i * 2 + j
                    pe.wait_ge(s_xt, at(t + 1))
                    pe.wait_ge(s_logc, at(i * 2))
                    for c in range(KD):
                        last = pe.matmul(lb[j][:, 0:E], xt[j][:, c, :], rw[:, c, :], start=c == 0, stop=c == KD - 1)
                    last.then_inc(s_log, 1)
            pe.wait_ge(s_cnt, at(1))
            pe.wait_ge(s_const, at(5))
            for b, w in enumerate((before, ones)):
                pe.matmul(lb[b][:, 0:T * E], w[:], cnt[:].rearrange("p t e -> p (t e)"), start=True,
                          stop=True).then_inc(s_before, 1)


def routed_experts(nc, banks, ident, tile_expert, token, gw_dram, uw_dram, dw_dram, xn_dram, y_dram, E, I, NT, TT):
    CT = TT // P
    MT = [(m, min(P, I - m)) for m in range(0, I, P)]
    M = len(MT)
    full, tail = I // P, MT[-1][1]
    with Phase(nc) as ctx:
        def sb(name, shape, dt=F32):
            return ctx.enter_context(nc.sbuf_tensor("m_" + name, shape, dt))

        def sem(name):
            return ctx.semaphore("m_" + name)

        wg, wu = ([Pair(ctx, nc, f"m_{n}{j}", [P, KD, I]) for j in range(2)] for n in ("wg", "wu"))
        wd = [Pair(ctx, nc, f"m_wd{j}", [P, M, D]) for j in range(2)]
        graw, uraw = ([sb(f"{n}{j}", [P, KD, I]) for j in range(2)] for n in ("graw", "uraw"))
        draw = [sb(f"draw{j}", [P, M, D]) for j in range(2)]
        idx = [sb(f"idx{j}", [P, CT], U32) for j in range(2)]
        xg = [sb(f"xg{c}", [P, D]) for c in range(2 * CT)]
        xT = Pair(ctx, nc, "m_xT", [P, KD, TT])
        sg, hf = ([sb(f"{n}{j}", [P, TT]) for j in range(2)] for n in ("sg", "hf"))
        h = Pair(ctx, nc, "m_h", [P, M, TT])
        y = [sb(f"y{j}", [P, D]) for j in range(CT)]
        gb, ub, tb, yb = banks[0:2], banks[2:4], banks[4:6], banks[6:8]
        s_raw = [sem(f"w{j}_loaded") for j in range(2)]
        s_whi, s_wlo, s_dlo, s_idx = sem("w_hi"), sem("w_lo"), sem("wd_lo"), sem("indices")
        s_x = [ctx.queue_semaphore(f"m_x{j}_gathered") for j in range(2)]
        tr = Flow(ctx, nc, "m_xT")
        s_g, s_sg, s_u, s_h, s_hi, s_lo, s_y, s_yc = (sem(n) for n in (
            "gate", "silu", "up", "h", "h_hi", "h_lo", "down", "y_copied"))
        s_st = [sem(f"y{j}_stored") for j in range(CT)]
        ctx.start()
        block = ctx.enter_context(nc.Block())
        NP = NT // 2

        @block.sync
        def _(sp):
            def load(t, j, first=False):
                e = sp.value_load(tile_expert[0:1, bass.ds(t, 1)], min_val=0, max_val=E - 1)
                if not first:
                    sp.wait_ge(s_wlo, at((t - 1) * 2))
                    sp.wait_ge(s_dlo, at(t - 1))
                one = bass.ds(e, 1)
                src = lambda w: w[one].rearrange("a (k p) n -> p (a k) n", p=P)
                sp.dma_start(graw[j][:], src(gw_dram)).then_inc(s_raw[j], 16)
                sp.dma_start(uraw[j][:], src(uw_dram)).then_inc(s_raw[j], 16)
                sp.dma_start(draw[j][:, 0:full, :], dw_dram[one, 0:full * P, :].rearrange("a (k p) n -> p (a k) n", p=P))\
                  .then_inc(s_raw[j], 16)
                sp.dma_start(draw[j][0:tail, full:M, :], dw_dram[one, MT[-1][0]:I, :].rearrange("a p n -> p a n"))\
                  .then_inc(s_raw[j], 16)

            def store(t):
                for c in range(CT):
                    sp.wait_ge(s_yc, at(t * CT + c + 1))
                    sp.dma_start(y_dram[:, bass.ds(t * CT + c, 1), :], y[c][:].rearrange("p (a n) -> p a n", a=1))\
                      .then_inc(s_st[c], 16)

            load(0, 0, True)
            load(1, 1, True)
            with sp.Fori(0, NP - 1) as i:
                for j in range(2):
                    load(i * 2 + j + 2, j)
                    store(i * 2 + j)
            store(NT - 2)
            store(NT - 1)
            for c in range(CT):
                sp.wait_ge(s_st[c], at(16 * NT))

        @block.gpsimd
        def _(pool):
            def gather(t, j):
                for c in range(CT):
                    pool.indirect_dma_start(out=xg[j * CT + c][:], out_offset=None, in_=xn_dram,
                                            in_offset=bass.IndirectOffsetOnAxis(ap=idx[j][:, c:c + 1], axis=0))\
                        .then_inc(s_x[j], 16)

            def split(t, j, more):
                for n, (w, raw) in enumerate(((wg[j], graw[j]), (wu[j], uraw[j]))):
                    if n and more:
                        pool.wait_ge(s_idx, at(t + 2))
                    pool.wait_ge(s_whi, at(t * 3 + n + 1))
                    pool.tensor_tensor(w.lo[:], raw[:], f32(w.hi[:]), ALU.subtract).then_inc(s_wlo, 1)

            def turn(i, more):
                for j in range(2):
                    t = i * 2 + j
                    if j == 0 or more:
                        split(t + 1, 1 - j, more)
                    if more:
                        gather(t + 2, j)

            pool.wait_ge(s_idx, at(2))
            gather(0, 0)
            gather(1, 1)
            split(0, 0, False)
            with pool.Fori(0, NP - 1) as i:
                turn(i, True)
            turn(NP - 1, False)

        @block.scalar
        def _(act):
            def split(t, j, which, first=False):
                act.wait_ge(s_raw[j], at((t - j) * 32 + 64))
                if not first:
                    act.wait_ge(s_y, at((t - 1) * CT))
                if 0 in which:
                    act.activation(wg[j].hi[:], graw[j][:], ACT.Copy).then_inc(s_whi, 1)
                if 1 in which:
                    act.activation(wu[j].hi[:], uraw[j][:], ACT.Copy).then_inc(s_whi, 1)
                if 2 in which:
                    down_hi(j)

            def down_hi(j):
                act.activation(wd[j].hi[:, 0:full, :], draw[j][:, 0:full, :], ACT.Copy)
                r = (slice(0, tail), full)
                act.activation(wd[j].hi[r], draw[j][r], ACT.Copy).then_inc(s_whi, 1)

            def transposed(t):
                for c in range(CT):
                    act.wait_ge(tr.mm, at(t * CT + c + 1))
                    act.activation(xT.hi[:, :, c * P:(c + 1) * P], tb[c][:].rearrange("p (k s) -> p k s", k=KD),
                                   ACT.Copy).then_inc(tr.hi, 1)

            def hidden(t, j, more):
                for m in range(M):
                    n, q = t * M + m, (j * M + m) % 2
                    act.wait_ge(s_g, at(n + 1))
                    act.wait_ge(s_h, at(t * M + max(m - 1, 0)))
                    r = slice(0, MT[m][1])
                    act.activation(sg[q][r, :], gb[q][r, 0:TT], ACT.Silu).then_inc(s_sg, 1)
                    act.wait_ge(s_h, at(n + 1))
                    if m == 0:
                        act.wait_ge(s_y, at(t * CT))
                    act.activation(h.hi[r, m, :], hf[q][r, :], ACT.Copy).then_inc(s_hi, 1)
                    if more:
                        split(t + 1, 1 - j, range(3 * m // M, 3 * (m + 1) // M))

            def turn(i, more):
                for j in range(2):
                    t = i * 2 + j
                    hidden(t, j, j == 0 or more)
                    if j == 0 or more:
                        transposed(t + 1)

            split(0, 0, (0, 1, 2), True)
            transposed(0)
            with act.Fori(0, NP - 1) as i:
                turn(i, True)
            turn(NP - 1, False)

        @block.vector
        def _(dve):
            def indices(t, j, first=False):
                if not first:
                    dve.wait_ge(s_x[j], (t - j) * 16)
                dve.tensor_copy(idx[j][:], token[:, bass.ds(t * CT, CT)]).then_inc(s_idx, 1)

            def down_weights(t, j):
                dve.wait_ge(s_whi, at(t * 3 + 3))
                dve.tensor_tensor(wd[j].lo[:, 0:full, :], draw[j][:, 0:full, :], f32(wd[j].hi[:, 0:full, :]), ALU.subtract)
                r = (slice(0, tail), full)
                dve.tensor_tensor(wd[j].lo[r], draw[j][r], f32(wd[j].hi[r]), ALU.subtract).then_inc(s_dlo, 1)

            def transposed(t):
                for c in range(CT):
                    dve.wait_ge(tr.hi, at(t * CT + c + 1))
                    cols = slice(c * P, (c + 1) * P)
                    dve.tensor_tensor(xT.lo[:, :, cols], tb[c][:].rearrange("p (k s) -> p k s", k=KD),
                                      f32(xT.hi[:, :, cols]), ALU.subtract).then_inc(tr.lo, 1)

            def hidden(t, j):
                for m in range(M):
                    n, q = t * M + m, (j * M + m) % 2
                    r = slice(0, MT[m][1])
                    dve.wait_ge(s_sg, at(n + 1))
                    dve.wait_ge(s_u, at(n + 1))
                    dve.wait_ge(s_lo, at(t * M + max(m - 1, 0)))
                    dve.tensor_tensor(hf[q][r, :], ub[q][r, 0:TT], sg[q][r, :], ALU.mult).then_inc(s_h, 1)
                    dve.wait_ge(s_hi, at(n + 1))
                    dve.tensor_tensor(h.lo[r, m, :], hf[q][r, :], f32(h.hi[r, m, :]), ALU.subtract).then_inc(s_lo, 1)

            def outputs(t):
                for c in range(CT):
                    dve.wait_ge(s_y, at(t * CT + c + 1))
                    dve.wait_ge(s_st[c], at(t * 16))
                    dve.tensor_copy(y[c][:], yb[c][:]).then_inc(s_yc, 1)

            def turn(i, more):
                for j in range(2):
                    t = i * 2 + j
                    if more:
                        indices(t + 2, j)
                    hidden(t, j)
                    if j == 0 or more:
                        transposed(t + 1)
                    outputs(t)
                    if j == 0 or more:
                        down_weights(t + 1, 1 - j)

            indices(0, 0, True)
            indices(1, 1, True)
            down_weights(0, 0)
            transposed(0)
            with dve.Fori(0, NP - 1) as i:
                turn(i, True)
            turn(NP - 1, False)

        @block.tensor
        def _(pe):
            def transposed(t, j):
                pe.wait_ge(s_x[j], (t - j) * 16 + 16 * CT)
                for c in range(CT):
                    for k in range(KD):
                        last = pe.transpose(tb[c][:, k * P:(k + 1) * P], xg[j * CT + c][:, k * P:(k + 1) * P], ident[:])
                    last.then_inc(tr.mm, 1)

            def hidden(t, j):
                pe.wait_ge(tr.lo, at(t * CT + CT))
                pe.wait_ge(s_wlo, at(t * 2 + 2))
                for m, (m0, mn) in enumerate(MT):
                    q = (j * M + m) % 2
                    for weights, dst, s_free, s_done in ((wg, gb, s_sg, s_g), (wu, ub, s_h, s_u)):
                        pe.wait_ge(s_free, at(t * M + max(m - 1, 0)))
                        for k in range(KD):
                            last = matmul3(pe, dst[q][0:mn, 0:TT], part(weights[j], slice(None), k, slice(m0, m0 + mn)),
                                           part(xT, slice(None), k), k == 0, k == KD - 1)
                        last.then_inc(s_done, 1)

            def down(t, j):
                pe.wait_ge(s_dlo, at(t + 1))
                for ms in (range(M - 1), range(M - 1, M)):
                    for c in range(CT):
                        pe.wait_ge(s_lo, at(t * M + max(ms) + 1))
                        pe.wait_ge(s_yc, at(t * CT))
                        for m in ms:
                            r = slice(0, MT[m][1])
                            last = matmul3(pe, yb[c][:], part(h, r, m, slice(c * P, (c + 1) * P)),
                                           part(wd[j], r, m), m == 0, m == M - 1)
                        if M - 1 in ms:
                            last.then_inc(s_y, 1)

            def turn(i, more):
                for j in range(2):
                    t = i * 2 + j
                    hidden(t, j)
                    if j == 0 or more:
                        transposed(t + 1, 1 - j)
                    down(t, j)

            transposed(0, 0)
            with pe.Fori(0, NP - 1) as i:
                turn(i, True)
            turn(NP - 1, False)


def shared_experts(nc, banks, X, ident, weight, slot, gw_dram, uw_dram, dw_dram, gb_dram, ub_dram, xn_dram, y_dram,
                   out_dram, E0, T, E, I):
    TOP = 2
    C = 512
    NC = T * P // C
    CT = C // P
    MT = [(m, min(P, I - m)) for m in range(0, I, P)]
    M = len(MT)
    with Phase(nc) as ctx:
        def sb(name, shape, dt=F32):
            return ctx.enter_context(nc.sbuf_tensor("e_" + name, shape, dt))

        def sem(name):
            return ctx.semaphore("e_" + name)

        wg, wu = ([Pair(ctx, nc, f"e_{n}{j}", [P, KD, I]) for j in range(2)] for n in ("wg", "wu"))
        wd = [Pair(ctx, nc, f"e_wd{j}", [P, M, D]) for j in range(2)]
        xT = Pair(ctx, nc, "e_xT", [P, KD, 2 * C])
        xn = [sb(f"xn{j}", [P, D]) for j in range(2)]
        yg = [sb(f"yg{j}", [P, D]) for j in range(2)]
        graw, uraw = ([sb(f"{n}{j}", [P, KD, I]) for j in range(2)] for n in ("graw", "uraw"))
        draw = [sb(f"draw{j}", [P, M, D]) for j in range(2)]
        gbias, ubias = sb("gbias", [P, E, M]), sb("ubias", [P, E, M])
        sg = [sb(f"sg{j}", [P, C]) for j in range(2)]
        hf = [sb(f"hf{j}", [P, C]) for j in range(2)]
        h = Pair(ctx, nc, "e_h", [P, M, C])
        gb, ub, yb = banks[0:2], banks[2:4], banks[4:8]
        s_small, s_whi, s_wlo, s_comb, s_out = (sem(n) for n in (
            "biases_loaded", "w_hi", "w_lo", "combined", "stored"))
        s_raw = [sem(f"w{e}_loaded") for e in range(E)]
        s_xn = [sem(f"xn{j}_loaded") for j in range(2)]
        s_yg = [ctx.queue_semaphore(f"e_y{j}_gathered") for j in range(TOP)]
        tr = Flow(ctx, nc, "e_xT")
        s_g, s_sg, s_u, s_h, s_hi, s_lo, s_y, s_add = (sem(n) for n in (
            "gate", "silu", "up", "h", "h_hi", "h_lo", "down", "added"))
        ctx.start()
        block = ctx.enter_context(nc.Block())

        full, tail = I // P, MT[-1][1]
        UNITS = E * NC
        ring = lambda t: slice(t % (2 * CT) * P, (t % (2 * CT) + 1) * P)
        PER = T // UNITS

        @block.sync
        def _(sp):
            def tokens(t):
                if t >= 2:
                    sp.wait_ge(tr.mm, at(t - 1))
                sp.dma_start(xn[t % 2][:], xn_dram[t * P:(t + 1) * P, :]).then_inc(s_xn[t % 2], 16)

            def weights(e):
                src = lambda w: w[E0 + e].rearrange("(k p) n -> p k n", p=P)
                sp.dma_start(graw[e][:], src(gw_dram)).then_inc(s_raw[e], 16)
                sp.dma_start(uraw[e][:], src(uw_dram)).then_inc(s_raw[e], 16)
                sp.dma_start(draw[e][:, 0:full, :], dw_dram[E0 + e, 0:full * P, :].rearrange("(k p) n -> p k n", p=P))\
                  .then_inc(s_raw[e], 16)
                sp.dma_start(draw[e][0:tail, full, :], dw_dram[E0 + e, MT[-1][0]:I, :]).then_inc(s_raw[e], 16)

            tokens(0)
            tokens(1)
            weights(0)
            sp.dma_start(gbias[:], gb_dram).then_inc(s_small, 16)
            sp.dma_start(ubias[:], ub_dram).then_inc(s_small, 16)
            for e in range(1, E):
                weights(e)
            for t in range(2, 2 * CT):
                tokens(t)
            for c in range(NC):
                for t in range((c + 2) * CT, min((c + 3) * CT, T)):
                    tokens(t)
                for t in range(c * CT, (c + 1) * CT):
                    sp.wait_ge(s_add, at((c + 1) * E * CT))
                    sp.wait_ge(s_comb, at((t + 1) * TOP))
                    sp.dma_start(out_dram[:, t, :], X[:, t, :]).then_inc(s_out, 16)
            sp.wait_ge(s_out, at(16 * T))

        @block.gpsimd
        def _(pool):
            def split(e):
                for n, (w, raw) in enumerate(((wg, graw[e]), (wu, uraw[e]), (wd, draw[e]))):
                    pool.wait_ge(s_whi, at(e * 3 + n + 1))
                    if n < 2:
                        ins = pool.tensor_tensor(w[e].lo[:], raw[:], f32(w[e].hi[:]), ALU.subtract)
                    else:
                        pool.tensor_tensor(w[e].lo[:, 0:full, :], raw[:, 0:full, :], f32(w[e].hi[:, 0:full, :]),
                                           ALU.subtract)
                        r = (slice(0, tail), full)
                        ins = pool.tensor_tensor(w[e].lo[r], raw[r], f32(w[e].hi[r]), ALU.subtract)
                    ins.then_inc(s_wlo, 1)

            for e in range(E):
                split(e)
            for t in range(T):
                for n in range(TOP):
                    if t:
                        pool.wait_ge(s_comb, at((t - 1) * TOP + n + 1))
                    pool.indirect_dma_start(out=yg[n][:], out_offset=None, in_=y_dram,
                                            in_offset=bass.IndirectOffsetOnAxis(ap=slot[:, t, n:n + 1], axis=0))\
                        .then_inc(s_yg[n], 16)

        @block.scalar
        def _(act):
            def split(e):
                act.wait_ge(s_raw[e], at(64))
                act.activation(wg[e].hi[:], graw[e][:], ACT.Copy).then_inc(s_whi, 1)
                act.activation(wu[e].hi[:], uraw[e][:], ACT.Copy).then_inc(s_whi, 1)
                act.activation(wd[e].hi[:, 0:full, :], draw[e][:, 0:full, :], ACT.Copy)
                r = (slice(0, tail), full)
                act.activation(wd[e].hi[r], draw[e][r], ACT.Copy).then_inc(s_whi, 1)

            def transposed(c):
                for t in range(c * CT, (c + 1) * CT):
                    act.wait_ge(tr.mm, at(t + 1))
                    act.activation(xT.hi[:, :, ring(t)], yb[t % 2][:].rearrange("p (k s) -> p k s", k=KD),
                                   ACT.Copy).then_inc(tr.hi, 1)

            for e in range(E):
                split(e)
            transposed(0)
            act.wait_ge(s_small, at(32))
            for u in range(UNITS):
                c, e = u // E, u % E
                for m in range(M):
                    n = u * M + m
                    q = n % 2
                    act.wait_ge(s_g, at(n + 1))
                    act.wait_ge(s_h, at(max(n - 1, 0)))
                    r = slice(0, MT[m][1])
                    act.activation(sg[q][r, :], gb[q][r, :], ACT.Silu, bias=gbias[r, e, m:m + 1]).then_inc(s_sg, 1)
                    act.wait_ge(s_h, at(n + 1))
                    if m == 0:
                        act.wait_ge(s_y, at(u * CT))
                    act.activation(h.hi[r, m, :], hf[q][r, :], ACT.Copy).then_inc(s_hi, 1)
                if e == 0 and c + 1 < NC:
                    transposed(c + 1)

        @block.vector
        def _(dve):
            def transposed(c):
                for t in range(c * CT, (c + 1) * CT):
                    dve.wait_ge(tr.hi, at(t + 1))
                    cols = ring(t)
                    dve.tensor_tensor(xT.lo[:, :, cols], yb[t % 2][:].rearrange("p (k s) -> p k s", k=KD),
                                      f32(xT.hi[:, :, cols]), ALU.subtract).then_inc(tr.lo, 1)

            transposed(0)
            dve.wait_ge(s_small, at(32))
            for u in range(UNITS):
                c, e = u // E, u % E
                for m in range(M):
                    n = u * M + m
                    q = n % 2
                    r = slice(0, MT[m][1])
                    dve.wait_ge(s_sg, at(n + 1))
                    dve.wait_ge(s_u, at(n + 1))
                    dve.wait_ge(s_lo, at(max(n - 1, 0)))
                    dve.scalar_tensor_tensor(hf[q][r, :], ub[q][r, :], ubias[r, e, m:m + 1], sg[q][r, :], ALU.add,
                                             ALU.mult).then_inc(s_h, 1)
                    dve.wait_ge(s_hi, at(n + 1))
                    dve.tensor_tensor(h.lo[r, m, :], hf[q][r, :], f32(h.hi[r, m, :]), ALU.subtract).then_inc(s_lo, 1)
                if e == 0 and c + 1 < NC:
                    transposed(c + 1)
                for t in range(CT):
                    dve.wait_ge(s_y, at(u * CT + t + 1))
                    row = X[:, c * CT + t, :]
                    dve.tensor_tensor(row, row, yb[t][:], ALU.add).then_inc(s_add, 1)
                for t in range(u * PER, (u + 1) * PER):
                    for n in range(TOP):
                        dve.wait_ge(s_yg[n], 16 * (t + 1))
                        dve.wait_ge(s_add, at(u * CT + CT))
                        dve.wait_ge(s_comb, at(t * TOP + n))
                        row = X[:, t, :]
                        dve.scalar_tensor_tensor(row, yg[n][:], weight[:, t, n:n + 1], row, ALU.mult,
                                                 ALU.add).then_inc(s_comb, 1)

        @block.tensor
        def _(pe):
            def transposed(tiles, u):
                pe.wait_ge(s_add, at(u * CT))
                for t in tiles:
                    pe.wait_ge(s_xn[t % 2], at(t // 2 * 16 + 16))
                    if t >= 2:
                        pe.wait_ge(tr.lo, at(t - 1))
                    for k in range(KD):
                        last = pe.transpose(yb[t % 2][:, k * P:(k + 1) * P], xn[t % 2][:, k * P:(k + 1) * P], ident[:])
                    last.then_inc(tr.mm, 1)

            transposed(range(CT), 0)
            for u in range(UNITS):
                c, j = u // E, u % E
                cols = slice(c % 2 * C, (c % 2 + 1) * C)
                if j == 0:
                    pe.wait_ge(tr.lo, at((c + 1) * CT))
                pe.wait_ge(s_wlo, at(3 * (j + 1)))
                for m, (m0, mn) in enumerate(MT):
                    n = u * M + m
                    q = n % 2
                    for weights, dst, s_free, s_done in ((wg, gb, s_sg, s_g), (wu, ub, s_h, s_u)):
                        pe.wait_ge(s_free, at(max(n - 1, 0)))
                        for k in range(KD):
                            last = matmul3(pe, dst[q][0:mn, :], part(weights[j], slice(None), k, slice(m0, m0 + mn)),
                                           part(xT, slice(None), k, cols), k == 0, k == KD - 1)
                        last.then_inc(s_done, 1)
                if j == 0 and c + 1 < NC:
                    transposed(range((c + 1) * CT, (c + 2) * CT), u)
                    pe.wait_ge(tr.lo, at((c + 2) * CT))
                for ms in (range(M - 1), range(M - 1, M)):
                    for t in range(CT):
                        pe.wait_ge(s_lo, at(u * M + max(ms) + 1))
                        pe.wait_ge(s_add, at(u * CT))
                        for m in ms:
                            r = slice(0, MT[m][1])
                            last = matmul3(pe, yb[t][:], part(h, r, m, slice(t * P, (t + 1) * P)),
                                           part(wd[j], r, m), m == 0, m == M - 1)
                        if M - 1 in ms:
                            last.then_inc(s_y, 1)


def program(nc, a, out, stop=4, start=0):
    B, S, _ = a["x"].shape
    T = B * S // P
    with ExitStack() as ctx:
        X = ctx.enter_context(nc.sbuf_tensor("X", [P, T, D], F32))
        eps = ctx.enter_context(nc.sbuf_tensor("eps", [P, 1], F32))
        ident = ctx.enter_context(nc.sbuf_tensor("ident", [P, P], F32))
        ones = ctx.enter_context(nc.sbuf_tensor("ones", [P, P], F32))
        banks = [ctx.enter_context(nc.psum_tensor(f"bank{j}", [P, 512], F32)) for j in range(8)]
        s_const = ctx.enter_context(nc.semaphore("constants"))
        s_out = ctx.enter_context(nc.semaphore("stored"))
        with nc.Block() as block:
            @block.gpsimd
            def _(pool):
                pool.memset(eps[:], LN_EPS).then_inc(s_const, 1)
                pool.memset(ident[:], 0.0).then_inc(s_const, 1)
                pool.memset(ones[:], 1.0).then_inc(s_const, 1)
                pool.wait_ge(s_const, 2)
                pool.affine_select(out=ident[:], in_=ident[:], compare_op=ALU.not_equal, fill=1.0, base=0,
                                   pattern=[[-1, P]], channel_multiplier=1).then_inc(s_const, 1)
        tok = lambda ap: ap.rearrange("b s d -> (b s) d").rearrange("(t p) d -> p t d", p=P)
        ktile = lambda ap: ap.rearrange("(k p) n -> p k n", p=P)
        if start:
            with nc.Block() as block:
                @block.sync
                def _(sp):
                    sp.dma_start(X[:], tok(a["x"])).then_inc(s_const, 16)
                    sp.wait_ge(s_const, 20)
        if start < 1:
          attention0(nc, banks, X, eps, ident, tok(a["x"]), tok(a["ctx"]), ktile(a["ctxT"]),
                   [ktile(a[n]) for n in ("wqT", "wkT", "wvT", "woT")], B, S)
        if start < 2 and stop >= 2:
            ffn0(nc, banks, X, eps, ident, ones, [ktile(a[n]) for n in ("gwT", "vwT", "owT")], [a[n] for n in ("gb", "vb", "ob")], T)
        if start < 3 and stop >= 3:
            G = 4
            k_dram = [nc.dram_tensor(f"K_{n}", (P, G, B * S), F32, kind="Internal").ap() for n in ("hi", "lo")]
            v_dram = [nc.dram_tensor(f"V_{n}", (P, T, D), F32, kind="Internal").ap() for n in ("hi", "lo")]
            with ExitStack() as cx:
                xT = Pair(cx, nc, "x1T", [P, KD, B * S])
                keys_values1(nc, banks, X, eps, ident, ones, xT, ktile(a["ctxT"]), ktile(a["Wk"]), ktile(a["Wv"]),
                             a["bk"], a["bv"], a["qn"], a["kn"], k_dram, v_dram, B, S, G)
                attention1(nc, banks, X, ident, ones, xT, a["mask"].rearrange("(t p) s -> p t s", p=P), ktile(a["Wq"]),
                           ktile(a["Wo"]), a["bqT"], k_dram, v_dram, B, S, G)
        if stop >= 4:
            E = a["rwT"].shape[1]
            EA, _, I = a["egw"].shape
            TT = 2 * P
            NT = 2 * B * S // TT + E
            dram = lambda name, shape, dt: nc.dram_tensor(name, shape, dt, kind="Internal").ap()
            xn_dram = dram("xn", (B * S, D), F32)
            y_dram = dram("y_routed", (NT * TT, D), F32)
            table_dram = dram("slot_tokens", (NT * TT, 1), U32)
            with ExitStack() as cx:
                sb = lambda name, shape, dt: cx.enter_context(nc.sbuf_tensor(name, shape, dt))
                weight, slot = sb("weight", [P, T, 2], F32), sb("slot", [P, T, 2], U32)
                tile_expert, token = sb("tile_expert", [P, NT], U32), sb("token", [P, NT * TT // P], U32)
                rows = lambda ap: ap.rearrange("(t p) d -> p t d", p=P)
                router(nc, banks, X, eps, ident, ones, weight, slot, tile_expert, token, ktile(a["rwT"]), a["sdb"],
                       rows(xn_dram), table_dram, T, E, NT, TT)
                routed_experts(nc, banks, ident, tile_expert, token, a["egw"], a["euw"], a["edw"], xn_dram, rows(y_dram),
                               E, I, NT, TT)
                shared_experts(nc, banks, X, ident, weight, slot, a["egw"], a["euw"], a["edw"], a["egb"], a["eub"],
                               xn_dram, y_dram, tok(out), E, T, EA - E, I)
            return
        with nc.Block() as block:
            @block.sync
            def _(sp):
                sp.dma_start(tok(out), X[:]).then_inc(s_out, 16)
                sp.wait_ge(s_out, 16)


def _layout(inputs):
    import numpy as np
    g = lambda n: np.asarray(inputs[n])
    t = lambda n: np.ascontiguousarray(g(n).T)
    E, _, I = g("L1_ffn_gate_w").shape

    def experts_in(n):
        shared = g(f"L1_ffn_s_{n}_w").reshape(512, 2, I).transpose(1, 0, 2)
        return np.concatenate([g(f"L1_ffn_{n}_w"), shared])

    def bias(n):
        b = np.zeros((2, -(-I // 128) * 128), np.float32)
        b[:, :I] = g(f"L1_ffn_s_{n}_b").reshape(2, I)
        return b.reshape(2, -1, 128).transpose(2, 0, 1)

    return {
        "x": g("x"), "ctx": g("ctx_2048"),
        "ctxT": np.ascontiguousarray(g("ctx_2048").reshape(-1, 512).T),
        "rwT": t("L1_ffn_router_w"), "sdb": g("L1_ffn_s_down_b"),
        "egw": experts_in("gate"), "euw": experts_in("up"),
        "edw": np.concatenate([g("L1_ffn_down_w"), g("L1_ffn_s_down_w").reshape(2, I, 512)]),
        "egb": bias("gate"), "eub": bias("up"),
        "Wq": g("L1_xattn_Wq"), "Wk": g("L1_xattn_Wk"), "Wv": g("L1_xattn_Wv"), "Wo": g("L1_xattn_Wo"),
        "bqT": g("L1_xattn_bq").reshape(-1, 128).T, "bk": g("L1_xattn_bk"), "bv": g("L1_xattn_bv"),
        "qn": g("L1_xattn_qn_w").reshape(128, 1), "kn": g("L1_xattn_kn_w").reshape(128, 1),
        "mask": g("mask_1xSxS2_ff0")[0],
        "gwT": t("L0_ffn_gate_w"), "vwT": t("L0_ffn_val_w"), "owT": t("L0_ffn_out_w"),
        "gb": g("L0_ffn_gate_b"), "vb": g("L0_ffn_val_b"), "ob": g("L0_ffn_out_b"),
        "wqT": t("L0_xattn_wq"), "wkT": t("L0_xattn_wk"), "wvT": t("L0_xattn_wv"), "woT": t("L0_xattn_wo"),
    }


def kernel(**inputs):
    import numpy as np
    import concourse.bacc as bacc
    from concourse.bass_utils import run_bass_kernel_spmd

    nc = bacc.Bacc("TRN2", target_bir_lowering=False, num_devices=1)
    arrays, args = {}, {}
    for name, a in _layout(inputs).items():
        a = np.ascontiguousarray(a)
        arrays["in_" + name] = a
        args[name] = nc.dram_tensor("in_" + name, a.shape, mybir.dt.from_np(a.dtype), kind="ExternalInput").ap()
    out = nc.dram_tensor("out", (8, 256, 512), F32, kind="ExternalOutput").ap()
    program(nc, args, out)
    r = run_bass_kernel_spmd(nc, [arrays], core_ids=[0])
    return r.results[0]["out"]
```
